# Optimizing a Trainium2 kernel written in Bass

```python
import numpy as np
import jax
import jax.numpy as jnp

def _softmax(x, axis=-1):
    return jax.nn.softmax(x, axis=axis)

def _gelu(x):
    return jax.nn.gelu(x, approximate=True)

def _silu(x):
    return jax.nn.silu(x)

def _sigmoid(x):
    return jax.nn.sigmoid(x)

def _layernorm(x, axis=-1, eps=1e-05):
    m = jnp.mean(x, axis=axis, keepdims=True)
    v = jnp.var(x, axis=axis, keepdims=True)
    return (x - m) / jnp.sqrt(v + eps)

def _scatter_add(tgt, idx, src, axis=0):
    return tgt.at[idx].add(src)

def _segment_sum(src, seg, n):
    return jax.ops.segment_sum(src, seg, n)
kernel_name = 'mk_prb_d1_jaxref_r8_37b57b'

def setup_inputs(seed: int=0):
    np.random.seed(seed)
    _w = jnp.asarray

    def _L0_attn_setup():
        import jax, jax.numpy as jnp
        import numpy as np
        from jax import lax
        BLOCK_LEN = 128
        NEG_INF = -1000000000.0
        key = jax.random.key(seed)
        ks = jax.random.split(key, 8)
        N, L, Dm = (2, 1024, 512)
        W, H, dh = (128, 16, 64)
        s = lambda fan: 1.0 / np.sqrt(fan)
        return {'inputs': jax.random.normal(ks[0], (N, L, Dm), jnp.float32), 'conv_w': jax.random.normal(ks[1], (3, Dm, 3 * W), jnp.float32) * s(3 * Dm), 'conv_b': jnp.zeros((3 * W,), jnp.float32), 'wq': jax.random.normal(ks[2], (W, H, dh), jnp.float32) * s(W), 'bq': jnp.zeros((H, dh), jnp.float32), 'wk': jax.random.normal(ks[3], (W, H, dh), jnp.float32) * s(W), 'bk': jnp.zeros((H, dh), jnp.float32), 'wv': jax.random.normal(ks[4], (W, H, dh), jnp.float32) * s(W), 'bv': jnp.zeros((H, dh), jnp.float32), 'wo': jax.random.normal(ks[5], (H, dh, W), jnp.float32) * s(H * dh), 'bo': jnp.zeros((W,), jnp.float32), 'proj_w': jax.random.normal(ks[6], (W, Dm), jnp.float32) * s(W), 'proj_b': jnp.zeros((Dm,), jnp.float32)}
    _L0_attn_in = _L0_attn_setup()

    def _L0_ffn_setup():
        import jax, jax.numpy as jnp
        import numpy as np
        H, F, E, K = (512, 800, 8, 2)
        B, S = (1, 64)
        key = jax.random.key(seed)
        k0, k1, k2, k3, k4 = jax.random.split(key, 5)
        x = jax.random.normal(k0, (B, S, H), dtype=jnp.float32)
        gate_w = jax.random.normal(k1, (E, H), dtype=jnp.float32) * 0.02
        w1 = jax.random.normal(k2, (E, F, H), dtype=jnp.float32) * 0.02
        w3 = jax.random.normal(k3, (E, F, H), dtype=jnp.float32) * 0.02
        w2 = jax.random.normal(k4, (E, H, F), dtype=jnp.float32) * 0.02
        return {'x': x, 'gate_w': gate_w, 'w1': w1, 'w2': w2, 'w3': w3}
    _L0_ffn_in = _L0_ffn_setup()
    _d = {'L0_attn_inputs': _L0_attn_in['inputs'], 'L0_attn_conv_w': _L0_attn_in['conv_w'], 'L0_attn_conv_b': _L0_attn_in['conv_b'], 'L0_attn_wq': _L0_attn_in['wq'], 'L0_attn_bq': _L0_attn_in['bq'], 'L0_attn_wk': _L0_attn_in['wk'], 'L0_attn_bk': _L0_attn_in['bk'], 'L0_attn_wv': _L0_attn_in['wv'], 'L0_attn_bv': _L0_attn_in['bv'], 'L0_attn_wo': _L0_attn_in['wo'], 'L0_attn_bo': _L0_attn_in['bo'], 'L0_attn_proj_w': _L0_attn_in['proj_w'], 'L0_attn_proj_b': _L0_attn_in['proj_b'], 'L0_ffn_gate_w': _L0_ffn_in['gate_w'], 'L0_ffn_w1': _L0_ffn_in['w1'], 'L0_ffn_w2': _L0_ffn_in['w2'], 'L0_ffn_w3': _L0_ffn_in['w3']}
    _x0 = _d['L0_attn_inputs']
    _d['L0_attn_inputs'] = jax.random.normal(jax.random.fold_in(jax.random.key(seed), 1), (4, 512, 512), dtype=_x0.dtype)
    del _x0
    return _d

def reference(L0_attn_inputs, L0_attn_conv_w, L0_attn_conv_b, L0_attn_wq, L0_attn_bq, L0_attn_wk, L0_attn_bk, L0_attn_wv, L0_attn_bv, L0_attn_wo, L0_attn_bo, L0_attn_proj_w, L0_attn_proj_b, L0_ffn_gate_w, L0_ffn_w1, L0_ffn_w2, L0_ffn_w3):

    def _L0_attn_ref(inputs, conv_w, conv_b, wq, bq, wk, bk, wv, bv, wo, bo, proj_w, proj_b):
        import jax, jax.numpy as jnp
        import numpy as np
        from jax import lax
        BLOCK_LEN = 128
        NEG_INF = -1000000000.0
        N, L, Dm = inputs.shape
        x = lax.conv_general_dilated(inputs, conv_w, window_strides=(1,), padding='SAME', dimension_numbers=('NWC', 'WIO', 'NWC')) + conv_b
        q, k, v = jnp.split(x, 3, axis=-1)
        W_ = q.shape[-1]
        nb = L // BLOCK_LEN
        q = q.reshape(N * nb, BLOCK_LEN, W_)
        k = k.reshape(N * nb, BLOCK_LEN, W_)
        v = v.reshape(N * nb, BLOCK_LEN, W_)
        dh = wq.shape[-1]
        qh = jnp.einsum('btd,dhe->bthe', q, wq) + bq
        kh = jnp.einsum('btd,dhe->bthe', k, wk) + bk
        vh = jnp.einsum('btd,dhe->bthe', v, wv) + bv
        scale = 1.0 / jnp.sqrt(jnp.asarray(dh, qh.dtype))
        scores = jnp.einsum('bqhe,bkhe->bhqk', qh * scale, kh)
        causal = jnp.tril(jnp.ones((BLOCK_LEN, BLOCK_LEN), bool))
        scores = jnp.where(causal, scores, NEG_INF)
        p = jax.nn.softmax(scores, axis=-1)
        o = jnp.einsum('bhqk,bkhe->bqhe', p, vh)
        o = jnp.einsum('bqhe,hed->bqd', o, wo) + bo
        o = o.reshape(N, L, W_)
        return o @ proj_w + proj_b

    def _L0_ffn_ref(x, gate_w, w1, w2, w3):
        import jax, jax.numpy as jnp
        import numpy as np
        H, F, E, K = (512, 800, 8, 2)
        B, S = (1, 64)
        b, s, h = x.shape
        xt = x.reshape(-1, h)
        T = xt.shape[0]
        logits = xt @ gate_w.T
        probs = jax.nn.softmax(logits, axis=-1)
        top_vals, top_idx = jax.lax.top_k(probs, K)
        top_vals = top_vals / jnp.sum(top_vals, axis=-1, keepdims=True)
        w_full = jnp.zeros((T, E), dtype=xt.dtype).at[jnp.arange(T)[:, None], top_idx].add(top_vals)
        h1 = jnp.einsum('th,efh->tef', xt, w1)
        h3 = jnp.einsum('th,efh->tef', xt, w3)
        act = jax.nn.silu(h1) * h3
        expert_out = jnp.einsum('tef,ehf->teh', act, w2)
        y = jnp.einsum('te,teh->th', w_full, expert_out)
        return y.reshape(b, s, h)
    x = L0_attn_inputs
    xn = _layernorm(x, axis=-1)
    x = x + _L0_attn_ref(xn, L0_attn_conv_w, L0_attn_conv_b, L0_attn_wq, L0_attn_bq, L0_attn_wk, L0_attn_bk, L0_attn_wv, L0_attn_bv, L0_attn_wo, L0_attn_bo, L0_attn_proj_w, L0_attn_proj_b) + _L0_ffn_ref(xn, L0_ffn_gate_w, L0_ffn_w1, L0_ffn_w2, L0_ffn_w3)
    return x

_drawn_inputs = setup_inputs


def setup_inputs(seed=0):
    import zlib

    import numpy as np

    out = dict(_drawn_inputs(seed))
    spreads = {'L0_attn_conv_b': (0.0, 0.1),
     'L0_attn_bq': (0.0, 0.403),
     'L0_attn_bk': (0.0, 0.8),
     'L0_attn_bv': (0.0, 0.1),
     'L0_attn_bo': (0.0, 0.1),
     'L0_attn_proj_b': (0.0, 0.1)}
    factors = {}
    for name, (base, spread) in spreads.items():
        noise = np.random.default_rng([zlib.crc32(name.encode()), seed]).standard_normal(out[name].shape)
        drawn = base * np.exp(spread * noise) if base else spread * noise
        out[name] = jnp.asarray(drawn.astype(out[name].dtype))
    for name, factor in factors.items():
        out[name] = (out[name] * factor).astype(out[name].dtype)
    return out
```

```python
import concourse.bass as bass
from concourse import mybir
from contextlib import ExitStack

F32 = mybir.dt.float32
F32R = mybir.dt.float32r
I32 = mybir.dt.int32
U32 = mybir.dt.uint32
ALU = mybir.AluOpType
ACT = mybir.ActivationFunctionType
AX = mybir.AxisListType.X

P = 128
BATCH, LEN, DM = 4, 512, 512
TOK = BATCH * LEN
NT = TOK // P
TPB = LEN // P
DC = DM // P
W, H, DH = 128, 16, 64
NE, FF, TOPK = 8, 800, 2
EPS = 1e-5
NEG = -1e9
BIG = 3e38
SCALE = DH ** -0.5

EXPERT_TILES = (TOPK * TOK + (P - 1) * NE) // P
LEAST_TILES = TOPK * TOK // P
SPARE = EXPERT_TILES - LEAST_TILES
SLOTS = EXPERT_TILES * P
NPAD = NE + SPARE
DUMP = SLOTS

FA, FB = 3 * P, FF - 3 * P
AC = (FF + P - 1) // P
FLAST = FF - (AC - 1) * P
PIECES = [(DC * FA, P), (DC * FA, P), (DC * FB, P), (DC * FB, P), (3 * DM, P), (3 * DM, P), (DM, FLAST)]
PIECE_AT = [sum(c for c, _ in PIECES[:i]) for i in range(len(PIECES))]
WCOLS = sum(c for c, _ in PIECES)
NPC = len(PIECES)
RAWW = max(c for c, _ in PIECES)


def build(nc, x, conv_w, columns, wq, wk, wv, bv, wo, proj_w, proj_b, gate, experts, out):
    xn_d = nc.dram_tensor("xn_rows", [TOK, DM], F32, kind="Internal").ap()
    xg_d = nc.dram_tensor("dispatched_rows", [SLOTS + NPAD * P, DM], F32, kind="Internal").ap()
    y_d = nc.dram_tensor("expert_rows", [SLOTS, DM], F32, kind="Internal").ap()
    ctx = ExitStack()
    with ctx:
        def keep(name, shape, dt=F32):
            return ctx.enter_context(nc.sbuf_tensor(name, shape, dt))

        t = dict(
            ident=keep("ident", [P, P]),
            slot=keep("slot", [P, TOPK, NT], I32),
            gates=keep("gates", [P, TOPK, NT]),
        )
        banks = [ctx.enter_context(nc.psum_tensor(f"bank{i}", [P, 512], F32)) for i in range(8)]
        experts_half(nc, t, banks, x, gate, experts, xn_d, xg_d, y_d)
        attention_half(nc, t, banks, x, xn_d, y_d, conv_w, columns, wq, wk, wv, bv, wo,
                       proj_w, proj_b, out)


def three_passes(nc, out, hi, lo, rhi, rlo, first=True, last=True):
    nc.tensor.matmul(out, hi, rhi, start=first, stop=False)
    nc.tensor.matmul(out, hi, rlo, start=False, stop=False)
    return nc.tensor.matmul(out, lo, rhi, start=False, stop=last)


def experts_half(nc, t, banks, x, gate, experts, xn_d, xg_d, y_d):
    ctx = ExitStack()
    with ctx:
        def sb(name, shape, dt=F32):
            return ctx.enter_context(nc.sbuf_tensor(name, shape, dt))

        def sem(name):
            return ctx.enter_context(nc.semaphore(name))

        ident, slot, gates = t["ident"], t["slot"], t["gates"]
        raw = sb("raw", [P, 2, RAWW])
        xrow = sb("xrow", [P, DM])
        xTh, xTl = sb("xTh", [P, DC, P], F32R), sb("xTl", [P, DC, P], F32R)
        silu, act = sb("silu", [P, FF]), sb("act", [P, FF])
        aTh, aTl = sb("aTh", [P, AC, P], F32R), sb("aTl", [P, AC, P], F32R)
        ysb = sb("ysb", [P, DM])
        tile_waits = sb("tile_waits", [1, EXPERT_TILES], I32)
        tile_slots = sb("tile_slots", [1, EXPERT_TILES], I32)
        released = sb("released", [1, NE], I32)
        slots_at = nc.sbuf_base
        whi, wlo = sb("whi", [P, 2 * WCOLS], F32R), sb("wlo", [P, 2 * WCOLS], F32R)
        at = {"whi": slots_at + 4 * WCOLS, "wlo": slots_at + 12 * WCOLS}

        def front(where, name, shape, dt=F32):
            size = 4
            for n in shape[1:]:
                size *= n
            h = nc.alloc_sbuf_tensor_at(name, shape, dt, offset=at[where])
            at[where] += (size + 31) // 32 * 32
            return h

        xb = front("wlo", "xb", [P, NT, DM])
        zrow = front("wlo", "zrow", [P, DM])
        gTf = front("whi", "gTf", [P, DC, NE])
        gTh, gTl = sb("gTh", [P, DC, NE], F32R), sb("gTl", [P, DC, NE], F32R)
        stats = front("whi", "stats", [P, NT, 6])
        mv = front("whi", "mv", [P, NT, 2])
        var = front("whi", "var", [P, NT])
        std = front("whi", "std", [P, NT])
        rstd = front("whi", "rstd", [P, NT])
        tmp = front("whi", "tmp", [P, NT])
        less = front("whi", "less", [P, P])
        ones = front("whi", "ones", [P, P])
        lane = front("whi", "lane", [P, 1])
        eno = front("whi", "eno", [P, NE])
        dumps = front("whi", "dumps", [P, NPAD])
        tails = front("whi", "tails", [P, SPARE])
        tileno = front("whi", "tileno", [1, EXPERT_TILES])
        prob = front("whi", "prob", [P, NT, NE])
        work = front("whi", "work", [P, NT, NE])
        first = front("whi", "first", [P, NT, NE])
        second = front("whi", "second", [P, NT, NE])
        before = front("whi", "before", [P, NT, NE])
        col = front("whi", "col", [P, 4, NT])
        picked = front("whi", "picked", [P, NE])
        need = front("whi", "need", [P, 6, NE])
        needi = front("whi", "needi", [P, NE], I32)
        padf = front("whi", "padf", [P, 3, NPAD])
        pads = front("whi", "pads", [P, NPAD], I32)
        cmp = front("whi", "cmp", [1, EXPERT_TILES, NE - 1])
        texp = front("whi", "texp", [1, EXPERT_TILES])
        texi = front("whi", "texi", [1, EXPERT_TILES], I32)
        assert at["whi"] <= slots_at + 8 * WCOLS and at["wlo"] <= slots_at + 16 * WCOLS

        hA1, hA3, hB1, hB3, tA, tB, tX, yP = banks
        logits, rank, total = tB, yP, hA1

        x_loaded = [sem(f"x_loaded{b}") for b in range(BATCH)]
        gate_loaded = sem("gate_loaded")
        consts = sem("consts")
        pool_turns, sp_turns = sem("pool_turns"), sem("sp_turns")
        dve_chain = sem("dve_chain")
        gate_split = sem("gate_split")
        var_ready, std_ready = sem("var_ready"), sem("std_ready")
        xn_ready = sem("xn_ready")
        xn_stored = sem("xn_stored")
        front_xT, front_hi, front_lo = sem("front_xT"), sem("front_hi"), sem("front_lo")
        logits_done = sem("logits_done")
        shifted, exp_done = sem("shifted"), sem("exp_done")
        picked_ready, rank_done = sem("picked_ready"), sem("rank_done")
        routed = sem("routed")
        sent, padded = sem("sent"), sem("padded")
        raw_loaded = [sem("raw_loaded0"), sem("raw_loaded1")]
        hi_split, lo_split = sem("hi_split"), sem("lo_split")
        row_loaded = sem("row_loaded")
        xT_done, xT_hi, xT_lo = sem("xT_done"), sem("xT_hi"), sem("xT_lo")
        hA_done, hB_done = sem("hA_done"), sem("hB_done")
        siluA, siluB, actA, actB = sem("siluA"), sem("siluB"), sem("actA"), sem("actB")
        aT_done, aT_hi, aT_lo = sem("aT_done"), sem("aT_hi"), sem("aT_lo")
        y_done, y_copied, y_stored = sem("y_done"), sem("y_copied"), sem("y_stored")

        block = ctx.enter_context(nc.Block())

        def piece(sb_tensor, slot_at, i):
            n, parts = PIECES[i]
            return sb_tensor[0:parts, bass.ds(slot_at + PIECE_AT[i], n)]

        @block.sync
        def _(sp):
            for b in range(BATCH):
                sp.dma_start(xb[:, TPB * b:TPB * (b + 1), :],
                             x[b * LEN:(b + 1) * LEN, :].rearrange("(j p) d -> p j d", p=P)).then_inc(x_loaded[b], 16)
                if b == 0:
                    sp.dma_start(gTf[:], gate).then_inc(gate_loaded, 16)

            def load(e, i, half, n):
                w, parts = PIECES[i]
                if n is not None:
                    sp.wait_ge(lo_split, n)
                    if not isinstance(n, int):
                        sp.sem_inc(sp_turns, 1)
                src = experts[bass.ds(e, 1), 0:parts, PIECE_AT[i]:PIECE_AT[i] + w].rearrange("a p w -> (a p) w")
                sp.dma_start(raw[0:parts, half, 0:w], src).then_inc(raw_loaded[half], 16)

            for i in range(NPC + 2):
                load(i // NPC, i % NPC, i % 2, i - 1 if i >= 2 else None)
            for b in range(BATCH):
                sp.wait_ge(xn_ready, TPB * (b + 1))
                sp.dma_start(xn_d[b * LEN:(b + 1) * LEN, :].rearrange("(j p) d -> p j d", p=P),
                             xb[:, TPB * b:TPB * (b + 1), :]).then_inc(xn_stored, 16)
            for i in range(NPC + 2, 2 * NPC):
                load(i // NPC, i % NPC, i % 2, i - 1)
            with sp.Fori(1, NE // 2) as k:
                for i in range(2 * NPC):
                    load(k * 2 + i // NPC, i % NPC, i % 2, k * (2 * NPC) + (i - 1))
            sp.wait_ge(xn_stored, 16 * BATCH)

        @block.gpsimd
        def _(pool):
            g = nc.gpsimd
            g.memset(ident[:], 0.0).then_inc(consts, 1)
            g.memset(less[:], 0.0).then_inc(consts, 1)
            g.memset(ones[:], 1.0).then_inc(consts, 1)
            g.memset(zrow[:], 0.0).then_inc(consts, 1)
            pool.wait_ge(consts, 2)
            g.affine_select(out=ident[:], in_=ident[:], compare_op=ALU.not_equal, fill=1.0, base=0,
                            pattern=[[-1, P]], channel_multiplier=1).then_inc(consts, 1)
            g.affine_select(out=less[:], in_=less[:], compare_op=ALU.is_ge, fill=1.0, base=0,
                            pattern=[[-1, P]], channel_multiplier=1).then_inc(consts, 1)
            ok = dict(allow_small_or_imprecise_dtypes=True)
            g.iota(lane[:], [[1, 1]], base=0, channel_multiplier=1, **ok).then_inc(consts, 1)
            g.iota(eno[:], [[1, NE]], base=-NE, channel_multiplier=0, **ok).then_inc(consts, 1)
            g.iota(dumps[:], [[P, NPAD]], base=DUMP, channel_multiplier=1, **ok).then_inc(consts, 1)
            g.iota(tails[:], [[P, SPARE]], base=0, channel_multiplier=1, **ok).then_inc(consts, 1)
            g.iota(tileno[:], [[1, EXPERT_TILES]], base=0, channel_multiplier=0, **ok).then_inc(consts, 1)

            def after(semaphore, count):
                pool.wait_ge(semaphore, count)
                pool.sem_inc(pool_turns, 1)

            def split(i, half, slot_at, loads, n):
                w, parts = PIECES[i]
                after(raw_loaded[half], loads)
                src = raw[0:parts, half, 0:w]
                hi, lo = piece(whi, slot_at, i), piece(wlo, slot_at, i)
                g.tensor_copy(hi, src).then_inc(hi_split, 1)
                pool.wait_ge(hi_split, n + 1)
                g.tensor_tensor(lo, src, hi.bitcast(F32), ALU.subtract).then_inc(lo_split, 1)

            for i in range(NPC):
                split(i, i % 2, 0, 16 * (i // 2 + 1), i)

            pool.wait_ge(routed, 1)
            for j in range(NPAD):
                g.indirect_dma_start(xg_d[:, :], bass.IndirectOffsetOnAxis(ap=pads[:, j:j + 1].bitcast(U32), axis=0),
                                     zrow[:], None).then_inc(padded, 16)
            for i in range(NT):
                for k in range(TOPK):
                    g.indirect_dma_start(xg_d[:, :],
                                         bass.IndirectOffsetOnAxis(ap=slot[:, k, i:i + 1].bitcast(U32), axis=0),
                                         xb[:, i, :], None).then_inc(sent, 16)
            pool.wait_ge(padded, 16 * NPAD)
            pool.wait_ge(sent, 16 * TOPK * NT)
            pool.wait_ge(xn_stored, 16 * BATCH)
            for i in range(NPC):
                n = NPC + i
                split(i, n % 2, WCOLS, 16 * (n // 2 + 1), n)
            with pool.Fori(1, NE // 2) as k:
                for e in range(2):
                    r = pool.value_load(released[0:1, bass.ds(k * 2 + e, 1)], min_val=1, max_val=EXPERT_TILES)
                    after(y_done, r)
                    for i in range(NPC):
                        n = e * NPC + i
                        split(i, n % 2, e * WCOLS, (k * NPC + (n // 2 + 1)) * 16, k * (2 * NPC) + n)

        @block.tensor
        def _(pe):
            mm = nc.tensor.matmul
            pe.wait_ge(consts, 6)

            def front_transpose(i):
                pe.wait_ge(xn_ready, i + 1)
                if i >= 2:
                    pe.wait_ge(front_hi, i - 1)
                    pe.wait_ge(front_lo, i - 1)
                bank = (tX, tA)[i % 2]
                for c in range(DC):
                    last = nc.tensor.transpose(bank[:, c * P:(c + 1) * P], xb[:, i, c * P:(c + 1) * P], ident[:])
                last.then_inc(front_xT, 1)

            def front_logits(i):
                pe.wait_ge(front_hi, i + 1)
                pe.wait_ge(front_lo, i + 1)
                h, l = ((xTh, xTl), (aTh, aTl))[i % 2]
                for c in range(DC):
                    last = three_passes(nc, logits[:, i * NE:(i + 1) * NE], h[:, c, :], l[:, c, :],
                                        gTh[:, c, :], gTl[:, c, :], c == 0, c == DC - 1)
                last.then_inc(logits_done, 1)

            pe.wait_ge(gate_split, 2)
            for i in range(NT):
                front_transpose(i)
                if i:
                    front_logits(i - 1)
            front_logits(NT - 1)
            pe.wait_ge(picked_ready, 1)
            mm(rank[:, 0:NT * NE], less[:], work[:], start=True, stop=False)
            mm(rank[:, 0:NT * NE], ones[:], before[:], start=False, stop=True)
            mm(total[:, 0:NE], ones[:], picked[:], start=True, stop=True).then_inc(rank_done, 1)

            def transpose_rows(n):
                pe.wait_ge(row_loaded, n * 16)
                for c in range(DC):
                    last = nc.tensor.transpose(tX[:, c * P:(c + 1) * P], xrow[:, c * P:(c + 1) * P], ident[:])
                last.then_inc(xT_done, 1)

            def up(n, part, base, at):
                f = (FA, FB)[part]
                pe.wait_ge(lo_split, base + (2 * part + 2))
                for w in range(2):
                    bank = ((hA1, hA3), (hB1, hB3))[part][w]
                    for c in range(DC):
                        o = PIECE_AT[2 * part + w] + c * f
                        last = three_passes(nc, bank[:, 0:f], xTh[:, c, :], xTl[:, c, :],
                                            whi[:, bass.ds(at + o, f)], wlo[:, bass.ds(at + o, f)],
                                            c == 0, c == DC - 1)
                last.then_inc((hA_done, hB_done)[part], 1)

            def transpose_act(n):
                pe.wait_ge(actA, n)
                pe.wait_ge(actB, n)
                for c in range(AC):
                    m = min(P, FF - c * P)
                    bank = (tA, tB)[c // 3 if c < 6 else 1]
                    o = c * P if c < 3 else (c - 3) * P
                    last = nc.tensor.transpose(bank[0:m, o:o + P], act[:, c * P:c * P + m], ident[:])
                last.then_inc(aT_done, 1)

            def down(n, base, at):
                pe.wait_ge(lo_split, base + NPC)
                pe.wait_ge(aT_hi, n)
                pe.wait_ge(aT_lo, n)
                if not isinstance(n, int) or n > 1:
                    pe.wait_ge(y_copied, n - 1)
                for c in range(AC):
                    m = min(P, FF - c * P)
                    o = PIECE_AT[4] + c * DM
                    last = three_passes(nc, yP[:, :], aTh[0:m, c, :], aTl[0:m, c, :],
                                        whi[0:m, bass.ds(at + o, DM)], wlo[0:m, bass.ds(at + o, DM)],
                                        c == 0, c == AC - 1)
                last.then_inc(y_done, 1)

            def place(n):
                base = pe.value_load(tile_waits[0:1, bass.ds(n, 1)], min_val=0, max_val=(NE - 1) * NPC)
                at = pe.value_load(tile_slots[0:1, bass.ds(n, 1)], min_val=0, max_val=WCOLS)
                return base, at

            def tile(n, before=True, after=True):
                base, at = place(n)
                pe.wait_ge(xT_hi, n + 1)
                pe.wait_ge(xT_lo, n + 1)
                up(n, 0, base, at)
                if before:
                    transpose_act(n)
                up(n, 1, base, at)
                if after:
                    transpose_rows(n + 2)
                if before:
                    down(n, *place(n - 1))

            pe.wait_ge(routed, 1)
            transpose_rows(1)
            tile(0, before=False)
            tile(1)
            with pe.Fori(2, EXPERT_TILES - 1) as n:
                tile(n)
            tile(EXPERT_TILES - 1, after=False)
            transpose_act(EXPERT_TILES)
            down(EXPERT_TILES, *place(EXPERT_TILES - 1))

        @block.scalar
        def _(a):
            s = nc.scalar
            a.wait_ge(var_ready, 1)
            s.activation(std[:], var[:], ACT.Sqrt).then_inc(std_ready, 1)
            for i in range(NT):
                a.wait_ge(front_xT, i + 1)
                if i >= 2:
                    a.wait_ge(logits_done, i - 1)
                h = (xTh[:], aTh[:, 0:DC, :])[i % 2]
                s.activation(h, (tX, tA)[i % 2][:].rearrange("p (c t) -> p c t", c=DC), ACT.Copy).then_inc(front_hi, 1)
            a.wait_ge(shifted, 1)
            s.activation(prob[:], work[:], ACT.Exp).then_inc(exp_done, 1)

            def load_rows(n):
                a.dma_start(xrow[:], xg_d[bass.ds(n * P, P), :]).then_inc(row_loaded, 16)

            def hi_xT(n):
                a.wait_ge(xT_done, n)
                s.activation(xTh[:], tX[:].rearrange("p (c t) -> p c t", c=DC), ACT.Copy).then_inc(xT_hi, 1)

            def hi_aT(n):
                a.wait_ge(aT_done, n)
                s.activation(aTh[:, 0:3, :], tA[:, 0:3 * P].rearrange("p (c t) -> p c t", c=3), ACT.Copy)
                s.activation(aTh[:, 3:6, :], tB[:, 0:3 * P].rearrange("p (c t) -> p c t", c=3), ACT.Copy)
                s.activation(aTh[0:FLAST, 6, :], tB[0:FLAST, 3 * P:4 * P], ACT.Copy).then_inc(aT_hi, 1)

            def gate_part(n, part):
                a.wait_ge((hA_done, hB_done)[part], n + 1)
                if not isinstance(n, int) or n:
                    a.wait_ge((actA, actB)[part], n)
                f0, f = (0, FA)[part], (FA, FB)[part]
                s.activation(silu[:, f0:f0 + f], (hA1, hB1)[part][:, 0:f], ACT.Silu).then_inc((siluA, siluB)[part], 1)

            def store_y(n):
                a.wait_ge(y_done, n)
                if not isinstance(n, int) or n > 1:
                    a.wait_ge(y_stored, (n - 1) * 16)
                s.activation(ysb[:], yP[:], ACT.Copy).then_inc(y_copied, 1)
                a.wait_ge(y_copied, n)
                a.dma_start(y_d[bass.ds((n - 1) * P, P), :], ysb[:]).then_inc(y_stored, 16)

            def tile(n, before=True, after=True, fetch=True):
                gate_part(n, 0)
                if before:
                    hi_aT(n)
                gate_part(n, 1)
                if after:
                    hi_xT(n + 2)
                    if fetch:
                        load_rows(n + 2)
                if before:
                    store_y(n)

            a.wait_ge(padded, 16 * NPAD)
            a.wait_ge(sent, 16 * TOPK * NT)
            load_rows(0)
            hi_xT(1)
            load_rows(1)
            tile(0, before=False)
            tile(1)
            with a.Fori(2, EXPERT_TILES - 2) as n:
                tile(n)
            tile(EXPERT_TILES - 2, fetch=False)
            tile(EXPERT_TILES - 1, after=False)
            hi_aT(EXPERT_TILES)
            store_y(EXPERT_TILES)
            a.wait_ge(y_stored, EXPERT_TILES * 16)

        @block.vector
        def _(d):
            v = nc.vector
            links = [0]

            def link(ins):
                links[0] += 1
                ins.then_inc(dve_chain, 1)
                d.wait_ge(dve_chain, links[0])

            def over_experts(ap):
                return ap.unsqueeze(2).to_broadcast([P, NT, NE])

            def over_tiles(ap):
                return ap.unsqueeze(1).to_broadcast([P, NT, NE])

            d.wait_ge(gate_loaded, 16)
            v.tensor_copy(gTh[:], gTf[:]).then_inc(gate_split, 1)
            d.wait_ge(gate_split, 1)
            v.tensor_tensor(gTl[:], gTf[:], gTh[:].bitcast(F32), ALU.subtract).then_inc(gate_split, 1)
            for b in range(BATCH):
                d.wait_ge(x_loaded[b], 16)
                for i in range(TPB * b, TPB * (b + 1)):
                    last = v.bn_stats(stats[:, i, :], xb[:, i, :])
            link(last)
            for i in range(NT):
                last = v.bn_aggr(mv[:, i, :], stats[:, i, :])
            link(last)
            link(v.tensor_scalar(var[:], mv[:, :, 1], EPS, None, ALU.add))
            v.tensor_scalar(tmp[:], var[:], 0.5, None, ALU.mult).then_inc(var_ready, 1)
            d.wait_ge(std_ready, 1)
            link(v.reciprocal(rstd[:], std[:]))
            link(v.tensor_tensor(tmp[:], tmp[:], rstd[:], ALU.mult))
            link(v.tensor_tensor(tmp[:], tmp[:], rstd[:], ALU.mult))
            link(v.tensor_scalar(tmp[:], tmp[:], -1.0, 1.5, ALU.mult, ALU.add))
            link(v.tensor_tensor(rstd[:], rstd[:], tmp[:], ALU.mult))

            def normalise(i):
                v.tensor_scalar(xb[:, i, :], xb[:, i, :], mv[:, i, 0:1], rstd[:, i:i + 1], ALU.subtract, ALU.mult)\
                    .then_inc(xn_ready, 1)

            normalise(0)
            for i in range(NT):
                if i + 1 < NT:
                    normalise(i + 1)
                d.wait_ge(front_hi, i + 1)
                l, h = ((xTl[:], xTh[:]), (aTl[:, 0:DC, :], aTh[:, 0:DC, :]))[i % 2]
                v.tensor_tensor(l, (tX, tA)[i % 2][:].rearrange("p (c t) -> p c t", c=DC), h.bitcast(F32),
                                ALU.subtract).then_inc(front_lo, 1)
            d.wait_ge(logits_done, NT)
            lg = logits[:, 0:NT * NE].rearrange("p (i e) -> p i e", e=NE)
            link(v.tensor_reduce(col[:, 0, :], lg, AX, ALU.max, negate=True))
            v.tensor_tensor(work[:], lg, over_experts(col[:, 0, :]), ALU.add).then_inc(shifted, 1)
            d.wait_ge(exp_done, 1)
            link(v.tensor_reduce(col[:, 1, :], prob[:], AX, ALU.add))
            link(v.reciprocal(col[:, 2, :], col[:, 1, :]))
            link(v.tensor_tensor(prob[:], prob[:], over_experts(col[:, 2, :]), ALU.mult))

            def pick(chosen, top):
                link(v.tensor_reduce(top, prob[:], AX, ALU.max))
                link(v.tensor_tensor(work[:], prob[:], over_experts(top), ALU.is_equal))
                link(v.tensor_tensor(work[:], work[:], over_tiles(eno[:]), ALU.mult))
                link(v.tensor_reduce(col[:, 2, :], work[:], AX, ALU.min))
                link(v.tensor_tensor(chosen[:], over_tiles(eno[:]), over_experts(col[:, 2, :]), ALU.is_equal))

            d.wait_ge(consts, 11)
            pick(first, col[:, 0, :])
            link(v.scalar_tensor_tensor(prob[:], first[:], -2.0, prob[:], ALU.mult, ALU.add))
            pick(second, col[:, 1, :])
            link(v.tensor_tensor(col[:, 2, :], col[:, 0, :], col[:, 1, :], ALU.add))
            link(v.reciprocal(col[:, 3, :], col[:, 2, :]))
            v.tensor_tensor(gates[:, 0, :], col[:, 0, :], col[:, 3, :], ALU.mult)
            v.tensor_tensor(gates[:, 1, :], col[:, 1, :], col[:, 3, :], ALU.mult)
            v.memset(before[:, 0, :], 0.0)
            link(v.tensor_tensor(work[:], first[:], second[:], ALU.add))
            for i in range(1, NT):
                link(v.tensor_tensor(before[:, i, :], before[:, i - 1, :], work[:, i - 1, :], ALU.add))
            v.tensor_tensor(picked[:], before[:, NT - 1, :], work[:, NT - 1, :], ALU.add).then_inc(picked_ready, 1)
            d.wait_ge(rank_done, 1)
            rows, tiles, ends, starts, cond, spare = (need[:, i, :] for i in range(6))
            link(v.tensor_copy(rows, total[:, 0:NE]))
            link(v.tensor_scalar(needi[:], rows, float(P - 1), None, ALU.add))
            link(v.tensor_single_scalar(needi[:], needi[:], P.bit_length() - 1, op=ALU.arith_shift_right))
            link(v.tensor_scalar(tiles, needi[:], 1.0, None, ALU.max))
            link(v.tensor_copy(ends[:, 0:1], tiles[:, 0:1]))
            for e in range(1, NE):
                link(v.tensor_tensor(ends[:, e:e + 1], ends[:, e - 1:e], tiles[:, e:e + 1], ALU.add))
            link(v.tensor_tensor(starts, ends, tiles, ALU.subtract))
            link(v.tensor_scalar(starts, starts, float(P), None, ALU.mult))
            link(v.tensor_tensor(work[:], rank[:, 0:NT * NE].rearrange("p (i e) -> p i e", e=NE), over_tiles(starts), ALU.add))
            link(v.tensor_tensor(first[:], first[:], work[:], ALU.mult))
            link(v.tensor_tensor(second[:], second[:], work[:], ALU.mult))
            v.tensor_reduce(col[:, 0, :], first[:], AX, ALU.add)
            link(v.tensor_reduce(col[:, 1, :], second[:], AX, ALU.add))
            v.tensor_copy(slot[:, 0, :], col[:, 0, :])
            v.tensor_copy(slot[:, 1, :], col[:, 1, :])
            want, take, use = (padf[:, i, :] for i in range(3))
            v.tensor_tensor(want[:, 0:NE], starts, rows, ALU.add)
            link(v.scalar_tensor_tensor(spare, tiles, float(P), rows, ALU.mult, ALU.subtract))
            link(v.tensor_scalar(want[:, 0:NE], want[:, 0:NE], lane[:, 0:1], None, ALU.add))
            v.tensor_scalar(take[:, 0:NE], spare, lane[:, 0:1], None, ALU.is_gt)
            link(v.tensor_scalar(cond[:, 0:1], ends[:, NE - 1:NE], float(P), None, ALU.mult))
            link(v.tensor_scalar(want[:, NE:], tails[:], cond[:, 0:1], None, ALU.add))
            link(v.tensor_scalar(take[:, NE:], want[:, NE:], float(SLOTS), None, ALU.is_lt))
            link(v.tensor_tensor(use, want, dumps[:], ALU.subtract))
            link(v.tensor_tensor(use, use, take, ALU.mult))
            link(v.tensor_tensor(use, use, dumps[:], ALU.add))
            v.tensor_copy(pads[:], use)
            link(v.tensor_tensor(cmp[:], ends[0:1, 0:NE - 1].unsqueeze(1).to_broadcast([1, EXPERT_TILES, NE - 1]),
                                 tileno[:].unsqueeze(2).to_broadcast([1, EXPERT_TILES, NE - 1]), ALU.is_le))
            link(v.tensor_reduce(texp[:], cmp[:], AX, ALU.add))
            v.tensor_scalar(tile_waits[:], texp[:], float(NPC), None, ALU.mult)
            link(v.tensor_copy(texi[:], texp[:]))
            link(v.tensor_single_scalar(texi[:], texi[:], 1, op=ALU.bitwise_and))
            v.tensor_scalar(tile_slots[:], texi[:], float(WCOLS), None, ALU.mult)
            link(v.memset(released[:], 0))
            v.tensor_copy(released[0:1, 2:NE], ends[0:1, 0:NE - 2]).then_inc(routed, 1)

            def up_part(n, part):
                d.wait_ge((siluA, siluB)[part], n + 1)
                d.wait_ge((hA_done, hB_done)[part], n + 1)
                if not isinstance(n, int) or n:
                    d.wait_ge(aT_done, n)
                f0, f = (0, FA)[part], (FA, FB)[part]
                v.tensor_tensor(act[:, f0:f0 + f], silu[:, f0:f0 + f], (hA3, hB3)[part][:, 0:f], ALU.mult)\
                    .then_inc((actA, actB)[part], 1)

            def lo_xT(n):
                d.wait_ge(xT_hi, n)
                v.tensor_tensor(xTl[:], tX[:].rearrange("p (c t) -> p c t", c=DC), xTh[:].bitcast(F32),
                                ALU.subtract).then_inc(xT_lo, 1)

            def lo_aT(n):
                d.wait_ge(aT_hi, n)
                v.tensor_tensor(aTl[:, 0:3, :], tA[:, 0:3 * P].rearrange("p (c t) -> p c t", c=3),
                                aTh[:, 0:3, :].bitcast(F32), ALU.subtract)
                v.tensor_tensor(aTl[:, 3:6, :], tB[:, 0:3 * P].rearrange("p (c t) -> p c t", c=3),
                                aTh[:, 3:6, :].bitcast(F32), ALU.subtract)
                v.tensor_tensor(aTl[0:FLAST, 6, :], tB[0:FLAST, 3 * P:4 * P],
                                aTh[0:FLAST, 6, :].bitcast(F32), ALU.subtract).then_inc(aT_lo, 1)

            def tile(n, before=True, after=True):
                up_part(n, 0)
                if before:
                    lo_aT(n)
                up_part(n, 1)
                if after:
                    lo_xT(n + 2)

            lo_xT(1)
            tile(0, before=False)
            with d.Fori(1, EXPERT_TILES - 1) as n:
                tile(n)
            tile(EXPERT_TILES - 1, after=False)
            lo_aT(EXPERT_TILES)


def attention_half(nc, t, banks, x, xn_d, y_d, conv_w, columns, wq, wk, wv, bv, wo, proj_w, proj_b, out):
    ctx = ExitStack()
    with ctx:
        def sb(name, shape, dt=F32):
            return ctx.enter_context(nc.sbuf_tensor(name, shape, dt))

        def sem(name):
            return ctx.enter_context(nc.semaphore(name))

        ident, slot, gates = t["ident"], t["slot"], t["gates"]
        TAPS, PROJ = 3, 3
        NO = W * PROJ
        HP = H // 2
        GH = 8
        GP = GH // 2
        STEPS = TPB * H // GH
        LP = LEN + 2
        cwh, cwl = sb("cwh", [P, TAPS * DC, NO], F32R), sb("cwl", [P, TAPS * DC, NO], F32R)
        pwh, pwl = sb("pwh", [P, PROJ, H * DH], F32R), sb("pwl", [P, PROJ, H * DH], F32R)
        wo_s, pj_s = sb("wo_s", [P, HP, W]), sb("pj_s", [P, DM])
        qk = sb("qk", [P, 2, HP, LEN])
        cwf = qk[:].rearrange("p a b c -> p (a b c)")[:, 0:TAPS * DC * NO].rearrange("p (a b) -> p a b", b=NO)
        pwf = qk[:].rearrange("p a b c -> p (a b c)")[:, TAPS * DC * NO:TAPS * DC * NO + PROJ * H * DH]\
            .rearrange("p (a b) -> p a b", b=H * DH)
        xs = sb("xs", [P, 2, DM])
        xTh, xTl = sb("axTh", [P, DC, LP], F32R), sb("axTl", [P, DC, LP], F32R)
        qkvh, qkvl = sb("qkvh", [P, PROJ, LEN], F32R), sb("qkvl", [P, PROJ, LEN], F32R)
        vh = sb("vh", [P, TPB, H * DH])
        s = sb("s", [P, 2, GH, P])
        pT = sb("pT", [P, GH, P])
        nmax, rsum = sb("nmax", [P, 2, GH]), sb("rsum", [P, 4, GH])
        rinv = sb("rinv", [P, 2, GH])
        o = sb("o", [P, 2, GH * DH])
        oT = sb("oT", [P, HP, LEN])
        att = sb("att", [P, LEN])
        res = sb("res", [P, 2, DM])
        ye = sb("ye", [P, TOPK, DM])
        idx, gate = sb("idx", [P, TOPK], I32), sb("gate", [P, TOPK])
        mask = sb("mask", [P, P])
        cols = sb("cols", [P, PROJ + 2 * HP + 1])
        cb, bqs, bks, bos = (cols[:, a:z] for a, z in ((0, PROJ), (PROJ, PROJ + HP), (PROJ + HP, PROJ + 2 * HP),
                                                       (PROJ + 2 * HP, PROJ + 2 * HP + 1)))
        bvb, pjb = sb("bvb", [P, H * DH]), sb("pjb", [P, DM])

        pool_turns, sp_turns = sem("a_pool_turns"), sem("a_sp_turns")
        weights_loaded, small_loaded = sem("weights_loaded"), sem("small_loaded")
        weights_hi, weights_lo = sem("weights_hi"), sem("weights_lo")
        bias_scaled, zeroed, masked_ready = sem("bias_scaled"), sem("zeroed"), sem("masked_ready")
        xs_loaded, xs_T = [sem("xs_loaded0"), sem("xs_loaded1")], sem("xs_T")
        x_hi, x_lo = sem("x_hi"), sem("x_lo")
        conv_done, conv_hi, conv_lo = sem("conv_done"), sem("conv_hi"), sem("conv_lo")
        proj_done, q_ready, kv_ready = sem("proj_done"), sem("q_ready"), sem("kv_ready")
        s_done, masked, maxed, p_ready = sem("s_done"), sem("masked"), sem("maxed"), sem("p_ready")
        pT_done, pT_ready, pv_done = sem("pT_done"), sem("pT_ready"), sem("pv_done")
        inv_ready = sem("inv_ready")
        o_ready, oT_done, oT_ready = sem("o_ready"), sem("oT_done"), sem("oT_ready")
        wo_done, att_ready, out_done, out_ready = sem("wo_done"), sem("att_ready"), sem("out_done"), sem("out_ready")
        picked, gathered = sem("picked_cols"), sem("gathered")
        out_stored, res_loaded = ([sem(f"{name}{i}") for i in range(2)] for name in ("out_stored", "res_loaded"))
        scaled, res_ready, pool_chain = sem("scaled"), sem("res_ready"), sem("res_parts")

        block = ctx.enter_context(nc.Block())

        def turn(b, n):
            return b * (TPB // 2) + (n // 2 + 1)

        def batches(eng, body):
            with eng.Fori(0, BATCH - 1) as b:
                body(b, True)
            body(BATCH - 1, False)

        @block.sync
        def _(sp):
            sp.dma_start(cwf, conv_w.rearrange("t (c p) o -> p (t c) o", p=P)).then_inc(weights_loaded, 16)
            for n, w in enumerate((wq, wk, wv)):
                sp.dma_start(pwf[:, n, :], w.rearrange("d h e -> d (h e)")).then_inc(weights_loaded, 16)
            for n in range(TPB):
                if n >= 2:
                    sp.wait_ge(xs_T, n - 1)
                sp.dma_start(xs[:, n % 2, :], xn_d[n * P:(n + 1) * P, :]).then_inc(xs_loaded[n % 2], 16)
            sp.dma_start(wo_s[:], wo.rearrange("h e w -> (h e) w").rearrange("(c p) w -> p c w", p=P)).then_inc(small_loaded, 16)
            sp.dma_start(pj_s[:], proj_w).then_inc(small_loaded, 16)

            def body(b, more):
                if more:
                    for n in range(TPB):
                        i = (b + 1) * TPB + n
                        sp.wait_ge(xs_T, i - 1)
                        sp.sem_inc(sp_turns, 1)
                        sp.dma_start(xs[:, n % 2, :], xn_d[bass.ds(i * P, P), :]).then_inc(xs_loaded[n % 2], 16)
                for n in range(TPB + 2):
                    if n < TPB:
                        i = b * TPB + n
                        if n >= 2:
                            sp.wait_ge(out_stored[n % 2], (turn(b, n) - 1) * 16)
                            sp.sem_inc(sp_turns, 1)
                        sp.dma_start(res[:, n % 2, :], x[bass.ds(i * P, P), :]).then_inc(res_loaded[n % 2], 16)
                    if 1 <= n <= TPB:
                        i = b * TPB + n - 1
                        sp.wait_ge(out_ready, i + 1)
                        sp.sem_inc(sp_turns, 1)
                        sp.dma_start(out[bass.ds(i * P, P), :], res[:, (n - 1) % 2, :]).then_inc(out_stored[(n - 1) % 2], 16)
                for buf in range(2):
                    sp.wait_ge(out_stored[buf], (b + 1) * (TPB // 2 * 16))
                    sp.sem_inc(sp_turns, 1)

            batches(sp, body)

        @block.gpsimd
        def _(pool):
            g = nc.gpsimd
            g.memset(mask[:], BIG).then_inc(masked_ready, 1)
            pool.wait_ge(masked_ready, 1)
            g.affine_select(out=mask[:], in_=mask[:], compare_op=ALU.is_ge, fill=NEG, base=0,
                            pattern=[[-1, P]], channel_multiplier=1).then_inc(masked_ready, 1)
            for z in (xTh, xTl):
                for col in (0, LP - 1):
                    g.memset(z[:, :, col:col + 1].bitcast(F32), 0.0).then_inc(zeroed, 1)
            pool.wait_ge(small_loaded, 16 * SMALL)

            def after(semaphore, count):
                pool.wait_ge(semaphore, count)
                pool.sem_inc(pool_turns, 1)

            def body(b, more):
                for n in range(TPB):
                    i = b * TPB + n
                    g.tensor_copy(idx[:], slot[:, :, bass.ds(i, 1)].rearrange("p k a -> p (k a)")).then_inc(picked, 1)
                    g.tensor_copy(gate[:], gates[:, :, bass.ds(i, 1)].rearrange("p k a -> p (k a)")).then_inc(picked, 1)
                    after(picked, (i + 1) * 2)
                    for k in range(TOPK):
                        g.indirect_dma_start(ye[:, k, :], None, y_d[:, :],
                                             bass.IndirectOffsetOnAxis(ap=idx[:, k:k + 1].bitcast(U32), axis=0))\
                            .then_inc(gathered, 16)
                    r = res[:, n % 2, :]
                    pool.wait_ge(res_loaded[n % 2], turn(b, n) * 16)
                    g.tensor_tensor(r, r, pjb[:], ALU.add).then_inc(pool_chain, 1)
                    after(gathered, (i + 1) * (16 * TOPK))
                    for k in range(TOPK):
                        g.tensor_scalar(ye[:, k, :], ye[:, k, :], gate[:, k:k + 1], None, ALU.mult).then_inc(scaled, 1)
                    pool.wait_ge(scaled, (i + 1) * TOPK)
                    pool.wait_ge(pool_chain, i * 2 + 1)
                    g.tensor_tensor(r, r, ye[:, 0, :], ALU.add).then_inc(pool_chain, 1)
                    pool.wait_ge(pool_chain, i * 2 + 2)
                    g.tensor_tensor(r, r, ye[:, 1, :], ALU.add).then_inc(res_ready, 1)
                    after(res_ready, i + 1)

            batches(pool, body)

        def conv_splits():
            for n in range(0, TAPS * DC, 3):
                yield cwh[:, n:n + 3, :], cwl[:, n:n + 3, :], cwf[:, n:n + 3, :]
            for n in range(PROJ):
                yield pwh[:, n, :], pwl[:, n, :], pwf[:, n, :]

        SPLITS = TAPS * DC // 3 + PROJ

        @block.tensor
        def _(pe):
            mm = nc.tensor.matmul

            def transpose_x(b, n):
                i = b * TPB + n
                pe.wait_ge(xs_loaded[n % 2], turn(b, n) * 16)
                if n >= 2:
                    pe.wait_ge(x_hi, i - 1)
                    pe.wait_ge(x_lo, i - 1)
                bank = banks[7 - n % 2]
                for c in range(DC):
                    last = nc.tensor.transpose(bank[:, c * P:(c + 1) * P], xs[:, n % 2, c * P:(c + 1) * P], ident[:])
                last.then_inc(xs_T, 1)

            for n in range(TPB):
                transpose_x(0, n)
            pe.wait_ge(zeroed, 4)
            pe.wait_ge(weights_lo, SPLITS)
            pe.wait_ge(small_loaded, 16 * SMALL)

            def body(b, more):
                pe.wait_ge(x_hi, (b + 1) * TPB)
                pe.wait_ge(x_lo, (b + 1) * TPB)
                for n in range(PROJ):
                    for j in range(TAPS * DC):
                        tap, c = j // DC, j % DC
                        last = three_passes(nc, banks[n][:], cwh[:, j, n * W:(n + 1) * W], cwl[:, j, n * W:(n + 1) * W],
                                            xTh[:, c, tap:tap + LEN], xTl[:, c, tap:tap + LEN],
                                            j == 0, j == TAPS * DC - 1)
                    last.then_inc(conv_done, 1)
                if more:
                    for n in range(TPB):
                        transpose_x(b + 1, n)
                pe.wait_ge(conv_hi, (b + 1) * PROJ)
                pe.wait_ge(conv_lo, (b + 1) * PROJ)
                for r in range(2 * HP + 2 * TPB):
                    if r >= 4:
                        r4 = r - 4
                        if r4 < 2 * HP and r4 % 2 == 0:
                            pe.wait_ge(q_ready, b * HP + (r4 // 2 + 1))
                        elif r4 < 2 * HP:
                            pe.wait_ge(kv_ready, b * (HP + 2 * TPB) + (r4 // 2 + 1))
                        else:
                            pe.wait_ge(kv_ready, b * (HP + 2 * TPB) + (r4 - HP + 1))
                    bank = banks[r % 4][:]
                    if r < 2 * HP:
                        c, w = r // 2, r % 2
                        last = three_passes(nc, bank, pwh[:, w, c * P:(c + 1) * P], pwl[:, w, c * P:(c + 1) * P],
                                            qkvh[:, w, :], qkvl[:, w, :])
                    else:
                        blk, half = (r - 2 * HP) // 2, r % 2
                        last = three_passes(nc, bank, qkvh[:, 2, blk * P:(blk + 1) * P], qkvl[:, 2, blk * P:(blk + 1) * P],
                                            pwh[:, 2, half * 512:(half + 1) * 512], pwl[:, 2, half * 512:(half + 1) * 512])
                    last.then_inc(proj_done, 1)
                pe.wait_ge(q_ready, (b + 1) * HP)
                pe.wait_ge(kv_ready, (b + 1) * (HP + 2 * TPB))

                def scores(g):
                    blk, hh = g // 2, g % 2
                    if g >= 2:
                        pe.wait_ge(masked, b * STEPS + (g - 1))
                    for pr in range(GP):
                        for half in range(2):
                            rows = slice(64 * half, 64 * half + 64)
                            tok = slice(blk * P, (blk + 1) * P)
                            last = mm(banks[2 * (g % 2) + half][:, pr * P:(pr + 1) * P],
                                      qk[rows, 0, hh * GP + pr, tok], qk[rows, 1, hh * GP + pr, tok],
                                      start=True, stop=True)
                    last.then_inc(s_done, 1)

                def transpose_o(g):
                    pe.wait_ge(o_ready, b * STEPS + (g + 1))
                    if g:
                        pe.wait_ge(oT_ready, b * STEPS + g)
                    for c in range(GP):
                        last = nc.tensor.transpose(banks[7][:, c * P:(c + 1) * P], o[:, g % 2, c * P:(c + 1) * P], ident[:])
                    last.then_inc(oT_done, 1)

                scores(0)
                scores(1)
                for g in range(STEPS):
                    pe.wait_ge(p_ready, b * STEPS + (g + 1))
                    if g:
                        pe.wait_ge(pT_ready, b * STEPS + g)
                    for j in range(GH):
                        last = nc.tensor.transpose(banks[4 + j // GP][:, (j % GP) * P:(j % GP + 1) * P],
                                                   s[:, g % 2, j, :], ident[:])
                    last.then_inc(pT_done, 1)
                    if g + 2 < STEPS:
                        scores(g + 2)
                    pe.wait_ge(pT_ready, b * STEPS + (g + 1))
                    if g:
                        pe.wait_ge(o_ready, b * STEPS + g)
                    blk, hh = g // 2, g % 2
                    for h in range(GH):
                        j = (h % 2) * GP + h // 2
                        at = (hh * GH + h) * DH
                        last = mm(banks[6][:, h * DH:(h + 1) * DH], pT[:, j, :], vh[:, blk, at:at + DH],
                                  start=True, stop=True)
                    last.then_inc(pv_done, 1)
                    if g:
                        transpose_o(g - 1)
                transpose_o(STEPS - 1)
                pe.wait_ge(oT_ready, (b + 1) * STEPS)
                for c in range(HP):
                    last = mm(banks[7][:], wo_s[:, c, :], oT[:, c, :], start=c == 0, stop=c == HP - 1)
                last.then_inc(wo_done, 1)
                pe.wait_ge(att_ready, b + 1)
                for n in range(TPB):
                    mm(banks[n][:], att[:, n * P:(n + 1) * P], pj_s[:], start=True, stop=True).then_inc(out_done, 1)
                pe.wait_ge(out_ready, (b + 1) * TPB)

            batches(pe, body)

        @block.scalar
        def _(a):
            sc = nc.scalar
            a.dma_start(cols[:], columns).then_inc(small_loaded, 16)
            a.dma_start(bvb[:], bv.rearrange("h e -> (h e)").rearrange("(n w) -> n w", n=1).to_broadcast([P, H * DH]))\
                .then_inc(small_loaded, 16)
            a.dma_start(pjb[:], proj_b.rearrange("(n w) -> n w", n=1).to_broadcast([P, DM])).then_inc(small_loaded, 16)
            a.wait_ge(weights_loaded, 16 * 4)
            for hi, _, src in conv_splits():
                sc.activation(hi, src, ACT.Copy).then_inc(weights_hi, 1)

            def hi_x(i, n):
                a.wait_ge(xs_T, i + 1)
                sc.activation(xTh[:, :, 1 + n * P:1 + (n + 1) * P], banks[7 - n % 2][:].rearrange("p (c t) -> p c t", c=DC),
                              ACT.Copy).then_inc(x_hi, 1)

            for n in range(TPB):
                hi_x(n, n)
            a.wait_ge(bias_scaled, 1)
            a.wait_ge(small_loaded, 16 * SMALL)

            def body(b, more):
                for n in range(PROJ):
                    a.wait_ge(conv_done, b * PROJ + (n + 1))
                    sc.activation(qkvh[:, n, :], banks[n][:], ACT.Identity, bias=cb[:, n:n + 1]).then_inc(conv_hi, 1)
                if more:
                    for n in range(TPB):
                        hi_x((b + 1) * TPB + n, n)
                NP = 2 * HP + 2 * TPB
                for c in range(HP):
                    a.wait_ge(proj_done, b * NP + (2 * c + 1))
                    sc.activation(qk[:, 0, c, :], banks[2 * c % 4][:], ACT.Identity, bias=bqs[:, c:c + 1], scale=SCALE)\
                        .then_inc(q_ready, 1)

                def exps(g):
                    a.wait_ge(maxed, b * STEPS + (g + 1))
                    for j in range(GH):
                        last = sc.activation(s[:, g % 2, j, :], s[:, g % 2, j, :], ACT.Exp, bias=nmax[:, g % 2, j:j + 1],
                                             accum_out=rsum[:, g % 4, j:j + 1])
                    last.then_inc(p_ready, 1)

                exps(0)
                for g in range(STEPS):
                    if g + 1 < STEPS:
                        exps(g + 1)
                    if g:
                        oT_copy(b, g - 1)
                oT_copy(b, STEPS - 1)
                a.wait_ge(wo_done, b + 1)
                sc.activation(att[:], banks[7][:], ACT.Identity, bias=bos).then_inc(att_ready, 1)

            def oT_copy(b, g):
                a.wait_ge(oT_done, b * STEPS + (g + 1))
                blk, hh = g // 2, g % 2
                sc.activation(oT[:, hh * GP:(hh + 1) * GP, blk * P:(blk + 1) * P],
                              banks[7][:].rearrange("p (c t) -> p c t", c=GP), ACT.Copy).then_inc(oT_ready, 1)

            batches(a, body)

        @block.vector
        def _(d):
            v = nc.vector
            for n, (hi, lo, src) in enumerate(conv_splits()):
                d.wait_ge(weights_hi, n + 1)
                v.tensor_tensor(lo, src, hi.bitcast(F32), ALU.subtract).then_inc(weights_lo, 1)
            d.wait_ge(small_loaded, 16 * SMALL)
            v.tensor_scalar(bqs, bqs, SCALE, None, ALU.mult).then_inc(bias_scaled, 1)
            d.wait_ge(masked_ready, 2)

            def lo_x(i, n):
                d.wait_ge(x_hi, i + 1)
                dst = slice(1 + n * P, 1 + (n + 1) * P)
                v.tensor_tensor(xTl[:, :, dst], banks[7 - n % 2][:].rearrange("p (c t) -> p c t", c=DC),
                                xTh[:, :, dst].bitcast(F32), ALU.subtract).then_inc(x_lo, 1)

            for n in range(TPB):
                lo_x(n, n)

            def body(b, more):
                for n in range(PROJ):
                    d.wait_ge(conv_hi, b * PROJ + (n + 1))
                    v.scalar_tensor_tensor(qkvl[:, n, :], banks[n][:], cb[:, n:n + 1], qkvh[:, n, :].bitcast(F32),
                                           ALU.add, ALU.subtract).then_inc(conv_lo, 1)
                if more:
                    for n in range(TPB):
                        lo_x((b + 1) * TPB + n, n)
                NP = 2 * HP + 2 * TPB
                for c in range(HP):
                    d.wait_ge(proj_done, b * NP + (2 * c + 2))
                    v.tensor_scalar(qk[:, 1, c, :], banks[(2 * c + 1) % 4][:], bks[:, c:c + 1], None, ALU.add)\
                        .then_inc(kv_ready, 1)
                for r in range(2 * TPB):
                    d.wait_ge(proj_done, b * NP + (2 * HP + r + 1))
                    half = slice((r % 2) * 512, (r % 2) * 512 + 512)
                    v.tensor_tensor(vh[:, r // 2, half], banks[r % 4][:], bvb[:, half], ALU.add).then_inc(kv_ready, 1)

                def mask_max(g):
                    d.wait_ge(s_done, b * STEPS + (g + 1))
                    for half in range(2):
                        last = v.tensor_tensor(s[:, g % 2, half * GP:(half + 1) * GP, :],
                                               banks[2 * (g % 2) + half][:].rearrange("p (j k) -> p j k", j=GP),
                                               mask[:].unsqueeze(1).to_broadcast([P, GP, P]), ALU.min)
                    last.then_inc(masked, 1)
                    d.wait_ge(masked, b * STEPS + (g + 1))
                    v.tensor_reduce(nmax[:, g % 2, :], s[:, g % 2, :, :], AX, ALU.max, negate=True).then_inc(maxed, 1)

                mask_max(0)
                mask_max(1)
                for g in range(STEPS):
                    d.wait_ge(pT_done, b * STEPS + (g + 1))
                    for half in range(2):
                        last = v.tensor_copy(pT[:, half * GP:(half + 1) * GP, :],
                                             banks[4 + half][:].rearrange("p (j k) -> p j k", j=GP))
                    last.then_inc(pT_ready, 1)
                    v.reciprocal(rinv[:, g % 2, :], rsum[:, g % 4, :]).then_inc(inv_ready, 1)
                    if g + 2 < STEPS:
                        mask_max(g + 2)
                    d.wait_ge(pv_done, b * STEPS + (g + 1))
                    d.wait_ge(inv_ready, b * STEPS + (g + 1))
                    v.tensor_tensor(o[:, g % 2, :].rearrange("p (c a e) -> p c a e", a=2, e=DH),
                                    banks[6][:].rearrange("p (c a e) -> p c a e", a=2, e=DH),
                                    rinv[:, g % 2, :].rearrange("p (a c) -> p c a", a=2).unsqueeze(3)
                                    .to_broadcast([P, GP, 2, DH]), ALU.mult).then_inc(o_ready, 1)
                for n in range(TPB):
                    i = b * TPB + n
                    d.wait_ge(out_done, i + 1)
                    d.wait_ge(res_ready, i + 1)
                    v.tensor_tensor(res[:, n % 2, :], banks[n][:], res[:, n % 2, :], ALU.add).then_inc(out_ready, 1)

            batches(d, body)


SMALL = 5


_OUT = ((TOK, DM), "float32")


def kernel(**inputs):
    import numpy as _np
    import concourse.bacc as _bacc
    from concourse import mybir as _mybir
    from concourse.bass_utils import run_bass_kernel_spmd as _run

    g = {k.replace("L0_attn_", "").replace("L0_ffn_", "ffn_"): _np.asarray(v) for k, v in inputs.items()}

    def chunked(w, rows):
        e, r, c = w.shape
        return w.reshape(e, r // rows, rows, c).transpose(0, 2, 1, 3).reshape(e, rows, -1)

    w1, w3, w2 = (g[k].transpose(0, 2, 1) for k in ("ffn_w1", "ffn_w3", "ffn_w2"))
    last = _np.zeros((NE, P, DM), w2.dtype)
    last[:, :FLAST] = w2[:, (AC - 1) * P:]
    experts = _np.concatenate(
        [chunked(w[:, :, f], P) for f in (slice(0, FA), slice(FA, FF)) for w in (w1, w3)]
        + [chunked(w2[:, :(AC - 1) * P], P), last], axis=2)
    arrays = {
        "x": g["inputs"].reshape(TOK, DM),
        "conv_w": g["conv_w"],
        "columns": _np.concatenate([g[k].reshape(-1, P).T for k in ("conv_b", "bq", "bk", "bo")], axis=1),
        **{k: g[k] for k in ("wq", "wk", "wv", "bv", "wo", "proj_w", "proj_b")},
        "gate": g["ffn_gate_w"].T.reshape(DC, P, NE).transpose(1, 0, 2),
        "experts": experts,
    }
    arrays = {k: _np.ascontiguousarray(v) for k, v in arrays.items()}
    nc = _bacc.Bacc("TRN2", target_bir_lowering=False, num_devices=1)
    args = [nc.dram_tensor(f"in_{k}", v.shape, _mybir.dt.from_np(v.dtype), kind="ExternalInput").ap()
            for k, v in arrays.items()]
    out = nc.dram_tensor("out_0", _OUT[0], _mybir.dt.from_np(_np.dtype(_OUT[1])), kind="ExternalOutput").ap()
    build(nc, *args, out)
    r = _run(nc, [{f"in_{k}": v for k, v in arrays.items()}], core_ids=[0])
    return _np.asarray(r.results[0]["out_0"]).reshape(BATCH, LEN, DM)
```

```python
import concourse.bass as bass
from concourse import mybir
from contextlib import ExitStack

F32 = mybir.dt.float32
F32R = mybir.dt.float32r
I32 = mybir.dt.int32
U32 = mybir.dt.uint32
ALU = mybir.AluOpType
ACT = mybir.ActivationFunctionType
AX = mybir.AxisListType.X

P = 128
BATCH, LEN, DM = 4, 512, 512
TOK = BATCH * LEN
NT = TOK // P
TPB = LEN // P
DC = DM // P
W, H, DH = 128, 16, 64
NE, FF, TOPK = 8, 800, 2
EPS = 1e-5
NEG = -1e9
BIG = 3e38
SCALE = DH ** -0.5

EXPERT_TILES = (TOPK * TOK + (P - 1) * NE) // P
LEAST_TILES = TOPK * TOK // P
SPARE = EXPERT_TILES - LEAST_TILES
SLOTS = EXPERT_TILES * P
NPAD = NE + SPARE
DUMP = SLOTS

FA, FB = 3 * P, FF - 3 * P
AC = (FF + P - 1) // P
FLAST = FF - (AC - 1) * P
PIECES = [(DC * FA, P), (DC * FA, P), (DC * FB, P), (DC * FB, P), (3 * DM, P), (3 * DM, P), (DM, 3 * FLAST)]
PIECE_AT = [sum(c for c, _ in PIECES[:i]) for i in range(len(PIECES))]
WCOLS = sum(c for c, _ in PIECES)
NPC = len(PIECES)
RAWW = max(c for c, _ in PIECES)
TAPS, PROJ = 3, 3
NO = W * PROJ
HP = H // 2
GH = 8
GP = GH // 2
STEPS = TPB * H // GH
LP = LEN + 2
NP = 2 * HP + 2 * TPB
NKV = HP + 2 * TPB
COLUMNS = PROJ + 2 * HP + 1
WSPLITS = TAPS + PROJ
FILL = [(0, 4), (0, 4), (0, 4), (1, 6), (1, 6), (2, 4), (2, 4), (2, 4)]



def three_passes(nc, out, hi, lo, rhi, rlo, first=True, last=True):
    nc.tensor.matmul(out, hi, rhi, start=first, stop=False)
    nc.tensor.matmul(out, hi, rlo, start=False, stop=False)
    return nc.tensor.matmul(out, lo, rhi, start=False, stop=last)


def Chain(eng, semaphore):
    count = [0]

    def link(ins):
        count[0] += 1
        ins.then_inc(semaphore, 1)
        eng.wait_ge(semaphore, count[0])
    return link


def build(nc, x, conv_w, columns, wq, wk, wv, bv, wo, proj_w, proj_b, gate, experts, out):
    xn_d = nc.dram_tensor("xn_rows", [TOK, DM], F32, kind="Internal").ap()
    xg_d = nc.dram_tensor("dispatched_rows", [SLOTS + NPAD * P, DM], F32, kind="Internal").ap()
    y_d = nc.dram_tensor("expert_rows", [SLOTS, DM], F32, kind="Internal").ap()
    base_d = nc.dram_tensor("first_attention", [LEN, DM], F32, kind="Internal").ap()
    ctx = ExitStack()
    with ctx:
        def keep(name, shape, dt=F32):
            return ctx.enter_context(nc.sbuf_tensor(name, shape, dt))

        t = dict(
            ident=keep("ident", [P, P]),
            slot=keep("slot", [P, TOPK, NT], I32),
            gates=keep("gates", [P, TOPK, NT]),
            tile_waits=keep("tile_waits", [1, EXPERT_TILES], I32),
            tile_slots=keep("tile_slots", [1, EXPERT_TILES], I32),
            released=keep("released", [1, NE], I32),
        )
        banks = [ctx.enter_context(nc.psum_tensor(f"bank{i}", [P, 512], F32)) for i in range(8)]
        weights = (conv_w, columns, wq, wk, wv, bv, wo, proj_w, proj_b)
        front(nc, t, banks, x, gate, weights, xn_d, xg_d, base_d)
        experts_block(nc, t, banks, experts, xg_d, y_d)
        back(nc, t, banks, x, weights, xn_d, y_d, base_d, out)


class Attention:

    def __init__(self, nc, ctx, t, banks, weights, name, alone, conv_banks):
        def sb(what, shape, dt=F32):
            return ctx.enter_context(nc.sbuf_tensor(name + what, shape, dt))

        def sem(what):
            return ctx.enter_context(nc.semaphore(name + what))

        self.nc, self.banks, self.ident, self.weights = nc, banks, t["ident"], weights
        self.conv_banks = [banks[i] for i in conv_banks]
        cw_at = nc.sbuf_base
        self.cwh, self.cwl = sb("cwh", [P, TAPS * DC, NO], F32R), sb("cwl", [P, TAPS * DC, NO], F32R)
        self.pwh, self.pwl = sb("pwh", [P, PROJ, H * DH], F32R), sb("pwl", [P, PROJ, H * DH], F32R)
        self.wo_s, self.pj_s = sb("wo_s", [P, HP, W]), sb("pj_s", [P, DM])
        self.qk = sb("qk", [P, 2, HP, LEN])
        flat = self.qk[:].rearrange("p a b c -> p (a b c)")
        self.cwf = flat[:, 0:TAPS * DC * NO].rearrange("p (a b) -> p a b", b=NO)
        self.pwf = flat[:, TAPS * DC * NO:TAPS * DC * NO + PROJ * H * DH].rearrange("p (a b) -> p a b", b=H * DH)
        xT_at = nc.sbuf_base
        self.xTh, self.xTl = sb("xTh", [P, DC, LP], F32R), sb("xTl", [P, DC, LP], F32R)
        self.qkvh, self.qkvl = sb("qkvh", [P, PROJ, LEN], F32R), sb("qkvl", [P, PROJ, LEN], F32R)
        if alone:
            self.vh = nc.alloc_sbuf_tensor_at(name + "vh", [P, TPB, H * DH], F32, offset=cw_at)
            self.oT = nc.alloc_sbuf_tensor_at(name + "oT", [P, HP, LEN], F32, offset=xT_at)
        else:
            self.vh, self.oT = sb("vh", [P, TPB, H * DH]), sb("oT", [P, HP, LEN])
        self.s = sb("s", [P, 2, GH, P])
        self.pT = sb("pT", [P, GH, P])
        self.nmax, self.rsum, self.rinv = sb("nmax", [P, 2, GH]), sb("rsum", [P, 4, GH]), sb("rinv", [P, 2, GH])
        self.o = sb("o", [P, 2, GH * DH])
        self.att = sb("att", [P, LEN])
        self.mask = sb("mask", [P, P])
        self.columns = sb("columns", [P, COLUMNS])
        self.cb, self.bqs, self.bks, self.bos = (
            self.columns[:, a:z] for a, z in ((0, PROJ), (PROJ, PROJ + HP), (PROJ + HP, PROJ + 2 * HP), (COLUMNS - 1, COLUMNS)))
        self.bvb, self.pjb = sb("bvb", [P, H * DH]), sb("pjb", [P, DM])

        self.piece_loaded = [sem(f"piece_loaded{i}") for i in range(WSPLITS)]
        self.small_loaded = sem("small_loaded")
        self.pieces_hi = sem("pieces_hi")
        self.pieces_lo = sem("pieces_lo")
        self.bias_scaled = sem("bias_scaled")
        self.zeroed = sem("zeroed")
        self.mask_ready = sem("mask_ready")
        self.xs_T = sem("xs_T")
        self.x_hi = sem("x_hi")
        self.x_lo = sem("x_lo")
        self.conv_done = sem("conv_done")
        self.conv_hi = sem("conv_hi")
        self.conv_lo = sem("conv_lo")
        self.proj_done = sem("proj_done")
        self.q_ready = sem("q_ready")
        self.kv_ready = sem("kv_ready")
        self.s_done = sem("s_done")
        self.masked = sem("masked")
        self.maxed = sem("maxed")
        self.p_ready = sem("p_ready")
        self.pT_done = sem("pT_done")
        self.pT_ready = sem("pT_ready")
        self.pv_done = sem("pv_done")
        self.inv_ready = sem("inv_ready")
        self.o_ready = sem("o_ready")
        self.oT_done = sem("oT_done")
        self.oT_ready = sem("oT_ready")
        self.wo_done = sem("wo_done")
        self.att_ready = sem("att_ready")
        self.out_done = sem("out_done")
        self.out_ready = sem("out_ready")


    def load_pieces(self, eng, which):
        conv_w, _, wq, wk, wv = self.weights[:5]
        for n in which:
            if n < TAPS:
                eng.dma_start(self.cwf[:, n * DC:(n + 1) * DC, :], conv_w[n].rearrange("(c p) o -> p c o", p=P))\
                    .then_inc(self.piece_loaded[n], 16)
            else:
                eng.dma_start(self.pwf[:, n - TAPS, :], (wq, wk, wv)[n - TAPS].rearrange("d h e -> d (h e)"))\
                    .then_inc(self.piece_loaded[n], 16)

    SMALL = 5

    def load_small(self, eng):
        _, columns, _, _, _, bv, wo, proj_w, proj_b = self.weights
        for dst, src in (
            (self.columns[:], columns),
            (self.bvb[:], bv.rearrange("h e -> (h e)").rearrange("(n w) -> n w", n=1).to_broadcast([P, H * DH])),
            (self.pjb[:], proj_b.rearrange("(n w) -> n w", n=1).to_broadcast([P, DM])),
            (self.wo_s[:], wo.rearrange("h e w -> (h e) w").rearrange("(c p) w -> p c w", p=P)),
            (self.pj_s[:], proj_w),
        ):
            eng.dma_start(dst, src).then_inc(self.small_loaded, 16)

    def piece(self, n):
        if n < TAPS:
            c = slice(n * DC, (n + 1) * DC)
            return self.cwh[:, c, :], self.cwl[:, c, :], self.cwf[:, c, :]
        return self.pwh[:, n - TAPS, :], self.pwl[:, n - TAPS, :], self.pwf[:, n - TAPS, :]

    def hi_piece(self, act, n):
        hi, _, src = self.piece(n)
        act.wait_ge(self.piece_loaded[n], 16)
        self.nc.scalar.activation(hi, src, ACT.Copy).then_inc(self.pieces_hi, 1)

    def lo_piece(self, eng, n):
        hi, lo, src = self.piece(n)
        eng.wait_ge(self.pieces_hi, n + 1)
        eng.tensor_tensor(lo, src, hi.bitcast(F32), ALU.subtract).then_inc(self.pieces_lo, 1)

    def constants(self, pool):
        g = self.nc.gpsimd
        g.memset(self.mask[:], BIG).then_inc(self.mask_ready, 1)
        pool.wait_ge(self.mask_ready, 1)
        g.affine_select(out=self.mask[:], in_=self.mask[:], compare_op=ALU.is_ge, fill=NEG, base=0,
                        pattern=[[-1, P]], channel_multiplier=1).then_inc(self.mask_ready, 1)
        for z in (self.xTh, self.xTl):
            for col in (0, LP - 1):
                g.memset(z[:, :, col:col + 1].bitcast(F32), 0.0).then_inc(self.zeroed, 1)


    def pe_transpose_x(self, pe, i, n, rows, ring):
        if n >= 2:
            pe.wait_ge(self.x_hi, i - 1)
            pe.wait_ge(self.x_lo, i - 1)
        bank = self.banks[ring[n % 2]]
        for c in range(DC):
            last = self.nc.tensor.transpose(bank[:, c * P:(c + 1) * P], rows[:, c * P:(c + 1) * P], self.ident[:])
        last.then_inc(self.xs_T, 1)

    def act_hi_x(self, act, i, n, ring):
        act.wait_ge(self.xs_T, i + 1)
        self.nc.scalar.activation(self.xTh[:, :, 1 + n * P:1 + (n + 1) * P],
                                  self.banks[ring[n % 2]][:].rearrange("p (c t) -> p c t", c=DC), ACT.Copy)\
            .then_inc(self.x_hi, 1)

    def dve_lo_x(self, dve, i, n, ring):
        dve.wait_ge(self.x_hi, i + 1)
        dst = slice(1 + n * P, 1 + (n + 1) * P)
        self.nc.vector.tensor_tensor(self.xTl[:, :, dst], self.banks[ring[n % 2]][:].rearrange("p (c t) -> p c t", c=DC),
                                     self.xTh[:, :, dst].bitcast(F32), ALU.subtract).then_inc(self.x_lo, 1)


    def pe_conv(self, b, n, js):
        for j in js:
            tap, c = j // DC, j % DC
            last = three_passes(self.nc, self.conv_banks[n][:], self.cwh[:, j, n * W:(n + 1) * W],
                                self.cwl[:, j, n * W:(n + 1) * W], self.xTh[:, c, tap:tap + LEN],
                                self.xTl[:, c, tap:tap + LEN], j == 0, j == TAPS * DC - 1)
        if js[-1] == TAPS * DC - 1:
            last.then_inc(self.conv_done, 1)

    def act_conv(self, act, b, n):
        act.wait_ge(self.conv_done, b * PROJ + (n + 1))
        self.nc.scalar.activation(self.qkvh[:, n, :], self.conv_banks[n][:], ACT.Identity, bias=self.cb[:, n:n + 1])\
            .then_inc(self.conv_hi, 1)

    def dve_conv(self, dve, b, n):
        dve.wait_ge(self.conv_hi, b * PROJ + (n + 1))
        self.nc.vector.scalar_tensor_tensor(self.qkvl[:, n, :], self.conv_banks[n][:], self.cb[:, n:n + 1],
                                            self.qkvh[:, n, :].bitcast(F32), ALU.add, ALU.subtract)\
            .then_inc(self.conv_lo, 1)


    def pe_proj(self, pe, b, between):
        pe.wait_ge(self.conv_hi, (b + 1) * PROJ)
        pe.wait_ge(self.conv_lo, (b + 1) * PROJ)
        for r in range(NP):
            if r >= 4:
                r4 = r - 4
                if r4 < 2 * HP and r4 % 2 == 0:
                    pe.wait_ge(self.q_ready, b * HP + (r4 // 2 + 1))
                elif r4 < 2 * HP:
                    pe.wait_ge(self.kv_ready, b * NKV + (r4 // 2 + 1))
                else:
                    pe.wait_ge(self.kv_ready, b * NKV + (r4 - HP + 1))
            bank = self.banks[r % 4][:]
            if r < 2 * HP:
                c, w = r // 2, r % 2
                last = three_passes(self.nc, bank, self.pwh[:, w, c * P:(c + 1) * P], self.pwl[:, w, c * P:(c + 1) * P],
                                    self.qkvh[:, w, :], self.qkvl[:, w, :])
            else:
                blk, half = (r - 2 * HP) // 2, r % 2
                last = three_passes(self.nc, bank, self.qkvh[:, 2, blk * P:(blk + 1) * P],
                                    self.qkvl[:, 2, blk * P:(blk + 1) * P],
                                    self.pwh[:, 2, half * 512:(half + 1) * 512], self.pwl[:, 2, half * 512:(half + 1) * 512])
            last.then_inc(self.proj_done, 1)
            if between and r < 2 * HP and r % 4 == 3:
                between(r // 4)
        pe.wait_ge(self.q_ready, (b + 1) * HP)
        pe.wait_ge(self.kv_ready, (b + 1) * NKV)

    def act_proj(self, act, b, between):
        for c in range(HP):
            act.wait_ge(self.proj_done, b * NP + (2 * c + 1))
            self.nc.scalar.activation(self.qk[:, 0, c, :], self.banks[2 * c % 4][:], ACT.Identity,
                                      bias=self.bqs[:, c:c + 1], scale=SCALE).then_inc(self.q_ready, 1)
            if between and c % 2 == 1:
                between(c // 2)

    def dve_proj(self, dve, b, between):
        v = self.nc.vector
        for c in range(HP):
            dve.wait_ge(self.proj_done, b * NP + (2 * c + 2))
            v.tensor_scalar(self.qk[:, 1, c, :], self.banks[(2 * c + 1) % 4][:], self.bks[:, c:c + 1], None, ALU.add)\
                .then_inc(self.kv_ready, 1)
            if between and c % 2 == 1:
                between(c // 2)
        for r in range(2 * TPB):
            dve.wait_ge(self.proj_done, b * NP + (2 * HP + r + 1))
            half = slice((r % 2) * 512, (r % 2) * 512 + 512)
            v.tensor_tensor(self.vh[:, r // 2, half], self.banks[r % 4][:], self.bvb[:, half], ALU.add)\
                .then_inc(self.kv_ready, 1)


    def pe_steps(self, pe, b, fill):
        nc, banks = self.nc, self.banks

        def scores(g):
            blk, hh = g // 2, g % 2
            if g >= 2:
                pe.wait_ge(self.masked, b * STEPS + (g - 1))
            for pr in range(GP):
                for half in range(2):
                    rows, tok = slice(64 * half, 64 * half + 64), slice(blk * P, (blk + 1) * P)
                    last = nc.tensor.matmul(banks[2 * (g % 2) + half][:, pr * P:(pr + 1) * P],
                                            self.qk[rows, 0, hh * GP + pr, tok], self.qk[rows, 1, hh * GP + pr, tok],
                                            start=True, stop=True)
            last.then_inc(self.s_done, 1)

        def transpose_o(g):
            pe.wait_ge(self.o_ready, b * STEPS + (g + 1))
            for c in range(GP):
                last = nc.tensor.transpose(banks[4][:, c * P:(c + 1) * P], self.o[:, g % 2, c * P:(c + 1) * P], self.ident[:])
            last.then_inc(self.oT_done, 1)

        scores(0)
        scores(1)
        for g in range(STEPS):
            pe.wait_ge(self.p_ready, b * STEPS + (g + 1))
            if g >= 2:
                pe.wait_ge(self.oT_ready, b * STEPS + (g - 1))
            for j in range(GH):
                last = nc.tensor.transpose(banks[4 + j // GP][:, (j % GP) * P:(j % GP + 1) * P],
                                           self.s[:, g % 2, j, :], self.ident[:])
            last.then_inc(self.pT_done, 1)
            if g + 2 < STEPS:
                scores(g + 2)
            if fill:
                fill(g, 0)
            pe.wait_ge(self.pT_ready, b * STEPS + (g + 1))
            if g:
                pe.wait_ge(self.o_ready, b * STEPS + g)
            blk, hh = g // 2, g % 2
            for h in range(GH):
                j = (h % 2) * GP + h // 2
                at = (hh * GH + h) * DH
                last = nc.tensor.matmul(banks[6][:, h * DH:(h + 1) * DH], self.pT[:, j, :], self.vh[:, blk, at:at + DH],
                                        start=True, stop=True)
            last.then_inc(self.pv_done, 1)
            if g:
                transpose_o(g - 1)
            if fill:
                fill(g, 1)
        pe.wait_ge(self.oT_ready, b * STEPS + (STEPS - 1))
        transpose_o(STEPS - 1)

    def act_steps(self, act, b, fill):
        sc = self.nc.scalar

        def exps(g):
            act.wait_ge(self.maxed, b * STEPS + (g + 1))
            for j in range(GH):
                last = sc.activation(self.s[:, g % 2, j, :], self.s[:, g % 2, j, :], ACT.Exp,
                                     bias=self.nmax[:, g % 2, j:j + 1], accum_out=self.rsum[:, g % 4, j:j + 1])
            last.then_inc(self.p_ready, 1)

        def oT_copy(g):
            act.wait_ge(self.oT_done, b * STEPS + (g + 1))
            blk, hh = g // 2, g % 2
            sc.activation(self.oT[:, hh * GP:(hh + 1) * GP, blk * P:(blk + 1) * P],
                          self.banks[4][:].rearrange("p (c t) -> p c t", c=GP), ACT.Copy).then_inc(self.oT_ready, 1)

        exps(0)
        for g in range(STEPS):
            if g + 1 < STEPS:
                exps(g + 1)
            if g:
                oT_copy(g - 1)
            if fill:
                fill(g)
        oT_copy(STEPS - 1)

    def dve_steps(self, dve, b, fill):
        v, banks = self.nc.vector, self.banks

        def mask_max(g):
            dve.wait_ge(self.s_done, b * STEPS + (g + 1))
            for half in range(2):
                last = v.tensor_tensor(self.s[:, g % 2, half * GP:(half + 1) * GP, :],
                                       banks[2 * (g % 2) + half][:].rearrange("p (j k) -> p j k", j=GP),
                                       self.mask[:].unsqueeze(1).to_broadcast([P, GP, P]), ALU.min)
            last.then_inc(self.masked, 1)
            dve.wait_ge(self.masked, b * STEPS + (g + 1))
            v.tensor_reduce(self.nmax[:, g % 2, :], self.s[:, g % 2, :, :], AX, ALU.max, negate=True)\
                .then_inc(self.maxed, 1)

        mask_max(0)
        mask_max(1)
        for g in range(STEPS):
            dve.wait_ge(self.pT_done, b * STEPS + (g + 1))
            for half in range(2):
                last = v.tensor_copy(self.pT[:, half * GP:(half + 1) * GP, :],
                                     banks[4 + half][:].rearrange("p (j k) -> p j k", j=GP))
            last.then_inc(self.pT_ready, 1)
            v.reciprocal(self.rinv[:, g % 2, :], self.rsum[:, g % 4, :]).then_inc(self.inv_ready, 1)
            if g + 2 < STEPS:
                mask_max(g + 2)
            dve.wait_ge(self.pv_done, b * STEPS + (g + 1))
            dve.wait_ge(self.inv_ready, b * STEPS + (g + 1))
            v.tensor_tensor(self.o[:, g % 2, :].rearrange("p (c a e) -> p c a e", a=2, e=DH),
                            banks[6][:].rearrange("p (c a e) -> p c a e", a=2, e=DH),
                            self.rinv[:, g % 2, :].rearrange("p (a c) -> p c a", a=2).unsqueeze(3)
                            .to_broadcast([P, GP, 2, DH]), ALU.mult).then_inc(self.o_ready, 1)
            if fill:
                fill(g)


    def pe_out(self, pe, b):
        pe.wait_ge(self.oT_ready, (b + 1) * STEPS)
        for c in range(HP):
            last = self.nc.tensor.matmul(self.banks[7][:], self.wo_s[:, c, :], self.oT[:, c, :], start=c == 0, stop=c == HP - 1)
        last.then_inc(self.wo_done, 1)
        pe.wait_ge(self.att_ready, b + 1)
        for n in range(TPB):
            self.nc.tensor.matmul(self.banks[n][:], self.att[:, n * P:(n + 1) * P], self.pj_s[:], start=True, stop=True)\
                .then_inc(self.out_done, 1)

    def act_out(self, act, b):
        act.wait_ge(self.wo_done, b + 1)
        self.nc.scalar.activation(self.att[:], self.banks[7][:], ACT.Identity, bias=self.bos).then_inc(self.att_ready, 1)



def front(nc, t, banks, x, gate, weights, xn_d, xg_d, base_d):
    ctx = ExitStack()
    with ctx:
        def sb(name, shape, dt=F32):
            return ctx.enter_context(nc.sbuf_tensor(name, shape, dt))

        def sem(name):
            return ctx.enter_context(nc.semaphore(name))

        ident, slot, gates = t["ident"], t["slot"], t["gates"]
        tile_waits, tile_slots, released = t["tile_waits"], t["tile_slots"], t["released"]
        A = Attention(nc, ctx, t, banks, weights, "f_", alone=True, conv_banks=(7, 0, 1))
        RING = (6, 7)
        xb = sb("xb", [P, NT, DM])
        zrow = sb("zrow", [P, DM])
        rTh, rTl = sb("rTh", [P, 2, DC, P], F32R), sb("rTl", [P, 2, DC, P], F32R)
        gTf = sb("gTf", [P, DC, NE])
        gT2 = sb("gT2", [P, DC, 2, NE], F32R)
        stats, mv = sb("stats", [P, NT, 6]), sb("mv", [P, NT, 2])
        var, std, rstd, tmp = (sb(n, [P, NT]) for n in ("var", "std", "rstd", "tmp"))
        less, ones = sb("less", [P, P]), sb("ones", [P, P])
        lane, eno = sb("lane", [P, 1]), sb("eno", [P, NE])
        dumps, tails = sb("dumps", [P, NPAD]), sb("tails", [P, SPARE])
        tileno = sb("tileno", [1, EXPERT_TILES])
        prob, work, first, second, before = (sb(n, [P, NT, NE]) for n in ("prob", "work", "first", "second", "before"))
        col = sb("col", [P, 4, NT])
        picked = sb("picked", [P, NE])
        need, needi = sb("need", [P, 6, NE]), sb("needi", [P, NE], I32)
        padf, pads = sb("padf", [P, 3, NPAD]), sb("pads", [P, NPAD], I32)
        cmp = sb("cmp", [1, EXPERT_TILES, NE - 1])
        texp, texi = sb("texp", [1, EXPERT_TILES]), sb("texi", [1, EXPERT_TILES], I32)
        base = sb("base", [P, 2, DM])

        logits, rank, total = banks[5], banks[2], banks[3]

        x_loaded = [sem(f"x_loaded{b}") for b in range(BATCH)]
        gate_loaded, consts, dve_chain, gate_split = sem("gate_loaded"), sem("consts"), sem("dve_chain"), sem("gate_split")
        var_ready, std_ready, xn_ready, xn_stored = sem("var_ready"), sem("std_ready"), sem("xn_ready"), sem("xn_stored")
        front_xT, front_hi, front_lo = sem("front_xT"), sem("front_hi"), sem("front_lo")
        logits_done, shifted, exp_done = sem("logits_done"), sem("shifted"), sem("exp_done")
        picked_ready, rank_done, routed = sem("picked_ready"), sem("rank_done"), sem("routed")
        sent, padded = sem("sent"), sem("padded")
        base_stored = [sem("base_stored0"), sem("base_stored1")]

        block = ctx.enter_context(nc.Block())

        @block.sync
        def _(sp):
            def load(b):
                sp.dma_start(xb[:, TPB * b:TPB * (b + 1), :],
                             x[b * LEN:(b + 1) * LEN, :].rearrange("(j p) d -> p j d", p=P)).then_inc(x_loaded[b], 16)

            load(0)
            sp.dma_start(gTf[:], gate).then_inc(gate_loaded, 16)
            load(1)
            A.load_pieces(sp, range(TAPS))
            load(2)
            load(3)
            A.load_pieces(sp, range(TAPS, WSPLITS))
            A.load_small(sp)
            for b in range(1, BATCH):
                sp.wait_ge(xn_ready, TPB * (b + 1))
                sp.dma_start(xn_d[b * LEN:(b + 1) * LEN, :].rearrange("(j p) d -> p j d", p=P),
                             xb[:, TPB * b:TPB * (b + 1), :]).then_inc(xn_stored, 16)
            for n in range(TPB):
                sp.wait_ge(A.out_ready, n + 1)
                sp.dma_start(base_d[n * P:(n + 1) * P, :], base[:, n % 2, :]).then_inc(base_stored[n % 2], 16)
            for stored in base_stored:
                sp.wait_ge(stored, TPB // 2 * 16)
            sp.wait_ge(xn_stored, 16 * (BATCH - 1))

        @block.gpsimd
        def _(pool):
            g = nc.gpsimd
            g.memset(ident[:], 0.0).then_inc(consts, 1)
            g.memset(less[:], 0.0).then_inc(consts, 1)
            g.memset(ones[:], 1.0).then_inc(consts, 1)
            g.memset(zrow[:], 0.0).then_inc(consts, 1)
            pool.wait_ge(consts, 2)
            g.affine_select(out=ident[:], in_=ident[:], compare_op=ALU.not_equal, fill=1.0, base=0,
                            pattern=[[-1, P]], channel_multiplier=1).then_inc(consts, 1)
            g.affine_select(out=less[:], in_=less[:], compare_op=ALU.is_ge, fill=1.0, base=0,
                            pattern=[[-1, P]], channel_multiplier=1).then_inc(consts, 1)
            ok = dict(allow_small_or_imprecise_dtypes=True)
            g.iota(lane[:], [[1, 1]], base=0, channel_multiplier=1, **ok).then_inc(consts, 1)
            g.iota(eno[:], [[1, NE]], base=-NE, channel_multiplier=0, **ok).then_inc(consts, 1)
            g.iota(dumps[:], [[P, NPAD]], base=DUMP, channel_multiplier=1, **ok).then_inc(consts, 1)
            g.iota(tails[:], [[P, SPARE]], base=0, channel_multiplier=1, **ok).then_inc(consts, 1)
            g.iota(tileno[:], [[1, EXPERT_TILES]], base=0, channel_multiplier=0, **ok).then_inc(consts, 1)
            A.constants(pool)
            for n in range(WSPLITS):
                A.lo_piece(g, n)
            pool.wait_ge(routed, 1)
            for j in range(NPAD):
                g.indirect_dma_start(xg_d[:, :], bass.IndirectOffsetOnAxis(ap=pads[:, j:j + 1].bitcast(U32), axis=0),
                                     zrow[:], None).then_inc(padded, 16)
            for i in range(NT):
                for k in range(TOPK):
                    g.indirect_dma_start(xg_d[:, :],
                                         bass.IndirectOffsetOnAxis(ap=slot[:, k, i:i + 1].bitcast(U32), axis=0),
                                         xb[:, i, :], None).then_inc(sent, 16)
            pool.wait_ge(padded, 16 * NPAD)
            pool.wait_ge(sent, 16 * TOPK * NT)

        @block.tensor
        def _(pe):
            mm = nc.tensor.matmul
            pe.wait_ge(consts, 6)
            pe.wait_ge(gate_split, 2)

            def transpose_rows(i):
                pe.wait_ge(xn_ready, i + 1)
                if i < TPB:
                    A.pe_transpose_x(pe, i, i, xb[:, i, :], RING)
                    return
                if i < TPB + 2:
                    pe.wait_ge(A.x_hi, i - 1)
                    pe.wait_ge(A.x_lo, i - 1)
                else:
                    pe.wait_ge(front_hi, i - 1 - TPB)
                    pe.wait_ge(front_lo, i - 1 - TPB)
                bank = banks[RING[i % 2]]
                for c in range(DC):
                    last = nc.tensor.transpose(bank[:, c * P:(c + 1) * P], xb[:, i, c * P:(c + 1) * P], ident[:])
                last.then_inc(front_xT, 1)

            def router(i):
                if i < TPB:
                    pe.wait_ge(A.x_hi, i + 1)
                    pe.wait_ge(A.x_lo, i + 1)
                    h, l = (z[:, :, 1 + i * P:1 + (i + 1) * P] for z in (A.xTh, A.xTl))
                else:
                    pe.wait_ge(front_hi, i + 1 - TPB)
                    pe.wait_ge(front_lo, i + 1 - TPB)
                    h, l = rTh[:, i % 2, :, :], rTl[:, i % 2, :, :]
                o = logits[:, i * 2 * NE:(i + 1) * 2 * NE]
                for c in range(DC):
                    mm(o, h[:, c, :], gT2[:, c, :, :].rearrange("p a e -> p (a e)"), start=c == 0, stop=False)
                    last = mm(o[:, 0:NE], l[:, c, :], gT2[:, c, 0, :], start=False, stop=c == DC - 1)
                last.then_inc(logits_done, 1)

            for i in range(NT):
                transpose_rows(i)
                if i:
                    router(i - 1)
            router(NT - 1)
            pe.wait_ge(A.zeroed, 4)
            for n in range(TAPS):
                pe.wait_ge(A.pieces_lo, n + 1)
                A.pe_conv(0, 0, range(n * DC, (n + 1) * DC))
            pe.wait_ge(picked_ready, 1)
            mm(rank[:, 0:NT * NE], less[:], work[:], start=True, stop=False)
            mm(rank[:, 0:NT * NE], ones[:], before[:], start=False, stop=True)
            mm(total[:, 0:NE], ones[:], picked[:], start=True, stop=True).then_inc(rank_done, 1)
            for n in range(1, PROJ):
                A.pe_conv(0, n, range(TAPS * DC))
            pe.wait_ge(A.pieces_lo, WSPLITS)
            pe.wait_ge(A.small_loaded, 16 * A.SMALL)
            A.pe_proj(pe, 0, None)
            A.pe_steps(pe, 0, None)
            A.pe_out(pe, 0)

        @block.scalar
        def _(a):
            s = nc.scalar

            def deviations(b):
                a.wait_ge(var_ready, b + 1)
                n = slice(b * TPB, (b + 1) * TPB)
                s.activation(std[:, n], var[:, n], ACT.Sqrt).then_inc(std_ready, 1)

            def hi(i):
                if i < TPB:
                    A.act_hi_x(a, i, i, RING)
                    return
                j = i - TPB
                a.wait_ge(front_xT, j + 1)
                if j >= 2:
                    a.wait_ge(logits_done, i - 1)
                s.activation(rTh[:, i % 2, :, :], banks[RING[i % 2]][:].rearrange("p (c t) -> p c t", c=DC), ACT.Copy)\
                    .then_inc(front_hi, 1)

            deviations(0)
            for b in range(BATCH):
                if b + 1 < BATCH:
                    deviations(b + 1)
                for n in range(TPB):
                    hi(b * TPB + n)
                    if b and (b - 1) * TPB + n < WSPLITS:
                        A.hi_piece(a, (b - 1) * TPB + n)
            a.wait_ge(shifted, 1)
            s.activation(prob[:], work[:], ACT.Exp).then_inc(exp_done, 1)
            a.wait_ge(A.small_loaded, 16 * A.SMALL)
            for n in range(PROJ):
                A.act_conv(a, 0, n)
            a.wait_ge(A.bias_scaled, 1)
            A.act_proj(a, 0, None)
            A.act_steps(a, 0, None)
            A.act_out(a, 0)

        @block.vector
        def _(d):
            v = nc.vector
            link = Chain(d, dve_chain)

            def over_experts(ap):
                return ap.unsqueeze(2).to_broadcast([P, NT, NE])

            def over_tiles(ap):
                return ap.unsqueeze(1).to_broadcast([P, NT, NE])

            def norm(b):
                d.wait_ge(x_loaded[b], 16)
                tiles = range(TPB * b, TPB * (b + 1))
                for i in tiles:
                    last = v.bn_stats(stats[:, i, :], xb[:, i, :])
                link(last)
                for i in tiles:
                    last = v.bn_aggr(mv[:, i, :], stats[:, i, :])
                link(last)
                n = slice(b * TPB, (b + 1) * TPB)
                link(v.tensor_scalar(var[:, n], mv[:, n, 1], EPS, None, ALU.add))
                v.tensor_scalar(tmp[:, n], var[:, n], 0.5, None, ALU.mult).then_inc(var_ready, 1)
                d.wait_ge(std_ready, b + 1)
                link(v.reciprocal(rstd[:, n], std[:, n]))
                link(v.tensor_tensor(tmp[:, n], tmp[:, n], rstd[:, n], ALU.mult))
                link(v.tensor_tensor(tmp[:, n], tmp[:, n], rstd[:, n], ALU.mult))
                link(v.tensor_scalar(tmp[:, n], tmp[:, n], -1.0, 1.5, ALU.mult, ALU.add))
                link(v.tensor_tensor(rstd[:, n], rstd[:, n], tmp[:, n], ALU.mult))
                for i in tiles:
                    v.tensor_scalar(xb[:, i, :], xb[:, i, :], mv[:, i, 0:1], rstd[:, i:i + 1], ALU.subtract, ALU.mult)\
                        .then_inc(xn_ready, 1)

            def lo(i):
                if i < TPB:
                    A.dve_lo_x(d, i, i, RING)
                    return
                d.wait_ge(front_hi, i + 1 - TPB)
                v.tensor_tensor(rTl[:, i % 2, :, :], banks[RING[i % 2]][:].rearrange("p (c t) -> p c t", c=DC),
                                rTh[:, i % 2, :, :].bitcast(F32), ALU.subtract).then_inc(front_lo, 1)

            norm(0)
            d.wait_ge(gate_loaded, 16)
            v.tensor_copy(gT2[:, :, 0, :], gTf[:]).then_inc(gate_split, 1)
            d.wait_ge(gate_split, 1)
            v.tensor_tensor(gT2[:, :, 1, :], gTf[:], gT2[:, :, 0, :].bitcast(F32), ALU.subtract).then_inc(gate_split, 1)
            for b in range(BATCH):
                if b + 1 < BATCH:
                    norm(b + 1)
                for n in range(TPB):
                    lo(b * TPB + n)
            d.wait_ge(logits_done, NT)
            lg = logits[:, 0:NT * 2 * NE].rearrange("p (i a e) -> p i a e", a=2, e=NE)
            link(v.tensor_copy(prob[:], lg[:, :, 0, :]))
            link(v.tensor_tensor(prob[:], lg[:, :, 1, :], prob[:], ALU.add))
            link(v.tensor_reduce(col[:, 0, :], prob[:], AX, ALU.max, negate=True))
            v.tensor_tensor(work[:], prob[:], over_experts(col[:, 0, :]), ALU.add).then_inc(shifted, 1)
            d.wait_ge(exp_done, 1)
            link(v.tensor_reduce(col[:, 1, :], prob[:], AX, ALU.add))
            link(v.reciprocal(col[:, 2, :], col[:, 1, :]))
            link(v.tensor_tensor(prob[:], prob[:], over_experts(col[:, 2, :]), ALU.mult))

            def pick(chosen, top):
                link(v.tensor_reduce(top, prob[:], AX, ALU.max))
                link(v.tensor_tensor(work[:], prob[:], over_experts(top), ALU.is_equal))
                link(v.tensor_tensor(work[:], work[:], over_tiles(eno[:]), ALU.mult))
                link(v.tensor_reduce(col[:, 2, :], work[:], AX, ALU.min))
                link(v.tensor_tensor(chosen[:], over_tiles(eno[:]), over_experts(col[:, 2, :]), ALU.is_equal))

            d.wait_ge(consts, 11)
            pick(first, col[:, 0, :])
            link(v.scalar_tensor_tensor(prob[:], first[:], -2.0, prob[:], ALU.mult, ALU.add))
            pick(second, col[:, 1, :])
            link(v.tensor_tensor(col[:, 2, :], col[:, 0, :], col[:, 1, :], ALU.add))
            link(v.reciprocal(col[:, 3, :], col[:, 2, :]))
            v.tensor_tensor(gates[:, 0, :], col[:, 0, :], col[:, 3, :], ALU.mult)
            v.tensor_tensor(gates[:, 1, :], col[:, 1, :], col[:, 3, :], ALU.mult)
            v.memset(before[:, 0, :], 0.0)
            link(v.tensor_tensor(work[:], first[:], second[:], ALU.add))
            for i in range(1, NT):
                link(v.tensor_tensor(before[:, i, :], before[:, i - 1, :], work[:, i - 1, :], ALU.add))
            v.tensor_tensor(picked[:], before[:, NT - 1, :], work[:, NT - 1, :], ALU.add).then_inc(picked_ready, 1)
            d.wait_ge(rank_done, 1)
            rows, tiles, ends, starts, cond, spare = (need[:, i, :] for i in range(6))
            link(v.tensor_copy(rows, total[:, 0:NE]))
            link(v.tensor_scalar(needi[:], rows, float(P - 1), None, ALU.add))
            link(v.tensor_single_scalar(needi[:], needi[:], P.bit_length() - 1, op=ALU.arith_shift_right))
            link(v.tensor_scalar(tiles, needi[:], 1.0, None, ALU.max))
            link(v.tensor_copy(ends[:, 0:1], tiles[:, 0:1]))
            for e in range(1, NE):
                link(v.tensor_tensor(ends[:, e:e + 1], ends[:, e - 1:e], tiles[:, e:e + 1], ALU.add))
            link(v.tensor_tensor(starts, ends, tiles, ALU.subtract))
            link(v.tensor_scalar(starts, starts, float(P), None, ALU.mult))
            link(v.tensor_tensor(work[:], rank[:, 0:NT * NE].rearrange("p (i e) -> p i e", e=NE), over_tiles(starts), ALU.add))
            link(v.tensor_tensor(first[:], first[:], work[:], ALU.mult))
            link(v.tensor_tensor(second[:], second[:], work[:], ALU.mult))
            v.tensor_reduce(col[:, 0, :], first[:], AX, ALU.add)
            link(v.tensor_reduce(col[:, 1, :], second[:], AX, ALU.add))
            v.tensor_copy(slot[:, 0, :], col[:, 0, :])
            v.tensor_copy(slot[:, 1, :], col[:, 1, :])
            want, take, use = (padf[:, i, :] for i in range(3))
            v.tensor_tensor(want[:, 0:NE], starts, rows, ALU.add)
            link(v.scalar_tensor_tensor(spare, tiles, float(P), rows, ALU.mult, ALU.subtract))
            link(v.tensor_scalar(want[:, 0:NE], want[:, 0:NE], lane[:, 0:1], None, ALU.add))
            v.tensor_scalar(take[:, 0:NE], spare, lane[:, 0:1], None, ALU.is_gt)
            link(v.tensor_scalar(cond[:, 0:1], ends[:, NE - 1:NE], float(P), None, ALU.mult))
            link(v.tensor_scalar(want[:, NE:], tails[:], cond[:, 0:1], None, ALU.add))
            link(v.tensor_scalar(take[:, NE:], want[:, NE:], float(SLOTS), None, ALU.is_lt))
            link(v.tensor_tensor(use, want, dumps[:], ALU.subtract))
            link(v.tensor_tensor(use, use, take, ALU.mult))
            link(v.tensor_tensor(use, use, dumps[:], ALU.add))
            v.tensor_copy(pads[:], use)
            link(v.tensor_tensor(cmp[:], ends[0:1, 0:NE - 1].unsqueeze(1).to_broadcast([1, EXPERT_TILES, NE - 1]),
                                 tileno[:].unsqueeze(2).to_broadcast([1, EXPERT_TILES, NE - 1]), ALU.is_le))
            link(v.tensor_reduce(texp[:], cmp[:], AX, ALU.add))
            v.tensor_scalar(tile_waits[:], texp[:], float(NPC), None, ALU.mult)
            link(v.tensor_copy(texi[:], texp[:]))
            link(v.tensor_single_scalar(texi[:], texi[:], 1, op=ALU.bitwise_and))
            v.tensor_scalar(tile_slots[:], texi[:], float(WCOLS), None, ALU.mult)
            link(v.memset(released[:], 0))
            v.tensor_copy(released[0:1, 2:NE], ends[0:1, 0:NE - 2]).then_inc(routed, 1)

            d.wait_ge(A.small_loaded, 16 * A.SMALL)
            v.tensor_scalar(A.bqs, A.bqs, SCALE, None, ALU.mult).then_inc(A.bias_scaled, 1)
            d.wait_ge(A.mask_ready, 2)
            for n in range(PROJ):
                A.dve_conv(d, 0, n)
            A.dve_proj(d, 0, None)
            A.dve_steps(d, 0, None)
            for n in range(TPB):
                d.wait_ge(A.out_done, n + 1)
                if n >= 2:
                    d.wait_ge(base_stored[n % 2], n // 2 * 16)
                v.tensor_tensor(base[:, n % 2, :], banks[n][:], A.pjb[:], ALU.add).then_inc(A.out_ready, 1)


def experts_block(nc, t, banks, experts, xg_d, y_d):
    ctx = ExitStack()
    with ctx:
        def sb(name, shape, dt=F32):
            return ctx.enter_context(nc.sbuf_tensor(name, shape, dt))

        def sem(name):
            return ctx.enter_context(nc.semaphore(name))

        ident, tile_waits, tile_slots, released = t["ident"], t["tile_waits"], t["tile_slots"], t["released"]
        raw = sb("raw", [P, 2, RAWW])
        xrow = sb("xrow", [P, DM])
        xTh, xTl = sb("xTh", [P, DC, P], F32R), sb("xTl", [P, DC, P], F32R)
        silu, act = sb("silu", [P, FF]), sb("act", [P, AC * P])
        aTh, aTl = sb("aTh", [P, AC, P], F32R), sb("aTl", [P, AC - 1, P], F32R)
        ysb = sb("ysb", [P, DM])
        whi, wlo = sb("whi", [P, 2 * WCOLS], F32R), sb("wlo", [P, 2 * WCOLS], F32R)

        hA1, hA3, hB1, hB3, tA, tB, tX, yP = banks

        pool_turns, sp_turns = sem("pool_turns"), sem("sp_turns")
        raw_loaded = [sem("raw_loaded0"), sem("raw_loaded1")]
        hi_split, lo_split = sem("hi_split"), sem("lo_split")
        row_loaded = sem("row_loaded")
        xT_done, xT_hi, xT_lo = sem("xT_done"), sem("xT_hi"), sem("xT_lo")
        hA_done, hB_done = sem("hA_done"), sem("hB_done")
        siluA, siluB, actA, actB = sem("siluA"), sem("siluB"), sem("actA"), sem("actB")
        aT_done, aT_hi, aT_lo = sem("aT_done"), sem("aT_hi"), sem("aT_lo")
        y_done, y_copied, y_stored = sem("y_done"), sem("y_copied"), sem("y_stored")

        block = ctx.enter_context(nc.Block())

        def hi_part(eng, i, half, slot_at):
            n, parts = PIECES[i]
            dst = whi[0:parts, bass.ds(slot_at + PIECE_AT[i], n)]
            src = raw[0:parts, half, 0:n]
            return eng.activation(dst, src, ACT.Copy) if eng is nc.scalar else eng.tensor_copy(dst, src)

        def lo_part(eng, i, half, slot_at):
            n, parts = PIECES[i]
            rows = slice(0, parts) if i < NPC - 1 else slice(FLAST, 2 * FLAST)
            at = bass.ds(slot_at + PIECE_AT[i], n)
            return eng.tensor_tensor((wlo if i < NPC - 1 else whi)[rows, at], raw[rows, half, 0:n],
                                     whi[rows, at].bitcast(F32), ALU.subtract)

        @block.sync
        def _(sp):
            def load(e, i, half, n):
                w, parts = PIECES[i]
                if n is not None:
                    sp.wait_ge(lo_split, n)
                    if not isinstance(n, int):
                        sp.sem_inc(sp_turns, 1)
                src = experts[bass.ds(e, 1), 0:parts, PIECE_AT[i]:PIECE_AT[i] + w].rearrange("a p w -> (a p) w")
                sp.dma_start(raw[0:parts, half, 0:w], src).then_inc(raw_loaded[half], 16)

            for i in range(2 * NPC):
                load(i // NPC, i % NPC, i % 2, i - 1 if i >= 2 else None)
            with sp.Fori(1, NE // 2) as k:
                for i in range(2 * NPC):
                    load(k * 2 + i // NPC, i % NPC, i % 2, k * (2 * NPC) + (i - 1))

        @block.gpsimd
        def _(pool):
            g = nc.gpsimd

            def after(semaphore, count):
                pool.wait_ge(semaphore, count)
                pool.sem_inc(pool_turns, 1)

            def split(i, half, slot_at, loads, n):
                if i == 0:
                    after(lo_split, n)
                after(raw_loaded[half], loads)
                hi_part(g, i, half, slot_at).then_inc(hi_split, 1)
                pool.wait_ge(hi_split, n + 1)
                lo_part(g, i, half, slot_at).then_inc(lo_split, 1)

            pool.wait_ge(lo_split, NPC)
            for i in range(NPC):
                n = NPC + i
                split(i, n % 2, WCOLS, 16 * (n // 2 + 1), n)
            with pool.Fori(1, NE // 2) as k:
                for e in range(2):
                    r = pool.value_load(released[0:1, bass.ds(k * 2 + e, 1)], min_val=1, max_val=EXPERT_TILES)
                    after(y_done, r)
                    for i in range(NPC):
                        n = e * NPC + i
                        split(i, n % 2, e * WCOLS, (k * NPC + (n // 2 + 1)) * 16, k * (2 * NPC) + n)

        @block.tensor
        def _(pe):
            mm = nc.tensor.matmul
            def transpose_rows(n):
                pe.wait_ge(row_loaded, n * 16)
                for c in range(DC):
                    last = nc.tensor.transpose(tX[:, c * P:(c + 1) * P], xrow[:, c * P:(c + 1) * P], ident[:])
                last.then_inc(xT_done, 1)

            def up(n, part, base, at):
                f = (FA, FB)[part]
                pe.wait_ge(lo_split, base + (2 * part + 2))
                for w in range(2):
                    bank = ((hA1, hA3), (hB1, hB3))[part][w]
                    for c in range(DC):
                        o = PIECE_AT[2 * part + w] + c * f
                        last = three_passes(nc, bank[:, 0:f], xTh[:, c, :], xTl[:, c, :],
                                            whi[:, bass.ds(at + o, f)], wlo[:, bass.ds(at + o, f)],
                                            c == 0, c == DC - 1)
                last.then_inc((hA_done, hB_done)[part], 1)

            def transpose_act(n):
                pe.wait_ge(actA, n)
                pe.wait_ge(actB, n)
                for c in range(AC):
                    bank, o = (tA, c * P) if c < 3 else (tB, (c - 3) * P)
                    last = nc.tensor.transpose(bank[:, o:o + P], act[:, c * P:(c + 1) * P], ident[:])
                last.then_inc(aT_done, 1)

            def down(n, base, at):
                pe.wait_ge(lo_split, base + NPC)
                pe.wait_ge(aT_hi, n)
                pe.wait_ge(aT_lo, n)
                if not isinstance(n, int) or n > 1:
                    pe.wait_ge(y_copied, n - 1)
                for c in range(AC - 1):
                    w = bass.ds(at + (PIECE_AT[4] + c * DM), DM)
                    three_passes(nc, yP[:, :], aTh[:, c, :], aTl[:, c, :], whi[:, w], wlo[:, w], c == 0, False)
                last = mm(yP[:, :], aTh[0:3 * FLAST, AC - 1, :], whi[0:3 * FLAST, bass.ds(at + PIECE_AT[NPC - 1], DM)],
                          start=False, stop=True)
                last.then_inc(y_done, 1)

            def place(n):
                base = pe.value_load(tile_waits[0:1, bass.ds(n, 1)], min_val=0, max_val=(NE - 1) * NPC)
                at = pe.value_load(tile_slots[0:1, bass.ds(n, 1)], min_val=0, max_val=WCOLS)
                return base, at

            def tile(n, before=True, after=True):
                base, at = place(n)
                pe.wait_ge(xT_hi, n + 1)
                pe.wait_ge(xT_lo, n + 1)
                up(n, 0, base, at)
                if before:
                    transpose_act(n)
                up(n, 1, base, at)
                if after:
                    transpose_rows(n + 2)
                if before:
                    down(n, *place(n - 1))

            transpose_rows(1)
            tile(0, before=False)
            tile(1)
            with pe.Fori(2, EXPERT_TILES - 1) as n:
                tile(n)
            tile(EXPERT_TILES - 1, after=False)
            transpose_act(EXPERT_TILES)
            down(EXPERT_TILES, *place(EXPERT_TILES - 1))

        @block.scalar
        def _(a):
            s = nc.scalar
            def load_rows(n):
                a.dma_start(xrow[:], xg_d[bass.ds(n * P, P), :]).then_inc(row_loaded, 16)

            def hi_xT(n):
                a.wait_ge(xT_done, n)
                s.activation(xTh[:], tX[:].rearrange("p (c t) -> p c t", c=DC), ACT.Copy).then_inc(xT_hi, 1)

            def hi_aT(n):
                a.wait_ge(aT_done, n)
                s.activation(aTh[:, 0:3, :], tA[:, 0:3 * P].rearrange("p (c t) -> p c t", c=3), ACT.Copy)
                s.activation(aTh[:, 3:AC, :], tB[:].rearrange("p (c t) -> p c t", c=4), ACT.Copy).then_inc(aT_hi, 1)

            def gate_part(n, part):
                a.wait_ge((hA_done, hB_done)[part], n + 1)
                if not isinstance(n, int) or n:
                    a.wait_ge((actA, actB)[part], n)
                f0, f = (0, FA)[part], (FA, FB)[part]
                s.activation(silu[:, f0:f0 + f], (hA1, hB1)[part][:, 0:f], ACT.Silu).then_inc((siluA, siluB)[part], 1)

            def store_y(n):
                a.wait_ge(y_done, n)
                if not isinstance(n, int) or n > 1:
                    a.wait_ge(y_stored, (n - 1) * 16)
                s.activation(ysb[:], yP[:], ACT.Copy).then_inc(y_copied, 1)
                a.wait_ge(y_copied, n)
                a.dma_start(y_d[bass.ds((n - 1) * P, P), :], ysb[:]).then_inc(y_stored, 16)

            def tile(n, before=True, after=True, fetch=True):
                gate_part(n, 0)
                if before:
                    hi_aT(n)
                gate_part(n, 1)
                if after:
                    hi_xT(n + 2)
                    if fetch:
                        load_rows(n + 2)
                if before:
                    store_y(n)

            load_rows(0)
            hi_xT(1)
            load_rows(1)
            for i in range(NPC):
                a.wait_ge(raw_loaded[i % 2], 16 * (i // 2 + 1))
                hi_part(s, i, i % 2, 0).then_inc(hi_split, 1)
            tile(0, before=False)
            tile(1)
            with a.Fori(2, EXPERT_TILES - 2) as n:
                tile(n)
            tile(EXPERT_TILES - 2, fetch=False)
            tile(EXPERT_TILES - 1, after=False)
            hi_aT(EXPERT_TILES)
            store_y(EXPERT_TILES)
            a.wait_ge(y_stored, EXPERT_TILES * 16)

        @block.vector
        def _(d):
            v = nc.vector
            def up_part(n, part):
                d.wait_ge((siluA, siluB)[part], n + 1)
                d.wait_ge((hA_done, hB_done)[part], n + 1)
                if not isinstance(n, int) or n:
                    d.wait_ge(aT_done, n)
                f0, f = (0, FA)[part], (FA, FB)[part]
                if part:
                    f -= FLAST
                    four = [P, P // FLAST, FLAST]
                    v.tensor_tensor(act[:, FF - FLAST:].rearrange("p (r c) -> p r c", c=FLAST),
                                    silu[:, FF - FLAST:FF].unsqueeze(1).to_broadcast(four),
                                    hB3[:, f:f + FLAST].unsqueeze(1).to_broadcast(four), ALU.mult)
                v.tensor_tensor(act[:, f0:f0 + f], silu[:, f0:f0 + f], (hA3, hB3)[part][:, 0:f], ALU.mult)\
                    .then_inc((actA, actB)[part], 1)

            def lo_xT(n):
                d.wait_ge(xT_hi, n)
                v.tensor_tensor(xTl[:], tX[:].rearrange("p (c t) -> p c t", c=DC), xTh[:].bitcast(F32),
                                ALU.subtract).then_inc(xT_lo, 1)

            def lo_aT(n):
                d.wait_ge(aT_hi, n)
                v.tensor_tensor(aTl[:, 0:3, :], tA[:, 0:3 * P].rearrange("p (c t) -> p c t", c=3),
                                aTh[:, 0:3, :].bitcast(F32), ALU.subtract)
                v.tensor_tensor(aTl[:, 3:6, :], tB[:, 0:3 * P].rearrange("p (c t) -> p c t", c=3),
                                aTh[:, 3:6, :].bitcast(F32), ALU.subtract)
                last = aTh[2 * FLAST:3 * FLAST, AC - 1, :]
                v.tensor_tensor(last, tB[2 * FLAST:3 * FLAST, 3 * P:4 * P], last.bitcast(F32),
                                ALU.subtract).then_inc(aT_lo, 1)

            def tile(n, before=True, after=True):
                up_part(n, 0)
                if before:
                    lo_aT(n)
                up_part(n, 1)
                if after:
                    lo_xT(n + 2)

            lo_xT(1)
            for i in range(NPC):
                d.wait_ge(hi_split, i + 1)
                lo_part(v, i, i % 2, 0).then_inc(lo_split, 1)
            tile(0, before=False)
            with d.Fori(1, EXPERT_TILES - 1) as n:
                tile(n)
            tile(EXPERT_TILES - 1, after=False)
            lo_aT(EXPERT_TILES)


def back(nc, t, banks, x, weights, xn_d, y_d, base_d, out):
    ctx = ExitStack()
    with ctx:
        def sb(name, shape, dt=F32):
            return ctx.enter_context(nc.sbuf_tensor(name, shape, dt))

        def sem(name):
            return ctx.enter_context(nc.semaphore(name))

        slot, gates = t["slot"], t["gates"]
        A = Attention(nc, ctx, t, banks, weights, "b_", alone=False, conv_banks=(7, 7, 7))
        RING = (4, 5)
        NB = BATCH - 1
        ALSO = TPB // (NB - 1)
        xs = sb("xs", [P, 2, DM])
        res = sb("res", [P, TPB, DM])
        also, alsob = sb("also", [P, DM]), sb("alsob", [P, DM])
        ye = sb("ye", [P, TOPK, DM])
        idx, gate = sb("idx", [P, TOPK], I32), sb("gate", [P, TOPK])

        xs_loaded = [sem(f"xs_loaded{i}") for i in range(2)]
        res_loaded, out_stored = ([sem(f"{name}{i}") for i in range(TPB)] for name in ("res_loaded", "out_stored"))
        picked, gathered, scaled, summed = sem("picked_cols"), sem("gathered"), sem("scaled"), sem("summed")
        res_ready, also_loaded, also_stored = sem("res_ready"), sem("also_loaded"), sem("also_stored")
        pool_turns, sp_turns = sem("a_pool_turns"), sem("a_sp_turns")

        block = ctx.enter_context(nc.Block())

        def batches(eng, body):
            with eng.Fori(0, NB - 1) as b:
                body(b, True)
            body(NB - 1, False)

        @block.sync
        def _(sp):
            def load_xs(b, n):
                rows = xn_d[bass.ds((b + 1) * LEN + n * P, P), :]
                sp.dma_start(xs[:, n % 2, :], rows).then_inc(xs_loaded[n % 2], 16)

            A.load_pieces(sp, [0])
            load_xs(0, 0)
            load_xs(0, 1)
            A.load_pieces(sp, range(1, TAPS))
            for n in range(2, TPB):
                sp.wait_ge(A.xs_T, n - 1)
                load_xs(0, n)
            A.load_small(sp)
            A.load_pieces(sp, range(TAPS, WSPLITS))

            def body(b, more):
                for n in range(TPB):
                    sp.dma_start(res[:, n, :], x[bass.ds((b + 1) * LEN + n * P, P), :]).then_inc(res_loaded[n], 16)
                if more:
                    for n in range(TPB):
                        sp.wait_ge(A.xs_T, (b + 1) * TPB + (n - 1))
                        sp.sem_inc(sp_turns, 1)
                        load_xs(b + 1, n)
                for n in range(TPB):
                    sp.wait_ge(A.out_ready, b * TPB + (n + 1))
                    sp.sem_inc(sp_turns, 1)
                    sp.dma_start(out[bass.ds((b + 1) * LEN + n * P, P), :], res[:, n, :]).then_inc(out_stored[n], 16)
                for n in range(TPB):
                    sp.wait_ge(out_stored[n], (b + 1) * 16)
                    sp.sem_inc(sp_turns, 1)

            batches(sp, body)

        @block.gpsimd
        def _(pool):
            g = nc.gpsimd
            A.constants(pool)
            pool.wait_ge(A.small_loaded, 16 * A.SMALL)

            def after(semaphore, count):
                pool.wait_ge(semaphore, count)
                pool.sem_inc(pool_turns, 1)

            def gather(i, n):
                g.tensor_copy(idx[:], slot[:, :, bass.ds(i, 1)].rearrange("p k a -> p (k a)")).then_inc(picked, 1)
                g.tensor_copy(gate[:], gates[:, :, bass.ds(i, 1)].rearrange("p k a -> p (k a)")).then_inc(picked, 1)
                after(picked, (n + 1) * 2)
                for k in range(TOPK):
                    g.indirect_dma_start(ye[:, k, :], None, y_d[:, :],
                                         bass.IndirectOffsetOnAxis(ap=idx[:, k:k + 1].bitcast(U32), axis=0))\
                        .then_inc(gathered, 16)

            def total(r, other, n):
                g.tensor_tensor(r, r, other, ALU.add).then_inc(summed, 1)
                after(gathered, (n + 1) * (16 * TOPK))
                for k in range(TOPK):
                    g.tensor_scalar(ye[:, k, :], ye[:, k, :], gate[:, k:k + 1], None, ALU.mult).then_inc(scaled, 1)
                after(scaled, (n + 1) * TOPK)
                pool.wait_ge(summed, n * 3 + 1)
                g.tensor_tensor(r, r, ye[:, 0, :], ALU.add).then_inc(summed, 1)
                pool.wait_ge(summed, n * 3 + 2)
                return g.tensor_tensor(r, r, ye[:, 1, :], ALU.add).then_inc(summed, 1)

            def body(b, more):
                for n in range(TPB):
                    k = b * (TPB + ALSO) + n
                    gather((b + 1) * TPB + n, k)
                    pool.wait_ge(res_loaded[n], (b + 1) * 16)
                    total(res[:, n, :], A.pjb[:], k)
                    after(summed, (k + 1) * 3)
                    pool.sem_inc(res_ready, 1)
                if more:
                    for n in range(ALSO):
                        k = b * (TPB + ALSO) + (TPB + n)
                        i = b * ALSO + n
                        at = bass.ds(i * P, P)
                        g.dma_start(also[:], x[at, :]).then_inc(also_loaded, 16)
                        g.dma_start(alsob[:], base_d[at, :]).then_inc(also_loaded, 16)
                        gather(i, k)
                        after(also_loaded, (i + 1) * 32)
                        total(also[:], alsob[:], k)
                        after(summed, (k + 1) * 3)
                        g.dma_start(out[at, :], also[:]).then_inc(also_stored, 16)
                        after(also_stored, (i + 1) * 16)

            batches(pool, body)

        @block.tensor
        def _(pe):
            def transpose_x(b, n):
                pe.wait_ge(xs_loaded[n % 2], (b * (TPB // 2) + (n // 2 + 1)) * 16)
                A.pe_transpose_x(pe, b * TPB + n, n, xs[:, n % 2, :], RING)

            for n in range(TPB):
                transpose_x(0, n)
            pe.wait_ge(A.zeroed, 4)
            pe.wait_ge(A.x_hi, TPB)
            pe.wait_ge(A.x_lo, TPB)
            for n in range(PROJ):
                if n:
                    pe.wait_ge(A.conv_hi, n)
                    pe.wait_ge(A.conv_lo, n)
                for tap in range(TAPS):
                    if n == 0:
                        pe.wait_ge(A.pieces_lo, tap + 1)
                    A.pe_conv(0, n, range(tap * DC, (tap + 1) * DC))
            pe.wait_ge(A.pieces_lo, WSPLITS)
            pe.wait_ge(A.small_loaded, 16 * A.SMALL)

            def body(b, more):
                def fill(g, when):
                    n, count = FILL[g]
                    begin = sum(c for m, c in FILL[:g] if m == n)
                    if g == 0 and when == 0:
                        pe.wait_ge(A.x_hi, (b + 2) * TPB)
                        pe.wait_ge(A.x_lo, (b + 2) * TPB)
                    if n and begin == 0 and when == 0:
                        pe.wait_ge(A.conv_hi, (b + 1) * PROJ + n)
                        pe.wait_ge(A.conv_lo, (b + 1) * PROJ + n)
                    j = begin + when * count // 2
                    A.pe_conv(b + 1, n, range(j, j + count // 2))

                A.pe_proj(pe, b, (lambda n: transpose_x(b + 1, n)) if more else None)
                A.pe_steps(pe, b, fill if more else None)
                if more:
                    pe.wait_ge(A.conv_hi, (b + 2) * PROJ)
                    pe.wait_ge(A.conv_lo, (b + 2) * PROJ)
                A.pe_out(pe, b)
                pe.wait_ge(A.out_ready, (b + 1) * TPB)

            batches(pe, body)

        @block.scalar
        def _(a):
            A.hi_piece(a, 0)
            for n in range(TPB):
                A.act_hi_x(a, n, n, RING)
            for n in range(1, WSPLITS):
                A.hi_piece(a, n)
            a.wait_ge(A.small_loaded, 16 * A.SMALL)
            for n in range(PROJ):
                A.act_conv(a, 0, n)
            a.wait_ge(A.bias_scaled, 1)

            def body(b, more):
                def fill(g):
                    n, count = FILL[g]
                    if g + 1 == STEPS or FILL[g + 1][0] != n:
                        A.act_conv(a, b + 1, n)

                A.act_proj(a, b, (lambda n: A.act_hi_x(a, (b + 1) * TPB + n, n, RING)) if more else None)
                A.act_steps(a, b, fill if more else None)
                A.act_out(a, b)

            batches(a, body)

        @block.vector
        def _(d):
            v = nc.vector
            A.lo_piece(v, 0)
            for n in range(TPB):
                A.dve_lo_x(d, n, n, RING)
            for n in range(1, WSPLITS):
                A.lo_piece(v, n)
            d.wait_ge(A.small_loaded, 16 * A.SMALL)
            v.tensor_scalar(A.bqs, A.bqs, SCALE, None, ALU.mult).then_inc(A.bias_scaled, 1)
            d.wait_ge(A.mask_ready, 2)
            for n in range(PROJ):
                A.dve_conv(d, 0, n)

            def body(b, more):
                def fill(g):
                    n, count = FILL[g]
                    if g + 1 == STEPS or FILL[g + 1][0] != n:
                        A.dve_conv(d, b + 1, n)

                A.dve_proj(d, b, (lambda n: A.dve_lo_x(d, (b + 1) * TPB + n, n, RING)) if more else None)
                A.dve_steps(d, b, fill if more else None)
                for n in range(TPB):
                    d.wait_ge(A.out_done, b * TPB + (n + 1))
                    d.wait_ge(res_ready, b * TPB + (n + 1))
                    v.tensor_tensor(res[:, n, :], banks[n][:], res[:, n, :], ALU.add).then_inc(A.out_ready, 1)

            batches(d, body)


_OUT = ((TOK, DM), "float32")


def kernel(**inputs):
    import numpy as _np
    import concourse.bacc as _bacc
    from concourse import mybir as _mybir
    from concourse.bass_utils import run_bass_kernel_spmd as _run

    g = {k.replace("L0_attn_", "").replace("L0_ffn_", "ffn_"): _np.asarray(v) for k, v in inputs.items()}

    def chunked(w, rows):
        e, r, c = w.shape
        return w.reshape(e, r // rows, rows, c).transpose(0, 2, 1, 3).reshape(e, rows, -1)

    w1, w3, w2 = (g[k].transpose(0, 2, 1) for k in ("ffn_w1", "ffn_w3", "ffn_w2"))
    last = _np.zeros((NE, P, DM), w2.dtype)
    last[:, :3 * FLAST] = _np.tile(w2[:, (AC - 1) * P:], (1, 3, 1))
    experts = _np.concatenate(
        [chunked(w[:, :, f], P) for f in (slice(0, FA), slice(FA, FF)) for w in (w1, w3)]
        + [chunked(w2[:, :(AC - 1) * P], P), last], axis=2)
    arrays = {
        "x": g["inputs"].reshape(TOK, DM),
        "conv_w": g["conv_w"],
        "columns": _np.concatenate([g[k].reshape(-1, P).T for k in ("conv_b", "bq", "bk", "bo")], axis=1),
        **{k: g[k] for k in ("wq", "wk", "wv", "bv", "wo", "proj_w", "proj_b")},
        "gate": g["ffn_gate_w"].T.reshape(DC, P, NE).transpose(1, 0, 2),
        "experts": experts,
    }
    arrays = {k: _np.ascontiguousarray(v) for k, v in arrays.items()}
    nc = _bacc.Bacc("TRN2", target_bir_lowering=False, num_devices=1)
    args = [nc.dram_tensor(f"in_{k}", v.shape, _mybir.dt.from_np(v.dtype), kind="ExternalInput").ap()
            for k, v in arrays.items()]
    out = nc.dram_tensor("out_0", _OUT[0], _mybir.dt.from_np(_np.dtype(_OUT[1])), kind="ExternalOutput").ap()
    build(nc, *args, out)
    r = _run(nc, [{f"in_{k}": v for k, v in arrays.items()}], core_ids=[0])
    return _np.asarray(r.results[0]["out_0"]).reshape(BATCH, LEN, DM)
```

```python
import concourse.bass as bass
from concourse import mybir
from contextlib import ExitStack

F32 = mybir.dt.float32
F32R = mybir.dt.float32r
I32 = mybir.dt.int32
U32 = mybir.dt.uint32
ALU = mybir.AluOpType
ACT = mybir.ActivationFunctionType
AX = mybir.AxisListType.X

P = 128
BATCH, LEN, DM = 4, 512, 512
TOK = BATCH * LEN
NT = TOK // P
TPB = LEN // P
DC = DM // P
W, H, DH = 128, 16, 64
NE, FF, TOPK = 8, 800, 2
EPS = 1e-5
NEG = -1e9
BIG = 3e38
SCALE = DH ** -0.5

EXPERT_TILES = (TOPK * TOK + (P - 1) * NE) // P
LEAST_TILES = TOPK * TOK // P
SPARE = EXPERT_TILES - LEAST_TILES
SLOTS = EXPERT_TILES * P
NPAD = NE + SPARE
DUMP = SLOTS

FA, FB = 3 * P, FF - 3 * P
AC = (FF + P - 1) // P
FLAST = FF - (AC - 1) * P
PIECES = [(DC * FA, P), (DC * FA, P), (DC * FB, P), (DC * FB, P), (3 * DM, P), (3 * DM, P), (DM, 3 * FLAST)]
PIECE_AT = [sum(c for c, _ in PIECES[:i]) for i in range(len(PIECES))]
WCOLS = sum(c for c, _ in PIECES)
NPC = len(PIECES)
FIRST = NPC - 1
RAWW = max(c for c, _ in PIECES)
TAPS, PROJ = 3, 3
NO = W * PROJ
HP = H // 2
GH = 8
GP = GH // 2
STEPS = TPB * H // GH
LP = LEN + 2
RINGS = 3
LATE = STEPS - TPB + 1
OUT_BANKS = (1, 2, 5, 7)
FILL_BANKS = (7, 7, 3)
TAKE = (1, LATE, STEPS - 1)
NP = 2 * HP + 2 * TPB
NV = 2 * TPB
COLUMNS = PROJ + 2 * HP + 1
WSPLITS = TAPS + PROJ
FILL = [(0, 6), (0, 6), (1, 6), (1, 4), (1, 2), (2, 6), (2, 4), (2, 2)]



def three_passes(nc, out, hi, lo, rhi, rlo, first=True, last=True):
    nc.tensor.matmul(out, hi, rhi, start=first, stop=False)
    nc.tensor.matmul(out, hi, rlo, start=False, stop=False)
    return nc.tensor.matmul(out, lo, rhi, start=False, stop=last)


def aligned(at):
    return -(-at // 32) * 32


def Chain(eng, semaphore):
    count = [0]

    def link(ins):
        count[0] += 1
        ins.then_inc(semaphore, 1)
        eng.wait_ge(semaphore, count[0])
    return link


def build(nc, x, conv_w, columns, wq, wk, wv, bv, wo, proj_w, proj_b, gate, experts, out):
    xn_d = nc.dram_tensor("xn_rows", [TOK, DM], F32, kind="Internal").ap()
    xg_d = nc.dram_tensor("dispatched_rows", [SLOTS + NPAD * P, DM], F32, kind="Internal").ap()
    y_d = nc.dram_tensor("expert_rows", [SLOTS, DM], F32, kind="Internal").ap()
    base_d = nc.dram_tensor("first_attention", [LEN, DM], F32, kind="Internal").ap()
    ctx = ExitStack()
    with ctx:
        def keep(name, shape, dt=F32):
            return ctx.enter_context(nc.sbuf_tensor(name, shape, dt))

        t = dict(
            ident=keep("ident", [P, P]),
            slot=keep("slot", [P, TOPK, NT], I32),
            gates=keep("gates", [P, TOPK, NT]),
            tile_waits=keep("tile_waits", [1, EXPERT_TILES], I32),
            tile_slots=keep("tile_slots", [1, EXPERT_TILES], I32),
            released=keep("released", [1, NE + 1], I32),
            qkvh=keep("second_qkvh", [P, PROJ, LEN], F32R),
            qkvl=keep("second_qkvl", [P, PROJ, LEN], F32R),
            columns=keep("columns_s", [P, COLUMNS]),
            bvb=keep("bvb", [P, H * DH]),
            shared_at=aligned(nc.sbuf_base),
            shared=keep("shared", [P, 2, RAWW]),
        )
        t["first_raw"] = nc.alloc_sbuf_tensor_at("first_raw", [P, PIECE_AT[FIRST]], F32, offset=nc.sbuf_base)
        t["cw_at"] = aligned(nc.sbuf_base) + 4 * (2 * HP * LEN + HP * W + 2 * DM)
        t["pw_at"] = t["cw_at"] + 4 * (2 * TAPS * DC * NO + 2 * DC * LP + TPB * H * DH + HP * LEN)
        t["cw"] = nc.alloc_sbuf_tensor_at("last_cw", [P, 2, TAPS * DC, NO], F32R, offset=t["cw_at"])
        t["pw"] = nc.alloc_sbuf_tensor_at("last_pw", [P, PROJ, 2, H * DH], F32R, offset=t["pw_at"])
        for slot, at, size in ((1, t["cw_at"], 2 * TAPS * DC * NO), (3, t["pw_at"], 2 * PROJ * H * DH)):
            assert nc.sbuf_base + 4 * slot * WCOLS <= at and at + 4 * size <= nc.sbuf_base + 4 * (slot + 1) * WCOLS
        t["base_stored"] = [ctx.enter_context(nc.semaphore(f"base_stored{i}")) for i in range(2)]
        t["y_stored"] = ctx.enter_context(nc.semaphore("y_stored"))
        t["first_loaded"] = ctx.enter_context(nc.semaphore("first_loaded"))
        banks = [ctx.enter_context(nc.psum_tensor(f"bank{i}", [P, 512], F32)) for i in range(8)]
        weights = (conv_w, columns, wq, wk, wv, bv, wo, proj_w, proj_b)
        front(nc, t, banks, x, gate, weights, experts, xn_d, xg_d, base_d)
        experts_block(nc, t, banks, experts, (conv_w, wq, wk, wv), xg_d, y_d)
        back(nc, t, banks, x, weights, xn_d, y_d, base_d, out)


class Attention:

    def __init__(self, nc, ctx, t, banks, weights, name, first):
        def sb(what, shape, dt=F32):
            return ctx.enter_context(nc.sbuf_tensor(name + what, shape, dt))

        def sem(what):
            return ctx.enter_context(nc.semaphore(name + what))

        self.nc, self.banks, self.ident, self.weights = nc, banks, t["ident"], weights
        qk_at = aligned(nc.sbuf_base)
        self.qk = sb("qk", [P, 2, HP, LEN])
        self.wo_s, self.pj_s = sb("wo_s", [P, HP, W]), sb("pj_s", [P, DM])
        self.pjb_at = aligned(nc.sbuf_base)
        self.pjb = sb("pjb", [P, DM])
        cw_at = aligned(nc.sbuf_base)
        cw = sb("cw", [P, 2, TAPS * DC, NO], F32R)
        self.xTh, self.xTl = sb("xTh", [P, DC, LP], F32R), sb("xTl", [P, DC, LP], F32R)
        if not first:
            self.vh, self.oT = sb("vh", [P, TPB, H * DH]), sb("oT", [P, HP, LEN])
        pw_at = aligned(nc.sbuf_base)
        pw = sb("pw", [P, PROJ, 2, H * DH], F32R)
        if first:
            self.qkvh, self.qkvl = sb("qkvh", [P, PROJ, LEN], F32R), sb("qkvl", [P, PROJ, LEN], F32R)
            self.vh_at = pw_at
            self.vh = nc.alloc_sbuf_tensor_at(name + "vh", [P, TPB, H * DH], F32, offset=pw_at)
            self.oT = nc.alloc_sbuf_tensor_at(name + "oT", [P, HP, LEN], F32, offset=pw_at + 4 * TPB * H * DH)
            self.cwf = nc.alloc_sbuf_tensor_at(name + "cwf", [P, TAPS * DC, NO], F32, offset=qk_at)
            self.pwf = nc.alloc_sbuf_tensor_at(name + "pwf", [P, PROJ, H * DH], F32, offset=qk_at + 4 * TAPS * DC * NO)
        else:
            self.qkvh, self.qkvl = t["qkvh"], t["qkvl"]
            assert (cw_at, pw_at) == (t["cw_at"], t["pw_at"])
            cw, pw = t["cw"], t["pw"]
        self.cwh, self.cwl = cw[:, 0, :, :], cw[:, 1, :, :]
        self.pwh, self.pwl = pw[:, :, 0, :], pw[:, :, 1, :]
        self.pT_at = aligned(nc.sbuf_base)
        self.pT = sb("pT", [P, GH, P])
        self.s = nc.alloc_sbuf_tensor_at(name + "s", [P, RINGS, GH, P], F32, offset=t["shared_at"])
        self.nmax, self.rsum, self.rinv = sb("nmax", [P, RINGS, GH]), sb("rsum", [P, 4, GH]), sb("rinv", [P, 2, GH])
        self.att = nc.alloc_sbuf_tensor_at(name + "att", [P, LEN], F32, offset=self.pT_at)
        self.mask = sb("mask", [P, P])
        self.columns, self.bvb, self.first = t["columns"], t["bvb"], first
        self.cb, self.bqs, self.bks, self.bos = (
            self.columns[:, a:z] for a, z in ((0, PROJ), (PROJ, PROJ + HP), (PROJ + HP, PROJ + 2 * HP), (COLUMNS - 1, COLUMNS)))

        self.piece_loaded = [sem(f"piece_loaded{i}") for i in range(WSPLITS)]
        self.small_loaded = sem("small_loaded")
        self.conv_pieces_hi, self.conv_pieces_lo = sem("conv_pieces_hi"), sem("conv_pieces_lo")
        self.proj_pieces_hi, self.proj_pieces_lo = sem("proj_pieces_hi"), sem("proj_pieces_lo")
        self.v_banks = (4, 5) if first else (4, 5, 6)
        self.small = 4 if first else 3
        self.pjb_loaded = sem("pjb_loaded") if first else self.small_loaded
        self.bias_scaled = sem("bias_scaled")
        self.zeroed = sem("zeroed")
        self.mask_ready = sem("mask_ready")
        self.xs_T = sem("xs_T")
        self.x_hi = sem("x_hi")
        self.x_lo = sem("x_lo")
        self.conv_done = sem("conv_done")
        self.conv_hi = sem("conv_hi")
        self.conv_lo = sem("conv_lo")
        self.proj_done = sem("proj_done")
        self.q_ready = sem("q_ready")
        self.k_ready = sem("k_ready")
        self.v_ready = sem("v_ready")
        self.s_done = sem("s_done")
        self.masked = sem("masked")
        self.maxed = sem("maxed")
        self.p_ready = sem("p_ready")
        self.p_scaled = sem("p_scaled")
        self.pT_done = sem("pT_done")
        self.pT_ready, self.pT_half = sem("pT_ready"), sem("pT_half")
        self.pv_done = sem("pv_done")
        self.inv_ready = sem("inv_ready")
        self.oT_ready = sem("oT_ready")
        self.wo_done = sem("wo_done")
        self.att_ready = sem("att_ready")
        self.out_done = sem("out_done")
        self.out_ready = sem("out_ready")


    def load_pieces(self, eng, which):
        conv_w, _, wq, wk, wv = self.weights[:5]
        for n in which:
            if n < TAPS:
                eng.dma_start(self.cwf[:, n * DC:(n + 1) * DC, :], conv_w[n].rearrange("(c p) o -> p c o", p=P))\
                    .then_inc(self.piece_loaded[n], 16)
            else:
                eng.dma_start(self.pwf[:, n - TAPS, :], (wq, wk, wv)[n - TAPS].rearrange("d h e -> d (h e)"))\
                    .then_inc(self.piece_loaded[n], 16)

    def load_small(self, eng):
        _, columns, _, _, _, bv, wo, proj_w, _ = self.weights
        if self.first:
            eng.dma_start(self.columns[:], columns).then_inc(self.small_loaded, 16)
            eng.dma_start(self.bvb[:], bv.rearrange("h e -> (h e)").rearrange("(n w) -> n w", n=1)
                          .to_broadcast([P, H * DH])).then_inc(self.small_loaded, 16)
        eng.dma_start(self.wo_s[:], wo.rearrange("h e w -> (h e) w").rearrange("(c p) w -> p c w", p=P))\
            .then_inc(self.small_loaded, 16)
        eng.dma_start(self.pj_s[:], proj_w).then_inc(self.small_loaded, 16)
        if not self.first:
            self.load_pjb(eng)

    def load_pjb(self, eng):
        proj_b = self.weights[-1]
        eng.dma_start(self.pjb[:], proj_b.rearrange("(n w) -> n w", n=1).to_broadcast([P, DM]))\
            .then_inc(self.pjb_loaded, 16)

    def piece(self, n):
        if n < TAPS:
            c = slice(n * DC, (n + 1) * DC)
            return self.cwh[:, c, :], self.cwl[:, c, :], self.cwf[:, c, :]
        return self.pwh[:, n - TAPS, :], self.pwl[:, n - TAPS, :], self.pwf[:, n - TAPS, :]

    def hi_piece(self, eng, n):
        hi, _, src = self.piece(n)
        eng.wait_ge(self.piece_loaded[n], 16)
        ins = eng.activation(hi, src, ACT.Copy) if eng is self.nc.scalar else eng.tensor_copy(hi, src)
        ins.then_inc(self.conv_pieces_hi if n < TAPS else self.proj_pieces_hi, 1)

    def lo_piece(self, eng, n):
        hi, lo, src = self.piece(n)
        if n < TAPS:
            eng.wait_ge(self.conv_pieces_hi, n + 1)
        else:
            eng.wait_ge(self.proj_pieces_hi, n + 1 - TAPS)
        eng.tensor_tensor(lo, src, hi.bitcast(F32), ALU.subtract)\
            .then_inc(self.conv_pieces_lo if n < TAPS else self.proj_pieces_lo, 1)

    def constants(self, pool):
        g = self.nc.gpsimd
        g.memset(self.mask[:], BIG).then_inc(self.mask_ready, 1)
        pool.wait_ge(self.mask_ready, 1)
        g.affine_select(out=self.mask[:], in_=self.mask[:], compare_op=ALU.is_ge, fill=NEG, base=0,
                        pattern=[[-1, P]], channel_multiplier=1).then_inc(self.mask_ready, 1)
        for z in (self.xTh, self.xTl):
            for col in (0, LP - 1):
                g.memset(z[:, :, col:col + 1].bitcast(F32), 0.0).then_inc(self.zeroed, 1)


    def pe_transpose_x(self, pe, i, n, rows, ring):
        if n >= len(ring):
            pe.wait_ge(self.x_hi, i - len(ring) + 1)
            pe.wait_ge(self.x_lo, i - len(ring) + 1)
        bank = self.banks[ring[n % len(ring)]]
        for c in range(DC):
            last = self.nc.tensor.transpose(bank[:, c * P:(c + 1) * P], rows[:, c * P:(c + 1) * P], self.ident[:])
        last.then_inc(self.xs_T, 1)

    def act_hi_x(self, act, i, n, ring):
        act.wait_ge(self.xs_T, i + 1)
        self.nc.scalar.activation(self.xTh[:, :, 1 + n * P:1 + (n + 1) * P],
                                  self.banks[ring[n % len(ring)]][:].rearrange("p (c t) -> p c t", c=DC), ACT.Copy)\
            .then_inc(self.x_hi, 1)

    def dve_lo_x(self, dve, i, n, ring):
        dve.wait_ge(self.x_hi, i + 1)
        dst = slice(1 + n * P, 1 + (n + 1) * P)
        self.nc.vector.tensor_tensor(self.xTl[:, :, dst], self.banks[ring[n % len(ring)]][:].rearrange("p (c t) -> p c t", c=DC),
                                     self.xTh[:, :, dst].bitcast(F32), ALU.subtract).then_inc(self.x_lo, 1)


    def pe_conv(self, bank, n, js):
        for j in js:
            tap, c = j // DC, j % DC
            last = three_passes(self.nc, self.banks[bank][:], self.cwh[:, j, n * W:(n + 1) * W],
                                self.cwl[:, j, n * W:(n + 1) * W], self.xTh[:, c, tap:tap + LEN],
                                self.xTl[:, c, tap:tap + LEN], j == 0, j == TAPS * DC - 1)
        if js[-1] == TAPS * DC - 1:
            last.then_inc(self.conv_done, 1)


    def act_conv(self, act, b, n, to, bank):
        act.wait_ge(self.conv_done, b * PROJ + (n + 1))
        self.nc.scalar.activation(to[0][:, n, :], self.banks[bank][:], ACT.Identity, bias=self.cb[:, n:n + 1])\
            .then_inc(self.conv_hi, 1)

    def dve_conv(self, dve, b, n, to, bank):
        dve.wait_ge(self.conv_hi, b * PROJ + (n + 1))
        self.nc.vector.scalar_tensor_tensor(to[1][:, n, :], self.banks[bank][:], self.cb[:, n:n + 1],
                                            to[0][:, n, :].bitcast(F32), ALU.add, ALU.subtract)\
            .then_inc(self.conv_lo, 1)


    def pe_proj(self, pe, b, between, fill=None):
        for r in range(NP):
            if r == 2 * HP:
                if self.first:
                    pe.wait_ge(self.conv_hi, PROJ)
                    pe.wait_ge(self.conv_lo, PROJ)
            if r < 2 * HP:
                bank = self.banks[r % 4][:]
                if r >= 4:
                    pe.wait_ge((self.q_ready, self.k_ready)[r % 2], b * HP + ((r - 4) // 2 + 1))
            else:
                i = r - 2 * HP
                bank = self.banks[self.v_banks[i % len(self.v_banks)]][:]
                if i >= len(self.v_banks):
                    pe.wait_ge(self.v_ready, b * NV + (i - len(self.v_banks) + 1))
                if i == 2 and between and not self.first:
                    pe.wait_ge(self.x_hi, (b + 1) * TPB)
                    pe.wait_ge(self.x_lo, (b + 1) * TPB)
            if r < 2 * HP:
                c, w = r // 2, r % 2
                last = three_passes(self.nc, bank, self.pwh[:, w, c * P:(c + 1) * P], self.pwl[:, w, c * P:(c + 1) * P],
                                    self.qkvh[:, w, :], self.qkvl[:, w, :])
            else:
                blk, half = (r - 2 * HP) // 2, r % 2
                last = three_passes(self.nc, bank, self.qkvh[:, 2, blk * P:(blk + 1) * P],
                                    self.qkvl[:, 2, blk * P:(blk + 1) * P],
                                    self.pwh[:, 2, half * 512:(half + 1) * 512], self.pwl[:, 2, half * 512:(half + 1) * 512])
            last.then_inc(self.proj_done, 1)
            if between and not self.first and r < 2 * HP and r % 4 == 3:
                between(r // 4)
            if self.first and r >= 2 * HP and r % 2:
                between((r - 2 * HP) // 2)
            if r == 2 * HP:
                pe.wait_ge(self.q_ready, (b + 1) * HP)
                pe.wait_ge(self.k_ready, (b + 1) * HP)
                self.pe_scores(pe, b, 0)
            if r == 2 * HP + 2:
                self.pe_scores(pe, b, 1)
            if fill and r == 2 * HP + 4:
                fill(0, 0)

    def act_proj(self, act, b, between):
        for c in range(HP):
            act.wait_ge(self.proj_done, b * NP + (2 * c + 1))
            self.nc.scalar.activation(self.qk[:, 0, c, :], self.banks[2 * c % 4][:], ACT.Identity,
                                      bias=self.bqs[:, c:c + 1], scale=SCALE).then_inc(self.q_ready, 1)
            if self.first:
                act.wait_ge(self.proj_done, b * NP + (2 * c + 2))
                self.nc.scalar.activation(self.qk[:, 1, c, :], self.banks[(2 * c + 1) % 4][:], ACT.Identity,
                                          bias=self.bks[:, c:c + 1]).then_inc(self.k_ready, 1)
            elif between and c % 2 == 1:
                between(c // 2)
        if self.first:
            for n in range(TPB):
                between(n)
                if n == 1:
                    self.exps(act, b, 0)

    def dve_proj(self, dve, b, between):
        v = self.nc.vector
        for c in () if self.first else range(HP):
            dve.wait_ge(self.proj_done, b * NP + (2 * c + 2))
            v.tensor_scalar(self.qk[:, 1, c, :], self.banks[(2 * c + 1) % 4][:], self.bks[:, c:c + 1], None, ALU.add)\
                .then_inc(self.k_ready, 1)
            if between and c % 2 == 1:
                between(c // 2)
        for r in range(2 * TPB):
            dve.wait_ge(self.proj_done, b * NP + (2 * HP + r + 1))
            half = slice((r % 2) * 512, (r % 2) * 512 + 512)
            v.tensor_tensor(self.vh[:, r // 2, half], self.banks[self.v_banks[r % len(self.v_banks)]][:], self.bvb[:, half], ALU.add)\
                .then_inc(self.v_ready, 1)
            if self.first and r % 2:
                between(r // 2)
            if r in (0, 2):
                self.mask_max(dve, b, r // 2)
            if r == NV - 3:
                self.scale(dve, b, 0)


    def pe_scores(self, pe, b, g):
        blk, hh = g // 2, g % 2
        if g >= 2:
            pe.wait_ge(self.masked, b * STEPS + (g - 1))
        for pr in range(GP):
            for half in range(2):
                rows, tok = slice(64 * half, 64 * half + 64), slice(blk * P, (blk + 1) * P)
                last = self.nc.tensor.matmul(self.banks[2 * (g % 2) + half][:, pr * P:(pr + 1) * P],
                                             self.qk[rows, 0, hh * GP + pr, tok], self.qk[rows, 1, hh * GP + pr, tok],
                                             start=True, stop=True)
        last.then_inc(self.s_done, 1)

    def pe_steps(self, pe, b, fill):
        nc, banks = self.nc, self.banks

        def transpose_p(g):
            pe.wait_ge(self.p_scaled, b * STEPS + (g + 1))
            for j in range(GH):
                last = nc.tensor.transpose(banks[4 + j // GP][:, (j % GP) * P:(j % GP + 1) * P],
                                           self.s[:, g % RINGS, j, :], self.ident[:])
            last.then_inc(self.pT_done, 1)

        self.pe_scores(pe, b, 2)
        pe.wait_ge(self.v_ready, (b + 1) * NV)
        transpose_p(0)
        if fill:
            if self.first:
                fill(0, 0)
            fill(0, 1)
        for g in range(STEPS):
            if g + RINGS < STEPS:
                self.pe_scores(pe, b, g + RINGS)
            if fill and g:
                fill(g, 0)
            pe.wait_ge(self.pT_ready, b * STEPS + (g + 1))
            if not fill:
                pe.wait_ge(self.pT_half, g + 1)
            if g:
                pe.wait_ge(self.oT_ready, b * STEPS + g)
            blk, hh = g // 2, g % 2
            for h in range(GH):
                j, rows = (h % 2) * GP + h // 2, slice((h % 2) * DH, (h % 2 + 1) * DH)
                at = (hh * GH + h) * DH
                last = nc.tensor.matmul(banks[6][rows, h // 2 * P:(h // 2 + 1) * P], self.vh[:, blk, at:at + DH],
                                        self.pT[:, j, :], start=True, stop=True)
            last.then_inc(self.pv_done, 1)
            if g + 1 < STEPS:
                transpose_p(g + 1)
            if g == LATE:
                pe.wait_ge(self.masked, b * STEPS + STEPS)
            if g >= LATE:
                self.pe_wo(pe, b, g - LATE)
            if fill and g:
                fill(g, 1)

    def exps(self, act, b, g):
        act.wait_ge(self.maxed, b * STEPS + (g + 1))
        for j in range(GH):
            last = self.nc.scalar.activation(self.s[:, g % RINGS, j, :], self.s[:, g % RINGS, j, :], ACT.Exp,
                                             bias=self.nmax[:, g % RINGS, j:j + 1], accum_out=self.rsum[:, g % 4, j:j + 1])
        last.then_inc(self.p_ready, 1)

    def act_steps(self, act, b, fill):
        sc = self.nc.scalar

        def oT_copy(g):
            act.wait_ge(self.pv_done, b * STEPS + (g + 1))
            blk, hh = g // 2, g % 2
            sc.activation(self.oT[:, hh * GP:(hh + 1) * GP, blk * P:(blk + 1) * P],
                          self.banks[6][:].rearrange("p (c t) -> p c t", c=GP), ACT.Copy).then_inc(self.oT_ready, 1)

        if not self.first:
            self.exps(act, b, 0)
        self.exps(act, b, 1)
        for g in range(STEPS):
            if not fill:
                act.wait_ge(self.pT_done, b * STEPS + (g + 1))
                sc.activation(self.pT[:, GP:, :], self.banks[5][:].rearrange("p (j k) -> p j k", j=GP), ACT.Copy)\
                    .then_inc(self.pT_half, 1)
            if g + 2 < STEPS:
                self.exps(act, b, g + 2)
            if g == STEPS - 1:
                self.act_out(act, b, 0)
            oT_copy(g)
            if fill:
                fill(g)
        self.act_out(act, b, 1)

    def mask_max(self, dve, b, g):
        v = self.nc.vector
        dve.wait_ge(self.s_done, b * STEPS + (g + 1))
        for half in range(2):
            last = v.tensor_tensor(self.s[:, g % RINGS, half * GP:(half + 1) * GP, :],
                                   self.banks[2 * (g % 2) + half][:].rearrange("p (j k) -> p j k", j=GP),
                                   self.mask[:].unsqueeze(1).to_broadcast([P, GP, P]), ALU.min)
        last.then_inc(self.masked, 1)
        dve.wait_ge(self.masked, b * STEPS + (g + 1))
        v.tensor_reduce(self.nmax[:, g % RINGS, :], self.s[:, g % RINGS, :, :], AX, ALU.max, negate=True)\
            .then_inc(self.maxed, 1)

    def scale(self, dve, b, g):
        v = self.nc.vector
        dve.wait_ge(self.p_ready, b * STEPS + (g + 1))
        v.reciprocal(self.rinv[:, g % 2, :], self.rsum[:, g % 4, :]).then_inc(self.inv_ready, 1)
        dve.wait_ge(self.inv_ready, b * STEPS + (g + 1))
        v.tensor_tensor(self.s[:, g % RINGS, :, :], self.s[:, g % RINGS, :, :],
                        self.rinv[:, g % 2, :].unsqueeze(2).to_broadcast([P, GH, P]), ALU.mult)\
            .then_inc(self.p_scaled, 1)

    def dve_steps(self, dve, b, fill):
        v, banks = self.nc.vector, self.banks

        self.mask_max(dve, b, 2)
        for g in range(STEPS):
            if g + 1 < STEPS:
                self.scale(dve, b, g + 1)
            dve.wait_ge(self.pT_done, b * STEPS + (g + 1))
            for half in range(2 if fill else 1):
                last = v.tensor_copy(self.pT[:, half * GP:(half + 1) * GP, :],
                                     banks[4 + half][:].rearrange("p (j k) -> p j k", j=GP))
            last.then_inc(self.pT_ready, 1)
            if g + RINGS < STEPS:
                self.mask_max(dve, b, g + RINGS)
            if fill:
                fill(g)


    def pe_fill(self, pe, b, c, g, when):
        n, count = FILL[g]
        begin = sum(m for k, m in FILL[:g] if k == n)
        if g == 0 and when == 0:
            pe.wait_ge(self.x_hi, (c + 1) * TPB)
            pe.wait_ge(self.x_lo, (c + 1) * TPB)
        if n == 1 and begin == 0 and when == 0:
            pe.wait_ge(self.conv_hi, c * PROJ + n)
            pe.wait_ge(self.conv_lo, c * PROJ + n)
        if n == 2 and begin == 0 and when == 0:
            pe.wait_ge(self.masked, b * STEPS + STEPS)
        j = begin + when * count // 2
        self.pe_conv(FILL_BANKS[n], n, range(j, j + count // 2))

    def act_fill(self, act, c, g, to):
        if g in TAKE:
            n = TAKE.index(g)
            self.act_conv(act, c, n, to, FILL_BANKS[n])

    def dve_fill(self, dve, c, g, to):
        if g in TAKE:
            n = TAKE.index(g)
            self.dve_conv(dve, c, n, to, FILL_BANKS[n])


    def pe_wo(self, pe, b, n):
        pe.wait_ge(self.oT_ready, b * STEPS + 2 * (n + 1))
        tok = slice(n * P, (n + 1) * P)
        for c in range(HP):
            last = self.nc.tensor.matmul(self.banks[0][:, tok], self.wo_s[:, c, :], self.oT[:, c, tok],
                                         start=c == 0, stop=c == HP - 1)
        if n >= TPB - 2:
            last.then_inc(self.wo_done, 1)

    def pe_out(self, pe, b):
        def out(n):
            self.nc.tensor.matmul(self.banks[OUT_BANKS[n]][:], self.att[:, n * P:(n + 1) * P], self.pj_s[:],
                                  start=True, stop=True).then_inc(self.out_done, 1)

        pe.wait_ge(self.att_ready, b * 2 + 1)
        for n in range(TPB - 1):
            out(n)
        self.pe_wo(pe, b, TPB - 1)
        pe.wait_ge(self.att_ready, b * 2 + 2)
        out(TPB - 1)

    def act_out(self, act, b, part):
        act.wait_ge(self.wo_done, b * 2 + (part + 1))
        tok = slice(0, (TPB - 1) * P) if part == 0 else slice((TPB - 1) * P, TPB * P)
        self.nc.scalar.activation(self.att[:, tok], self.banks[0][:, tok], ACT.Identity, bias=self.bos)\
            .then_inc(self.att_ready, 1)


def front(nc, t, banks, x, gate, weights, experts, xn_d, xg_d, base_d):
    ctx = ExitStack()
    with ctx:
        def sb(name, shape, dt=F32):
            return ctx.enter_context(nc.sbuf_tensor(name, shape, dt))

        def sem(name):
            return ctx.enter_context(nc.semaphore(name))

        ident, slot, gates = t["ident"], t["slot"], t["gates"]
        tile_waits, tile_slots, released = t["tile_waits"], t["tile_slots"], t["released"]
        RING, RING2 = (6, 4, 3), (6, 7)
        CONV_BANKS = (7, 0, 5)
        front_at = aligned(nc.sbuf_base)
        xb = sb("xb", [P, NT, DM])
        rT = nc.alloc_sbuf_tensor_at("rT", [P, 3, DC, P], F32, offset=t["shared_at"])
        lT = nc.alloc_sbuf_tensor_at("lT", [NE, 2, LEN], F32, offset=t["shared_at"] + 4 * 3 * DM)
        gTf = sb("gTf", [P, DC, NE])
        stats, mv = sb("stats", [P, NT, 6]), sb("mv", [P, NT, 2])
        var, std, rstd, tmp = (sb(n, [P, NT]) for n in ("var", "std", "rstd", "tmp"))
        less, ones = sb("less", [P, P]), sb("ones", [P, P])
        lane, eno = sb("lane", [P, 1]), sb("eno", [P, NE])
        dumps, tails = sb("dumps", [P, NPAD]), sb("tails", [P, SPARE])
        tileno = sb("tileno", [1, EXPERT_TILES])
        prob, work, first, second, before, upto = (sb(n, [P, NT, NE]) for n in ("prob", "work", "first", "second", "before", "upto"))
        col = sb("col", [P, 4, NT])
        need, needi = sb("need", [P, 6, NE]), sb("needi", [P, NE], I32)
        padf, pads = sb("padf", [P, 3, NPAD]), sb("pads", [P, NPAD], I32)
        cmp = sb("cmp", [1, EXPERT_TILES, NE - 1])
        texp, texi = sb("texp", [1, EXPERT_TILES]), sb("texi", [1, EXPERT_TILES], I32)
        assert nc.sbuf_base >= front_at + 4 * PIECE_AT[FIRST], "the first expert's weights come over buffers in use"
        A = Attention(nc, ctx, t, banks, weights, "f_", first=True)
        zrow = nc.alloc_sbuf_tensor_at("zrow", [P, DM], F32, offset=A.pjb_at)
        base = nc.alloc_sbuf_tensor_at("base", [P, 2, DM], F32, offset=A.vh_at)

        logits, rank, total, LT_BANKS = banks[5], banks[6], banks[7], banks[1:3]

        x_loaded = [sem(f"x_loaded{b}") for b in range(BATCH)]
        gate_loaded, consts, dve_chain = sem("gate_loaded"), sem("consts"), sem("dve_chain")
        var_ready, std_ready, xn_ready, xn_stored = sem("var_ready"), sem("std_ready"), sem("xn_ready"), sem("xn_stored")
        front_xT, copied = sem("front_xT"), sem("copied")
        lT_done, lT_copied = sem("lT_done"), sem("lT_copied")
        logits_done, shifted, exp_done = sem("logits_done"), sem("shifted"), sem("exp_done")
        picked_ready, rank_done, routed = sem("picked_ready"), sem("rank_done"), sem("routed")
        sent, padded = sem("sent"), sem("padded")
        base_stored = t["base_stored"]

        block = ctx.enter_context(nc.Block())

        @block.sync
        def _(sp):
            def load(b):
                sp.dma_start(xb[:, TPB * b:TPB * (b + 1), :],
                             x[b * LEN:(b + 1) * LEN, :].rearrange("(j p) d -> p j d", p=P)).then_inc(x_loaded[b], 16)

            load(0)
            sp.dma_start(gTf[:], gate).then_inc(gate_loaded, 16)
            for b in range(1, BATCH):
                load(b)
            A.load_pieces(sp, range(WSPLITS))
            A.load_small(sp)
            for b in range(2, BATCH):
                sp.wait_ge(xn_ready, TPB * (b + 1))
                sp.dma_start(xn_d[b * LEN:(b + 1) * LEN, :].rearrange("(j p) d -> p j d", p=P),
                             xb[:, TPB * b:TPB * (b + 1), :]).then_inc(xn_stored, 16)
            sp.wait_ge(xn_stored, 16 * (BATCH - 2))
            sp.wait_ge(A.xs_T, 2 * TPB)
            sp.wait_ge(routed, 1)
            sp.wait_ge(padded, 16 * NPAD)
            A.load_pjb(sp)
            sp.wait_ge(sent, 16 * TOPK * NT)
            for i in range(FIRST):
                at = slice(PIECE_AT[i], PIECE_AT[i + 1])
                sp.dma_start(t["first_raw"][:, at], experts[0, :, at]).then_inc(t["first_loaded"], 16)
            for n in range(TPB):
                sp.wait_ge(A.out_ready, n + 1)
                sp.dma_start(base_d[n * P:(n + 1) * P, :], base[:, n % 2, :]).then_inc(base_stored[n % 2], 16)

        @block.gpsimd
        def _(pool):
            g = nc.gpsimd
            g.memset(ident[:], 0.0).then_inc(consts, 1)
            g.memset(less[:], 0.0).then_inc(consts, 1)
            g.memset(ones[:], 1.0).then_inc(consts, 1)
            g.memset(zrow[:], 0.0).then_inc(consts, 1)
            pool.wait_ge(consts, 2)
            g.affine_select(out=ident[:], in_=ident[:], compare_op=ALU.not_equal, fill=1.0, base=0,
                            pattern=[[-1, P]], channel_multiplier=1).then_inc(consts, 1)
            g.affine_select(out=less[:], in_=less[:], compare_op=ALU.is_ge, fill=1.0, base=0,
                            pattern=[[-1, P]], channel_multiplier=1).then_inc(consts, 1)
            ok = dict(allow_small_or_imprecise_dtypes=True)
            g.iota(lane[:], [[1, 1]], base=0, channel_multiplier=1, **ok).then_inc(consts, 1)
            g.iota(eno[:], [[1, NE]], base=-NE, channel_multiplier=0, **ok).then_inc(consts, 1)
            g.iota(dumps[:], [[P, NPAD]], base=DUMP, channel_multiplier=1, **ok).then_inc(consts, 1)
            g.iota(tails[:], [[P, SPARE]], base=0, channel_multiplier=1, **ok).then_inc(consts, 1)
            g.iota(tileno[:], [[1, EXPERT_TILES]], base=0, channel_multiplier=0, **ok).then_inc(consts, 1)
            A.constants(pool)
            for n in range(WSPLITS):
                A.lo_piece(g, n)
            pool.wait_ge(routed, 1)
            for j in range(NPAD):
                g.indirect_dma_start(xg_d[:, :], bass.IndirectOffsetOnAxis(ap=pads[:, j:j + 1].bitcast(U32), axis=0),
                                     zrow[:], None).then_inc(padded, 16)
            for i in range(NT):
                for k in range(TOPK):
                    g.indirect_dma_start(xg_d[:, :],
                                         bass.IndirectOffsetOnAxis(ap=slot[:, k, i:i + 1].bitcast(U32), axis=0),
                                         xb[:, i, :], None).then_inc(sent, 16)
            pool.wait_ge(padded, 16 * NPAD)
            pool.wait_ge(sent, 16 * TOPK * NT)

        @block.tensor
        def _(pe):
            mm = nc.tensor.matmul
            pe.wait_ge(consts, 6)

            def transpose_rows(i):
                pe.wait_ge(xn_ready, i + 1)
                if i < TPB:
                    if i == 3:
                        pe.wait_ge(copied, 1)
                    A.pe_transpose_x(pe, i, i, xb[:, i, :], RING)
                    return
                pe.wait_ge(copied, i - 2)
                if i < TPB + 3:
                    pe.wait_ge(A.x_hi, i - 2)
                    pe.wait_ge(A.x_lo, i - 2)
                bank = banks[RING[i % 3]]
                for c in range(DC):
                    last = nc.tensor.transpose(bank[:, c * P:(c + 1) * P], xb[:, i, c * P:(c + 1) * P], ident[:])
                last.then_inc(front_xT, 1)

            def router(i):
                if i == 0:
                    pe.wait_ge(gate_loaded, 16)
                pe.wait_ge(copied, i + 1)
                for c in range(DC):
                    last = mm(LT_BANKS[i // TPB % 2][0:NE, i % TPB * P:(i % TPB + 1) * P], gTf[:, c, :],
                              rT[:, i % 3, c, :], start=c == 0, stop=c == DC - 1)
                last.then_inc(lT_done, 1)

            def transpose_logits(b):
                pe.wait_ge(lT_copied, b + 1)
                for n in range(TPB):
                    i = b * TPB + n
                    last = nc.tensor.transpose(logits[:, i * NE:(i + 1) * NE], lT[:, b % 2, n * P:(n + 1) * P],
                                               ident[0:NE, 0:NE])
                last.then_inc(logits_done, 1)

            for i in range(NT + 2):
                if i < NT:
                    transpose_rows(i)
                if i >= 2:
                    router(i - 2)
                    if (i - 2) % TPB == 0 and i - 2:
                        transpose_logits((i - 2) // TPB - 1)
            transpose_logits(BATCH - 1)
            pe.wait_ge(A.zeroed, 4)
            pe.wait_ge(A.conv_pieces_lo, TAPS)
            for n in range(PROJ - 1):
                A.pe_conv(CONV_BANKS[n], n, range(TAPS * DC))
            pe.wait_ge(picked_ready, 1)
            mm(rank[:, 0:NT * NE], less[:], work[:], start=True, stop=False)
            mm(rank[:, NE:NT * NE], ones[:], upto[:, 0:NT - 1, :], start=False, stop=True)
            mm(total[:, 0:NE], ones[:], upto[:, NT - 1, :], start=True, stop=True).then_inc(rank_done, 1)
            A.pe_conv(CONV_BANKS[PROJ - 1], PROJ - 1, range(TAPS * DC))
            pe.wait_ge(A.proj_pieces_lo, PROJ)
            pe.wait_ge(A.small_loaded, 16 * A.small)
            pe.wait_ge(A.conv_hi, PROJ - 1)
            pe.wait_ge(A.conv_lo, PROJ - 1)
            A.pe_proj(pe, 0, lambda n: A.pe_transpose_x(pe, TPB + n, n, xb[:, TPB + n, :], RING2))
            A.pe_steps(pe, 0, lambda g, when: A.pe_fill(pe, 0, 1, g, when))
            A.pe_out(pe, 0)

        @block.scalar
        def _(a):
            s = nc.scalar

            def deviations(b):
                a.wait_ge(var_ready, b + 1)
                n = slice(b * TPB, (b + 1) * TPB)
                s.activation(std[:, n], var[:, n], ACT.Sqrt).then_inc(std_ready, 1)

            def hi(i):
                if i < TPB:
                    A.act_hi_x(a, i, i, RING)
                else:
                    a.wait_ge(front_xT, i - TPB + 1)
                if i >= 3:
                    a.wait_ge(lT_done, i - 2)
                s.activation(rT[:, i % 3, :, :], banks[RING[i % 3]][:].rearrange("p (c t) -> p c t", c=DC), ACT.Copy)\
                    .then_inc(copied, 1)

            def copy_lT(b):
                a.wait_ge(lT_done, (b + 1) * TPB)
                s.activation(lT[:, b % 2, :], LT_BANKS[b % 2][0:NE, :], ACT.Copy).then_inc(lT_copied, 1)

            deviations(0)
            for i in range(NT):
                if i % TPB == 2 and i // TPB + 1 < BATCH:
                    deviations(i // TPB + 1)
                hi(i)
                if 2 <= i < 2 + WSPLITS:
                    A.hi_piece(nc.scalar, i - 2)
                if i % TPB == 1 and i > 1:
                    copy_lT(i // TPB - 1)
            copy_lT(BATCH - 1)
            a.wait_ge(A.small_loaded, 16 * A.small)
            for n in range(PROJ):
                if n == 0:
                    a.wait_ge(shifted, 1)
                    s.activation(prob[:], work[:], ACT.Exp).then_inc(exp_done, 1)
                A.act_conv(a, 0, n, (A.qkvh, A.qkvl), CONV_BANKS[n])
            a.wait_ge(A.bias_scaled, 1)
            A.act_proj(a, 0, lambda n: A.act_hi_x(a, TPB + n, n, RING2))
            A.act_steps(a, 0, lambda g: A.act_fill(a, 1, g, (t["qkvh"], t["qkvl"])))

        @block.vector
        def _(d):
            v = nc.vector
            link = Chain(d, dve_chain)

            def over_experts(ap):
                return ap.unsqueeze(2).to_broadcast([P, NT, NE])

            def over_tiles(ap):
                return ap.unsqueeze(1).to_broadcast([P, NT, NE])

            def norm(b, part):
                tiles = range(TPB * b, TPB * (b + 1))
                n = slice(b * TPB, (b + 1) * TPB)
                if part == 0:
                    d.wait_ge(x_loaded[b], 16)
                    for i in tiles:
                        last = v.bn_stats(stats[:, i, :], xb[:, i, :])
                    link(last)
                elif part == 1:
                    for i in tiles:
                        last = v.bn_aggr(mv[:, i, :], stats[:, i, :])
                    link(last)
                    link(v.tensor_scalar(var[:, n], mv[:, n, 1], EPS, None, ALU.add))
                    v.tensor_scalar(tmp[:, n], var[:, n], 0.5, None, ALU.mult).then_inc(var_ready, 1)
                elif part == 2:
                    d.wait_ge(std_ready, b + 1)
                    link(v.reciprocal(rstd[:, n], std[:, n]))
                    link(v.tensor_tensor(tmp[:, n], tmp[:, n], rstd[:, n], ALU.mult))
                    link(v.tensor_tensor(tmp[:, n], tmp[:, n], rstd[:, n], ALU.mult))
                    link(v.tensor_scalar(tmp[:, n], tmp[:, n], -1.0, 1.5, ALU.mult, ALU.add))
                    link(v.tensor_tensor(rstd[:, n], rstd[:, n], tmp[:, n], ALU.mult))
                else:
                    for i in tiles:
                        v.tensor_scalar(xb[:, i, :], xb[:, i, :], mv[:, i, 0:1], rstd[:, i:i + 1], ALU.subtract, ALU.mult)\
                            .then_inc(xn_ready, 1)

            norm(0, 0)
            norm(0, 1)
            norm(1, 0)
            norm(0, 2)
            norm(0, 3)
            for i in range(TPB):
                if i:
                    norm(1, i)
                d.wait_ge(copied, i + 1)
                A.dve_lo_x(d, i, i, RING)
            for b in range(2, BATCH):
                for part in range(4):
                    norm(b, part)
            d.wait_ge(A.small_loaded, 16 * A.small)
            v.tensor_scalar(A.bqs, A.bqs, SCALE, None, ALU.mult).then_inc(A.bias_scaled, 1)
            d.wait_ge(logits_done, BATCH)
            lg = logits[:, 0:NT * NE].rearrange("p (i e) -> p i e", e=NE)
            link(v.tensor_reduce(col[:, 0, :], lg, AX, ALU.max, negate=True))
            v.tensor_tensor(work[:], lg, over_experts(col[:, 0, :]), ALU.add).then_inc(shifted, 1)
            d.wait_ge(exp_done, 1)
            link(v.tensor_reduce(col[:, 1, :], prob[:], AX, ALU.add))
            link(v.reciprocal(col[:, 2, :], col[:, 1, :]))
            link(v.tensor_tensor(prob[:], prob[:], over_experts(col[:, 2, :]), ALU.mult))

            def pick(chosen, top):
                link(v.tensor_reduce(top, prob[:], AX, ALU.max))
                link(v.tensor_tensor(work[:], prob[:], over_experts(top), ALU.is_equal))
                link(v.tensor_tensor(work[:], work[:], over_tiles(eno[:]), ALU.mult))
                link(v.tensor_reduce(col[:, 2, :], work[:], AX, ALU.min))
                link(v.tensor_tensor(chosen[:], over_tiles(eno[:]), over_experts(col[:, 2, :]), ALU.is_equal))

            d.wait_ge(consts, 11)
            pick(first, col[:, 0, :])
            link(v.scalar_tensor_tensor(prob[:], first[:], -2.0, prob[:], ALU.mult, ALU.add))
            pick(second, col[:, 1, :])
            A.dve_conv(d, 0, 0, (A.qkvh, A.qkvl), CONV_BANKS[0])
            link(v.tensor_tensor(col[:, 2, :], col[:, 0, :], col[:, 1, :], ALU.add))
            link(v.reciprocal(col[:, 3, :], col[:, 2, :]))
            v.tensor_tensor(gates[:, 0, :], col[:, 0, :], col[:, 3, :], ALU.mult)
            v.tensor_tensor(gates[:, 1, :], col[:, 1, :], col[:, 3, :], ALU.mult)
            link(v.tensor_tensor(work[:], first[:], second[:], ALU.add))
            step, have = 1, work
            for there in (before, upto, before, upto):
                v.tensor_copy(there[:, 0:step, :], have[:, 0:step, :])
                last = v.tensor_tensor(there[:, step:, :], have[:, step:, :], have[:, 0:NT - step, :], ALU.add)
                step, have = 2 * step, there
                if step < NT:
                    link(last)
            last.then_inc(picked_ready, 1)
            A.dve_conv(d, 0, 1, (A.qkvh, A.qkvl), CONV_BANKS[1])
            d.wait_ge(rank_done, 1)
            rows, tiles, ends, starts, cond, spare = (need[:, i, :] for i in range(6))
            link(v.tensor_copy(rows, total[:, 0:NE]))
            link(v.tensor_scalar(needi[:], rows, float(P - 1), None, ALU.add))
            link(v.tensor_single_scalar(needi[:], needi[:], P.bit_length() - 1, op=ALU.arith_shift_right))
            link(v.tensor_scalar(tiles, needi[:], 1.0, None, ALU.max))
            have = tiles
            for step, there in ((1, ends), (2, cond), (4, ends)):
                v.tensor_copy(there[:, 0:step], have[:, 0:step])
                link(v.tensor_tensor(there[:, step:], have[:, step:], have[:, 0:NE - step], ALU.add))
                have = there
            link(v.tensor_tensor(starts, ends, tiles, ALU.subtract))
            link(v.tensor_scalar(starts, starts, float(P), None, ALU.mult))
            link(v.tensor_tensor(work[:], rank[:, 0:NT * NE].rearrange("p (i e) -> p i e", e=NE), over_tiles(starts), ALU.add))
            link(v.tensor_tensor(first[:], first[:], work[:], ALU.mult))
            link(v.tensor_tensor(second[:], second[:], work[:], ALU.mult))
            v.tensor_reduce(col[:, 0, :], first[:], AX, ALU.add)
            link(v.tensor_reduce(col[:, 1, :], second[:], AX, ALU.add))
            v.tensor_copy(slot[:, 0, :], col[:, 0, :])
            v.tensor_copy(slot[:, 1, :], col[:, 1, :])
            want, take, use = (padf[:, i, :] for i in range(3))
            v.tensor_tensor(want[:, 0:NE], starts, rows, ALU.add)
            link(v.scalar_tensor_tensor(spare, tiles, float(P), rows, ALU.mult, ALU.subtract))
            link(v.tensor_scalar(want[:, 0:NE], want[:, 0:NE], lane[:, 0:1], None, ALU.add))
            v.tensor_scalar(take[:, 0:NE], spare, lane[:, 0:1], None, ALU.is_gt)
            link(v.tensor_scalar(cond[:, 0:1], ends[:, NE - 1:NE], float(P), None, ALU.mult))
            link(v.tensor_scalar(want[:, NE:], tails[:], cond[:, 0:1], None, ALU.add))
            link(v.tensor_scalar(take[:, NE:], want[:, NE:], float(SLOTS), None, ALU.is_lt))
            link(v.tensor_tensor(use, want, dumps[:], ALU.subtract))
            link(v.tensor_tensor(use, use, take, ALU.mult))
            link(v.tensor_tensor(use, use, dumps[:], ALU.add))
            v.tensor_copy(pads[:], use)
            link(v.tensor_tensor(cmp[:], ends[0:1, 0:NE - 1].unsqueeze(1).to_broadcast([1, EXPERT_TILES, NE - 1]),
                                 tileno[:].unsqueeze(2).to_broadcast([1, EXPERT_TILES, NE - 1]), ALU.is_le))
            link(v.tensor_reduce(texp[:], cmp[:], AX, ALU.add))
            v.tensor_scalar(tile_waits[:], texp[:], float(NPC), None, ALU.mult)
            link(v.tensor_scalar(texi[:], texp[:], 1.0, None, ALU.add))
            link(v.tensor_single_scalar(texi[:], texi[:], 1, op=ALU.bitwise_and))
            v.tensor_scalar(tile_slots[:], texi[:], float(WCOLS), None, ALU.mult)
            link(v.memset(released[:], 0))
            v.tensor_copy(released[0:1, 2:], ends[0:1, 0:NE - 1]).then_inc(routed, 1)

            A.dve_conv(d, 0, 2, (A.qkvh, A.qkvl), CONV_BANKS[2])
            d.wait_ge(A.mask_ready, 2)
            A.dve_proj(d, 0, lambda n: A.dve_lo_x(d, TPB + n, n, RING2))
            A.dve_steps(d, 0, lambda g: A.dve_fill(d, 1, g, (t["qkvh"], t["qkvl"])))
            d.wait_ge(A.pjb_loaded, 16)
            for n in range(TPB):
                d.wait_ge(A.out_done, n + 1)
                if n >= 2:
                    d.wait_ge(base_stored[n % 2], n // 2 * 16)
                v.tensor_tensor(base[:, n % 2, :], banks[OUT_BANKS[n]][:], A.pjb[:], ALU.add).then_inc(A.out_ready, 1)


def experts_block(nc, t, banks, experts, attention_weights, xg_d, y_d):
    ctx = ExitStack()
    with ctx:
        def sb(name, shape, dt=F32):
            return ctx.enter_context(nc.sbuf_tensor(name, shape, dt))

        def sem(name):
            return ctx.enter_context(nc.semaphore(name))

        ident, tile_waits, tile_slots, released = t["ident"], t["tile_waits"], t["tile_slots"], t["released"]
        raw = t["shared"]
        whi, wlo = sb("whi", [P, 2 * WCOLS], F32R), sb("wlo", [P, 2 * WCOLS], F32R)
        xrow = sb("xrow", [P, DM])
        xTh, xTl = sb("xTh", [P, DC, P], F32R), sb("xTl", [P, DC, P], F32R)
        silu, act = sb("silu", [P, FF]), sb("act", [P, AC * P])
        aTh, aTl = sb("aTh", [P, AC, P], F32R), sb("aTl", [P, AC - 1, P], F32R)
        ysb = sb("ysb", [P, DM])

        hA1, hA3, hB1, hB3, tA, tB, tX, yP = banks

        pool_turns, sp_turns = sem("pool_turns"), sem("sp_turns")
        raw_loaded = [sem("raw_loaded0"), sem("raw_loaded1")]
        hi_split, lo_split = sem("hi_split"), sem("lo_split")
        row_loaded = sem("row_loaded")
        xT_done, xT_hi, xT_lo = sem("xT_done"), sem("xT_hi"), sem("xT_lo")
        hA_done, hB_done = sem("hA_done"), sem("hB_done")
        siluA, siluB, actA, actB = sem("siluA"), sem("siluB"), sem("actA"), sem("actB")
        aT_done, aT_hi, aT_lo = sem("aT_done"), sem("aT_hi"), sem("aT_lo")
        y_done, y_copied, y_stored = sem("y_done"), sem("y_copied"), t["y_stored"]

        block = ctx.enter_context(nc.Block())

        LAST_PIECES = [(DC * NO, *(t["cw"][:, k, i * DC:(i + 1) * DC, :].rearrange("p c o -> p (c o)") for k in range(2)))
                       for i in range(TAPS)] + [(H * DH, t["pw"][:, i, 0, :], t["pw"][:, i, 1, :]) for i in range(PROJ)]

        def source(i, half, rows):
            if half is None:
                return t["first_raw"][rows, PIECE_AT[i]:PIECE_AT[i + 1]]
            return raw[rows, half, 0:PIECES[i][0]]

        def hi_part(eng, i, half, slot_at):
            n, parts = PIECES[i]
            dst = whi[0:parts, bass.ds(slot_at + PIECE_AT[i], n)]
            src = source(i, half, slice(0, parts))
            return eng.activation(dst, src, ACT.Copy) if eng is nc.scalar else eng.tensor_copy(dst, src)

        def lo_part(eng, i, half, slot_at):
            n, parts = PIECES[i]
            rows = slice(0, parts) if i < NPC - 1 else slice(FLAST, 2 * FLAST)
            at = bass.ds(slot_at + PIECE_AT[i], n)
            return eng.tensor_tensor((wlo if i < NPC - 1 else whi)[rows, at], source(i, half, rows),
                                     whi[rows, at].bitcast(F32), ALU.subtract)

        @block.sync
        def _(sp):
            def load(e, i, half, n):
                w, parts = PIECES[i]
                if n is not None:
                    sp.wait_ge(lo_split, n)
                    if not isinstance(n, int):
                        sp.sem_inc(sp_turns, 1)
                src = experts[bass.ds(e, 1), 0:parts, PIECE_AT[i]:PIECE_AT[i] + w].rearrange("a p w -> (a p) w")
                sp.dma_start(raw[0:parts, half, 0:w], src).then_inc(raw_loaded[half], 16)

            for n in range(FIRST, 2 * NPC):
                load(n // NPC, n % NPC, n % 2, n - 1 if n >= FIRST + 2 else None)
            with sp.Fori(1, NE // 2) as k:
                for i in range(2 * NPC):
                    load(k * 2 + i // NPC, i % NPC, i % 2, k * (2 * NPC) + (i - 1))
            for i in range(WSPLITS):
                n = NE * NPC + i
                sp.wait_ge(lo_split, n - 1)
                dst = raw[:, n % 2, 0:LAST_PIECES[i][0]]
                if i < TAPS:
                    src = attention_weights[0][i].rearrange("(c p) o -> p c o", p=P)
                    dst = dst.rearrange("p (c o) -> p c o", o=NO)
                else:
                    src = attention_weights[1 + i - TAPS].rearrange("d h e -> d (h e)")
                sp.dma_start(dst, src).then_inc(raw_loaded[n % 2], 16)

        @block.gpsimd
        def _(pool):
            g = nc.gpsimd

            def after(semaphore, count):
                pool.wait_ge(semaphore, count)
                pool.sem_inc(pool_turns, 1)

            def split(i, half, slot_at, loads, n):
                if i == 0:
                    after(lo_split, n)
                after(raw_loaded[half], loads)
                hi_part(g, i, half, slot_at).then_inc(hi_split, 1)
                pool.wait_ge(hi_split, n + 1)
                lo_part(g, i, half, slot_at).then_inc(lo_split, 1)

            pool.wait_ge(lo_split, NPC)
            for i in range(NPC):
                n = NPC + i
                split(i, n % 2, 0, 16 * (n // 2 + 1 - FIRST // 2), n)
            with pool.Fori(1, NE // 2) as k:
                for e in range(2):
                    r = pool.value_load(released[0:1, bass.ds(k * 2 + e, 1)], min_val=1, max_val=EXPERT_TILES)
                    after(y_done, r)
                    for i in range(NPC):
                        n = e * NPC + i
                        split(i, n % 2, (1 - e) * WCOLS, (k * NPC + (n // 2 + 1 - FIRST // 2)) * 16, k * (2 * NPC) + n)
            r = pool.value_load(released[0:1, NE:NE + 1], min_val=1, max_val=EXPERT_TILES)
            after(y_done, r)
            after(lo_split, NE * NPC)
            for i, (w, hi, lo) in enumerate(LAST_PIECES):
                n = NE * NPC + i
                pool.wait_ge(raw_loaded[n % 2], 16 * (n // 2 + 1 - FIRST // 2))
                g.tensor_copy(hi, raw[:, n % 2, 0:w]).then_inc(hi_split, 1)
                pool.wait_ge(hi_split, n + 1)
                g.tensor_tensor(lo, raw[:, n % 2, 0:w], hi.bitcast(F32), ALU.subtract).then_inc(lo_split, 1)
            pool.wait_ge(lo_split, NE * NPC + WSPLITS)

        @block.tensor
        def _(pe):
            mm = nc.tensor.matmul
            def transpose_rows(n):
                pe.wait_ge(row_loaded, n * 16)
                for c in range(DC):
                    last = nc.tensor.transpose(tX[:, c * P:(c + 1) * P], xrow[:, c * P:(c + 1) * P], ident[:])
                last.then_inc(xT_done, 1)

            def up(n, part, base, at):
                f = (FA, FB)[part]
                for w in range(2):
                    pe.wait_ge(lo_split, base + (2 * part + w + 1))
                    bank = ((hA1, hA3), (hB1, hB3))[part][w]
                    for c in range(DC):
                        o = PIECE_AT[2 * part + w] + c * f
                        last = three_passes(nc, bank[:, 0:f], xTh[:, c, :], xTl[:, c, :],
                                            whi[:, bass.ds(at + o, f)], wlo[:, bass.ds(at + o, f)],
                                            c == 0, c == DC - 1)
                last.then_inc((hA_done, hB_done)[part], 1)

            def transpose_act(n):
                pe.wait_ge(actA, n)
                pe.wait_ge(actB, n)
                for c in range(AC):
                    bank, o = (tA, c * P) if c < 3 else (tB, (c - 3) * P)
                    last = nc.tensor.transpose(bank[:, o:o + P], act[:, c * P:(c + 1) * P], ident[:])
                last.then_inc(aT_done, 1)

            def down(n, base, at):
                pe.wait_ge(lo_split, base + NPC)
                pe.wait_ge(aT_hi, n)
                pe.wait_ge(aT_lo, n)
                if not isinstance(n, int) or n > 1:
                    pe.wait_ge(y_copied, n - 1)
                for c in range(AC - 1):
                    w = bass.ds(at + (PIECE_AT[4] + c * DM), DM)
                    three_passes(nc, yP[:, :], aTh[:, c, :], aTl[:, c, :], whi[:, w], wlo[:, w], c == 0, False)
                last = mm(yP[:, :], aTh[0:3 * FLAST, AC - 1, :], whi[0:3 * FLAST, bass.ds(at + PIECE_AT[NPC - 1], DM)],
                          start=False, stop=True)
                last.then_inc(y_done, 1)

            def place(n):
                base = pe.value_load(tile_waits[0:1, bass.ds(n, 1)], min_val=0, max_val=(NE - 1) * NPC)
                at = pe.value_load(tile_slots[0:1, bass.ds(n, 1)], min_val=0, max_val=WCOLS)
                return base, at

            def tile(n, before=True, after=True):
                base, at = place(n)
                pe.wait_ge(xT_hi, n + 1)
                pe.wait_ge(xT_lo, n + 1)
                up(n, 0, base, at)
                if before:
                    transpose_act(n)
                up(n, 1, base, at)
                if after:
                    transpose_rows(n + 2)
                if before:
                    down(n, *place(n - 1))

            transpose_rows(1)
            tile(0, before=False)
            tile(1)
            with pe.Fori(2, EXPERT_TILES - 1) as n:
                tile(n)
            tile(EXPERT_TILES - 1, after=False)
            transpose_act(EXPERT_TILES)
            down(EXPERT_TILES, *place(EXPERT_TILES - 1))

        @block.scalar
        def _(a):
            s = nc.scalar
            def load_rows(n):
                a.dma_start(xrow[:], xg_d[bass.ds(n * P, P), :]).then_inc(row_loaded, 16)

            def hi_xT(n):
                a.wait_ge(xT_done, n)
                s.activation(xTh[:], tX[:].rearrange("p (c t) -> p c t", c=DC), ACT.Copy).then_inc(xT_hi, 1)

            def hi_aT(n):
                a.wait_ge(aT_done, n)
                s.activation(aTh[:, 0:3, :], tA[:, 0:3 * P].rearrange("p (c t) -> p c t", c=3), ACT.Copy)
                s.activation(aTh[:, 3:AC, :], tB[:].rearrange("p (c t) -> p c t", c=4), ACT.Copy).then_inc(aT_hi, 1)

            def gate_part(n, part):
                a.wait_ge((hA_done, hB_done)[part], n + 1)
                if not isinstance(n, int) or n:
                    a.wait_ge((actA, actB)[part], n)
                f0, f = (0, FA)[part], (FA, FB)[part]
                s.activation(silu[:, f0:f0 + f], (hA1, hB1)[part][:, 0:f], ACT.Silu).then_inc((siluA, siluB)[part], 1)

            def store_y(n):
                a.wait_ge(y_done, n)
                if not isinstance(n, int) or n > 1:
                    a.wait_ge(y_stored, (n - 1) * 16)
                s.activation(ysb[:], yP[:], ACT.Copy).then_inc(y_copied, 1)
                a.wait_ge(y_copied, n)
                a.dma_start(y_d[bass.ds((n - 1) * P, P), :], ysb[:]).then_inc(y_stored, 16)

            def tile(n, before=True, after=True, fetch=True):
                gate_part(n, 0)
                if before:
                    hi_aT(n)
                gate_part(n, 1)
                if after:
                    hi_xT(n + 2)
                    if fetch:
                        load_rows(n + 2)
                if before:
                    store_y(n)

            load_rows(0)
            a.wait_ge(t["first_loaded"], 16 * FIRST)
            for i in range(FIRST):
                if i == 2:
                    hi_xT(1)
                    load_rows(1)
                hi_part(s, i, None, WCOLS).then_inc(hi_split, 1)
            a.wait_ge(raw_loaded[FIRST % 2], 16)
            hi_part(s, FIRST, FIRST % 2, WCOLS).then_inc(hi_split, 1)
            tile(0, before=False)
            tile(1)
            with a.Fori(2, EXPERT_TILES - 2) as n:
                tile(n)
            tile(EXPERT_TILES - 2, fetch=False)
            tile(EXPERT_TILES - 1, after=False)
            hi_aT(EXPERT_TILES)
            store_y(EXPERT_TILES)

        @block.vector
        def _(d):
            v = nc.vector
            def up_part(n, part):
                d.wait_ge((siluA, siluB)[part], n + 1)
                d.wait_ge((hA_done, hB_done)[part], n + 1)
                if not isinstance(n, int) or n:
                    d.wait_ge(aT_done, n)
                f0, f = (0, FA)[part], (FA, FB)[part]
                if part:
                    f -= FLAST
                    four = [P, P // FLAST, FLAST]
                    v.tensor_tensor(act[:, FF - FLAST:].rearrange("p (r c) -> p r c", c=FLAST),
                                    silu[:, FF - FLAST:FF].unsqueeze(1).to_broadcast(four),
                                    hB3[:, f:f + FLAST].unsqueeze(1).to_broadcast(four), ALU.mult)
                v.tensor_tensor(act[:, f0:f0 + f], silu[:, f0:f0 + f], (hA3, hB3)[part][:, 0:f], ALU.mult)\
                    .then_inc((actA, actB)[part], 1)

            def lo_xT(n):
                d.wait_ge(xT_hi, n)
                v.tensor_tensor(xTl[:], tX[:].rearrange("p (c t) -> p c t", c=DC), xTh[:].bitcast(F32),
                                ALU.subtract).then_inc(xT_lo, 1)

            def lo_aT(n):
                d.wait_ge(aT_hi, n)
                v.tensor_tensor(aTl[:, 0:3, :], tA[:, 0:3 * P].rearrange("p (c t) -> p c t", c=3),
                                aTh[:, 0:3, :].bitcast(F32), ALU.subtract)
                v.tensor_tensor(aTl[:, 3:6, :], tB[:, 0:3 * P].rearrange("p (c t) -> p c t", c=3),
                                aTh[:, 3:6, :].bitcast(F32), ALU.subtract)
                last = aTh[2 * FLAST:3 * FLAST, AC - 1, :]
                v.tensor_tensor(last, tB[2 * FLAST:3 * FLAST, 3 * P:4 * P], last.bitcast(F32),
                                ALU.subtract).then_inc(aT_lo, 1)

            def tile(n, before=True, after=True):
                up_part(n, 0)
                if before:
                    lo_aT(n)
                up_part(n, 1)
                if after:
                    lo_xT(n + 2)

            for i in range(NPC):
                if i == 2:
                    lo_xT(1)
                    for stored in t["base_stored"]:
                        d.wait_ge(stored, TPB // 2 * 16)
                d.wait_ge(hi_split, i + 1)
                lo_part(v, i, None if i < FIRST else i % 2, WCOLS).then_inc(lo_split, 1)
            tile(0, before=False)
            with d.Fori(1, EXPERT_TILES - 1) as n:
                tile(n)
            tile(EXPERT_TILES - 1, after=False)
            lo_aT(EXPERT_TILES)


def back(nc, t, banks, x, weights, xn_d, y_d, base_d, out):
    ctx = ExitStack()
    with ctx:
        def sb(name, shape, dt=F32):
            return ctx.enter_context(nc.sbuf_tensor(name, shape, dt))

        def sem(name):
            return ctx.enter_context(nc.semaphore(name))

        slot, gates = t["slot"], t["gates"]
        A = Attention(nc, ctx, t, banks, weights, "b_", first=False)
        RING = (6, 7)
        NB = BATCH - 1
        ALSO = TPB // (NB - 1)
        xs = sb("xs", [P, 2, DM])
        res = sb("res", [P, TPB, DM])
        also, alsob = sb("also", [P, DM]), sb("alsob", [P, DM])
        ye = sb("ye", [P, TOPK, DM])
        idx, gate = sb("idx", [P, TOPK], I32), sb("gate", [P, TOPK])

        xs_loaded = [sem(f"xs_loaded{i}") for i in range(2)]
        res_loaded, out_stored = ([sem(f"{name}{i}") for i in range(TPB)] for name in ("res_loaded", "out_stored"))
        picked, gathered, scaled, summed = sem("picked_cols"), sem("gathered"), sem("scaled"), sem("summed")
        res_ready, also_loaded, also_stored = sem("res_ready"), sem("also_loaded"), sem("also_stored")
        pool_turns, sp_turns = sem("a_pool_turns"), sem("a_sp_turns")

        block = ctx.enter_context(nc.Block())

        def batches(eng, body):
            with eng.Fori(0, NB - 1) as b:
                body(b, True)
            body(NB - 1, False)

        @block.sync
        def _(sp):
            A.load_small(sp)

            def body(b, more):
                for n in range(TPB):
                    sp.dma_start(res[:, n, :], x[bass.ds((b + 1) * LEN + n * P, P), :]).then_inc(res_loaded[n], 16)
                for n in range(TPB):
                    sp.wait_ge(A.out_ready, b * TPB + (n + 1))
                    sp.sem_inc(sp_turns, 1)
                    sp.dma_start(out[bass.ds((b + 1) * LEN + n * P, P), :], res[:, n, :]).then_inc(out_stored[n], 16)
                for n in range(TPB):
                    sp.wait_ge(out_stored[n], (b + 1) * 16)
                    sp.sem_inc(sp_turns, 1)

            batches(sp, body)

        @block.gpsimd
        def _(pool):
            g = nc.gpsimd
            A.constants(pool)
            pool.wait_ge(A.small_loaded, 16 * A.small)
            pool.wait_ge(t["y_stored"], EXPERT_TILES * 16)

            def after(semaphore, count):
                pool.wait_ge(semaphore, count)
                pool.sem_inc(pool_turns, 1)

            def gather(i, n):
                g.tensor_copy(idx[:], slot[:, :, bass.ds(i, 1)].rearrange("p k a -> p (k a)")).then_inc(picked, 1)
                g.tensor_copy(gate[:], gates[:, :, bass.ds(i, 1)].rearrange("p k a -> p (k a)")).then_inc(picked, 1)
                after(picked, (n + 1) * 2)
                for k in range(TOPK):
                    g.indirect_dma_start(ye[:, k, :], None, y_d[:, :],
                                         bass.IndirectOffsetOnAxis(ap=idx[:, k:k + 1].bitcast(U32), axis=0))\
                        .then_inc(gathered, 16)

            def total(r, other, n):
                g.tensor_tensor(r, r, other, ALU.add).then_inc(summed, 1)
                after(gathered, (n + 1) * (16 * TOPK))
                for k in range(TOPK):
                    g.tensor_scalar(ye[:, k, :], ye[:, k, :], gate[:, k:k + 1], None, ALU.mult).then_inc(scaled, 1)
                after(scaled, (n + 1) * TOPK)
                pool.wait_ge(summed, n * 3 + 1)
                g.tensor_tensor(r, r, ye[:, 0, :], ALU.add).then_inc(summed, 1)
                pool.wait_ge(summed, n * 3 + 2)
                return g.tensor_tensor(r, r, ye[:, 1, :], ALU.add).then_inc(summed, 1)

            def body(b, more):
                for n in range(TPB):
                    k = b * (TPB + ALSO) + n
                    gather((b + 1) * TPB + n, k)
                    pool.wait_ge(res_loaded[n], (b + 1) * 16)
                    total(res[:, n, :], A.pjb[:], k)
                    after(summed, (k + 1) * 3)
                    pool.sem_inc(res_ready, 1)
                if more:
                    for n in range(ALSO):
                        k = b * (TPB + ALSO) + (TPB + n)
                        i = b * ALSO + n
                        at = bass.ds(i * P, P)
                        g.dma_start(also[:], x[at, :]).then_inc(also_loaded, 16)
                        g.dma_start(alsob[:], base_d[at, :]).then_inc(also_loaded, 16)
                        gather(i, k)
                        after(also_loaded, (i + 1) * 32)
                        total(also[:], alsob[:], k)
                        after(summed, (k + 1) * 3)
                        g.dma_start(out[at, :], also[:]).then_inc(also_stored, 16)
                        after(also_stored, (i + 1) * 16)

            batches(pool, body)

        @block.tensor
        def _(pe):
            def transpose_x(b, n):
                pe.wait_ge(xs_loaded[n % 2], (b * (TPB // 2) + (n // 2 + 1)) * 16)
                A.pe_transpose_x(pe, b * TPB + n, n, xs[:, n % 2, :], RING)

            pe.wait_ge(A.zeroed, 4)

            def body(b, more):
                A.pe_proj(pe, b, (lambda n: transpose_x(b, n)) if more else None,
                          (lambda g, when: A.pe_fill(pe, b, b, g, when)) if more else None)
                pe.wait_ge(A.small_loaded, 16 * A.small)
                A.pe_steps(pe, b, (lambda g, when: A.pe_fill(pe, b, b, g, when)) if more else None)
                A.pe_out(pe, b)
                if more:
                    pe.wait_ge(A.conv_hi, (b + 1) * PROJ)
                    pe.wait_ge(A.conv_lo, (b + 1) * PROJ)
                pe.wait_ge(A.out_ready, b * TPB + (TPB - 1))

            batches(pe, body)

        @block.scalar
        def _(a):
            def load_xs(b, n):
                rows = xn_d[bass.ds((b + 2) * LEN + n * P, P), :]
                a.dma_start(xs[:, n % 2, :], rows).then_inc(xs_loaded[n % 2], 16)

            def body(b, more):
                def next_x(n):
                    A.act_hi_x(a, b * TPB + n, n, RING)
                    if n + 2 < TPB:
                        load_xs(b, n + 2)

                if more:
                    for n in range(2):
                        load_xs(b, n)
                A.act_proj(a, b, next_x if more else None)
                A.act_steps(a, b, (lambda g: A.act_fill(a, b, g, (A.qkvh, A.qkvl))) if more else None)

            batches(a, body)

        @block.vector
        def _(d):
            v = nc.vector
            d.wait_ge(A.mask_ready, 2)

            def body(b, more):
                A.dve_proj(d, b, (lambda n: A.dve_lo_x(d, b * TPB + n, n, RING)) if more else None)
                A.dve_steps(d, b, (lambda g: A.dve_fill(d, b, g, (A.qkvh, A.qkvl))) if more else None)
                for n in range(TPB):
                    d.wait_ge(A.out_done, b * TPB + (n + 1))
                    d.wait_ge(res_ready, b * TPB + (n + 1))
                    v.tensor_tensor(res[:, n, :], banks[OUT_BANKS[n]][:], res[:, n, :], ALU.add).then_inc(A.out_ready, 1)

            batches(d, body)


_OUT = ((TOK, DM), "float32")


def kernel(**inputs):
    import numpy as _np
    import concourse.bacc as _bacc
    from concourse import mybir as _mybir
    from concourse.bass_utils import run_bass_kernel_spmd as _run

    g = {k.replace("L0_attn_", "").replace("L0_ffn_", "ffn_"): _np.asarray(v) for k, v in inputs.items()}

    def chunked(w, rows):
        e, r, c = w.shape
        return w.reshape(e, r // rows, rows, c).transpose(0, 2, 1, 3).reshape(e, rows, -1)

    w1, w3, w2 = (g[k].transpose(0, 2, 1) for k in ("ffn_w1", "ffn_w3", "ffn_w2"))
    last = _np.zeros((NE, P, DM), w2.dtype)
    last[:, :3 * FLAST] = _np.tile(w2[:, (AC - 1) * P:], (1, 3, 1))
    experts = _np.concatenate(
        [chunked(w[:, :, f], P) for f in (slice(0, FA), slice(FA, FF)) for w in (w1, w3)]
        + [chunked(w2[:, :(AC - 1) * P], P), last], axis=2)
    arrays = {
        "x": g["inputs"].reshape(TOK, DM),
        "conv_w": g["conv_w"],
        "columns": _np.concatenate([g[k].reshape(-1, P).T for k in ("conv_b", "bq", "bk", "bo")], axis=1),
        **{k: g[k] for k in ("wq", "wk", "wv", "bv", "wo", "proj_w", "proj_b")},
        "gate": g["ffn_gate_w"].T.reshape(DC, P, NE).transpose(1, 0, 2),
        "experts": experts,
    }
    arrays = {k: _np.ascontiguousarray(v) for k, v in arrays.items()}
    nc = _bacc.Bacc("TRN2", target_bir_lowering=False, num_devices=1)
    args = [nc.dram_tensor(f"in_{k}", v.shape, _mybir.dt.from_np(v.dtype), kind="ExternalInput").ap()
            for k, v in arrays.items()]
    out = nc.dram_tensor("out_0", _OUT[0], _mybir.dt.from_np(_np.dtype(_OUT[1])), kind="ExternalOutput").ap()
    build(nc, *args, out)
    r = _run(nc, [{f"in_{k}": v for k, v in arrays.items()}], core_ids=[0])
    return _np.asarray(r.results[0]["out_0"]).reshape(BATCH, LEN, DM)
```
